# Optimizing a Trainium2 kernel written in Bass

```python
import numpy as np
import jax
import jax.numpy as jnp

def _softmax(x, axis=-1):
    return jax.nn.softmax(x, axis=axis)

def _gelu(x):
    return jax.nn.gelu(x, approximate=True)

def _silu(x):
    return jax.nn.silu(x)

def _sigmoid(x):
    return jax.nn.sigmoid(x)

def _layernorm(x, axis=-1, eps=1e-05):
    m = jnp.mean(x, axis=axis, keepdims=True)
    v = jnp.var(x, axis=axis, keepdims=True)
    return (x - m) / jnp.sqrt(v + eps)

def _scatter_add(tgt, idx, src, axis=0):
    return tgt.at[idx].add(src)

def _segment_sum(src, seg, n):
    return jax.ops.segment_sum(src, seg, n)
kernel_name = 'mk_gnn_ffn_d2_gnn_r8_ac5d8b'

def setup_inputs(seed: int=0):
    np.random.seed(seed)
    _w = jnp.asarray

    def _rec_inputs():
        import jax
        import jax.numpy as jnp
        _gk = jax.random.key(seed)
        x = -7.329e-05 + 0.9999 * jax.random.normal(jax.random.fold_in(_gk, 1), (1250, 1024), jnp.float32)
        _s = jax.random.randint(jax.random.fold_in(_gk, 2), (20000,), 0, 1250, jnp.int32)
        _d = jax.random.randint(jax.random.fold_in(_gk, 3), (20000,), 0, 1250, jnp.int32)
        _loop = jnp.arange(1250, dtype=jnp.int32)
        src = jnp.concatenate([_s, _d, _loop])
        dst = jnp.concatenate([_d, _s, _loop])
        _o = jnp.argsort(dst, stable=True)
        src = src[_o]
        dst = dst[_o]
        edge_weight = -0.000130211 + 0.031236 * jax.random.normal(jax.random.fold_in(_gk, 12), (41250,), jnp.float32)
        return (x, src, dst, edge_weight)
    x, src, dst, edge_weight = _rec_inputs()

    def _L0_gnn_setup():
        import jax, jax.numpy as jnp
        import numpy as np
        INDIM = 1024
        OUTDIM = 1024
        NNZ = 8192
        N = 6250
        key = jax.random.key(seed)
        k1, k2, k3, k4, k5 = jax.random.split(key, 5)
        x = jax.random.normal(k1, (N, INDIM), dtype=jnp.float32)
        stdv = np.sqrt(6.0 / (INDIM + OUTDIM))
        nnz_weight = jax.random.uniform(k2, (NNZ,), dtype=jnp.float32, minval=-stdv, maxval=stdv)
        bias = jax.random.normal(k3, (OUTDIM,), dtype=jnp.float32) * 0.02
        row = jax.random.randint(k4, (NNZ,), 0, OUTDIM, dtype=jnp.int64)
        col = jax.random.randint(k5, (NNZ,), 0, INDIM, dtype=jnp.int64)
        edge_index = jnp.stack([row, col])
        return {'x': x, 'nnz_weight': nnz_weight, 'bias': bias, 'edge_index': edge_index}
    _L0_gnn_all = _L0_gnn_setup()
    _L0_gnn_in = {k: v for k, v in _L0_gnn_all.items() if k in ('bias',)}
    del _L0_gnn_all

    def _L0_ffn_setup():
        import jax, jax.numpy as jnp
        import numpy as np
        B, S, D = (2, 256, 1024)
        E, K, H = (8, 2, 512)
        CAP_FACTOR = 1.0

        def _moe_forward(x, wg, w1, b1, w2, b2):
            Bb, Ss, Dd = x.shape
            T = Bb * Ss
            cap = int(K * CAP_FACTOR * ((T + E - 1) // E))
            xt = x.reshape(T, Dd)
            logits = xt @ wg
            scores = jax.nn.softmax(logits, axis=-1)
            gates_k, idx_k = jax.lax.top_k(scores, K)
            gates_k = gates_k / jnp.sum(gates_k, axis=-1, keepdims=True)
            masks = jax.nn.one_hot(idx_k, E, dtype=jnp.int32)
            m = jnp.transpose(masks, (1, 0, 2)).reshape(K * T, E)
            locs_full = jnp.cumsum(m, axis=0) - 1
            loc = jnp.sum(locs_full * m, axis=-1)
            loc = loc.reshape(K, T).T
            valid = (loc < cap).astype(xt.dtype)
            loc_c = jnp.clip(loc, 0, cap - 1)
            contrib = (xt[:, None, :] * valid[:, :, None]).reshape(T * K, Dd)
            disp = jnp.zeros((E, cap, Dd), xt.dtype)
            disp = disp.at[idx_k.reshape(-1), loc_c.reshape(-1)].add(contrib)
            h = jax.nn.relu(jnp.einsum('ecd,edh->ech', disp, w1) + b1[:, None, :])
            out = jnp.einsum('ech,ehd->ecd', h, w2) + b2[:, None, :]
            gathered = out[idx_k, loc_c]
            y = jnp.einsum('tk,tkd->td', gates_k * valid, gathered)
            return y.reshape(Bb, Ss, Dd)
        key = jax.random.key(seed)
        ks = jax.random.split(key, 6)
        scale_in = 1.0 / np.sqrt(D)
        scale_h = 1.0 / np.sqrt(H)
        return {'x': jax.random.normal(ks[0], (B, S, D), jnp.float32), 'wg': jax.random.normal(ks[1], (D, E), jnp.float32) * scale_in, 'w1': jax.random.normal(ks[2], (E, D, H), jnp.float32) * scale_in, 'b1': jnp.zeros((E, H), jnp.float32), 'w2': jax.random.normal(ks[3], (E, H, D), jnp.float32) * scale_h, 'b2': jnp.zeros((E, D), jnp.float32)}
    _L0_ffn_all = _L0_ffn_setup()
    _L0_ffn_in = {k: v for k, v in _L0_ffn_all.items() if k in ('wg', 'w1', 'b1', 'w2', 'b2')}
    del _L0_ffn_all

    def _L1_gnn_setup():
        import jax, jax.numpy as jnp
        import numpy as np
        N = 2500
        E = 40000
        D_IN = 1024
        D_OUT = 1024
        key = jax.random.key(seed)
        k1, k2, k3, k4 = jax.random.split(key, 4)
        x = jax.random.normal(k1, (N, D_IN), dtype=jnp.float32)
        edge_index = jax.random.randint(k2, (2, E), 0, N, dtype=jnp.int64)
        W = jax.random.normal(k3, (D_OUT, D_IN), dtype=jnp.float32) * (1.0 / np.sqrt(D_IN))
        b = jax.random.normal(k4, (D_OUT,), dtype=jnp.float32) * 0.01
        return {'x': x, 'edge_index': edge_index, 'W': W, 'b': b}
    _L1_gnn_all = _L1_gnn_setup()
    _L1_gnn_in = {k: v for k, v in _L1_gnn_all.items() if k in ('W', 'b')}
    del _L1_gnn_all

    def _L1_ffn_setup():
        import jax, jax.numpy as jnp
        import numpy as np
        EMBED_DIM = 1024
        HIDDEN = 4 * EMBED_DIM
        BATCH, SEQ = (4, 512)
        EPS = 1e-05

        def _quant_weight(w):
            s = jnp.clip(jnp.mean(jnp.abs(w)), EPS, None)
            wq = jnp.clip(jnp.round(w / s), -1.0, 1.0) * s
            return w + jax.lax.stop_gradient(wq - w)

        def _quant_act(x):
            scale = 127.0 / jnp.clip(jnp.max(jnp.abs(x), axis=-1, keepdims=True), EPS, None)
            xq = jnp.clip(jnp.round(x * scale), -128.0, 127.0) / scale
            return x + jax.lax.stop_gradient(xq - x)

        def _bitlinear(x, w):
            return jnp.einsum('bsi,oi->bso', _quant_act(x), _quant_weight(w))
        key = jax.random.key(seed)
        k1, k2, k3 = jax.random.split(key, 3)
        x = jax.random.normal(k1, (BATCH, SEQ, EMBED_DIM), dtype=jnp.float32)
        w1 = jax.random.normal(k2, (HIDDEN, EMBED_DIM), dtype=jnp.float32) * (1.0 / np.sqrt(EMBED_DIM))
        w2 = jax.random.normal(k3, (EMBED_DIM, HIDDEN), dtype=jnp.float32) * (1.0 / np.sqrt(HIDDEN))
        return {'x': x, 'w1': w1, 'w2': w2}
    _L1_ffn_all = _L1_ffn_setup()
    _L1_ffn_in = {k: v for k, v in _L1_ffn_all.items() if k in ('w1', 'w2')}
    del _L1_ffn_all
    return {'x': x, 'src': src, 'dst': dst, 'edge_weight': edge_weight, 'L0_gnn_bias': _L0_gnn_in['bias'], 'L0_ffn_wg': _L0_ffn_in['wg'], 'L0_ffn_w1': _L0_ffn_in['w1'], 'L0_ffn_b1': _L0_ffn_in['b1'], 'L0_ffn_w2': _L0_ffn_in['w2'], 'L0_ffn_b2': _L0_ffn_in['b2'], 'L1_gnn_W': _L1_gnn_in['W'], 'L1_gnn_b': _L1_gnn_in['b'], 'L1_ffn_w1': _L1_ffn_in['w1'], 'L1_ffn_w2': _L1_ffn_in['w2']}

def reference(x, src, dst, edge_weight, L0_gnn_bias, L0_ffn_wg, L0_ffn_w1, L0_ffn_b1, L0_ffn_w2, L0_ffn_b2, L1_gnn_W, L1_gnn_b, L1_ffn_w1, L1_ffn_w2):
    import jax
    import jax.numpy as jnp

    def _L0_gnn_ref(x, nnz_weight, bias, edge_index):
        import jax, jax.numpy as jnp
        import numpy as np
        INDIM = 1024
        OUTDIM = 1024
        NNZ = 8192
        N = 6250
        row, col = (edge_index[0], edge_index[1])
        W = jnp.zeros((OUTDIM, INDIM), dtype=nnz_weight.dtype).at[row, col].add(nnz_weight)
        return x @ W.T + bias

    def _L0_ffn_ref(x, wg, w1, b1, w2, b2):
        import jax, jax.numpy as jnp
        import numpy as np
        B, S, D = (2, 256, 1024)
        E, K, H = (8, 2, 512)
        CAP_FACTOR = 1.0

        def _moe_forward(x, wg, w1, b1, w2, b2):
            Bb, Ss, Dd = x.shape
            T = Bb * Ss
            cap = int(K * CAP_FACTOR * ((T + E - 1) // E))
            xt = x.reshape(T, Dd)
            logits = xt @ wg
            scores = jax.nn.softmax(logits, axis=-1)
            gates_k, idx_k = jax.lax.top_k(scores, K)
            gates_k = gates_k / jnp.sum(gates_k, axis=-1, keepdims=True)
            masks = jax.nn.one_hot(idx_k, E, dtype=jnp.int32)
            m = jnp.transpose(masks, (1, 0, 2)).reshape(K * T, E)
            locs_full = jnp.cumsum(m, axis=0) - 1
            loc = jnp.sum(locs_full * m, axis=-1)
            loc = loc.reshape(K, T).T
            valid = (loc < cap).astype(xt.dtype)
            loc_c = jnp.clip(loc, 0, cap - 1)
            contrib = (xt[:, None, :] * valid[:, :, None]).reshape(T * K, Dd)
            disp = jnp.zeros((E, cap, Dd), xt.dtype)
            disp = disp.at[idx_k.reshape(-1), loc_c.reshape(-1)].add(contrib)
            h = jax.nn.relu(jnp.einsum('ecd,edh->ech', disp, w1) + b1[:, None, :])
            out = jnp.einsum('ech,ehd->ecd', h, w2) + b2[:, None, :]
            gathered = out[idx_k, loc_c]
            y = jnp.einsum('tk,tkd->td', gates_k * valid, gathered)
            return y.reshape(Bb, Ss, Dd)
        return _moe_forward(x, wg, w1, b1, w2, b2)

    def _L1_gnn_ref(x, edge_index, W, b):
        import jax, jax.numpy as jnp
        import numpy as np
        N = 2500
        E = 40000
        D_IN = 1024
        D_OUT = 1024
        num_nodes = x.shape[0]
        self_idx = jnp.arange(num_nodes, dtype=edge_index.dtype)
        ei = jnp.concatenate([edge_index, jnp.stack([self_idx, self_idx], axis=0)], axis=1)
        row, col = (ei[0], ei[1])
        h = jnp.einsum('nd,od->no', x, W) + b
        deg = jnp.zeros((num_nodes,), dtype=h.dtype).at[row].add(1.0)
        deg_inv_sqrt = deg ** (-0.5)
        norm = deg_inv_sqrt[row] * deg_inv_sqrt[col]
        msg = norm[:, None] * h[col]
        out = jax.ops.segment_sum(msg, row, num_segments=num_nodes)
        return out

    def _L1_ffn_ref(x, w1, w2):
        import jax, jax.numpy as jnp
        import numpy as np
        EMBED_DIM = 1024
        HIDDEN = 4 * EMBED_DIM
        BATCH, SEQ = (4, 512)
        EPS = 1e-05

        def _quant_weight(w):
            s = jnp.clip(jnp.mean(jnp.abs(w)), EPS, None)
            wq = jnp.clip(jnp.round(w / s), -1.0, 1.0) * s
            return w + jax.lax.stop_gradient(wq - w)

        def _quant_act(x):
            scale = 127.0 / jnp.clip(jnp.max(jnp.abs(x), axis=-1, keepdims=True), EPS, None)
            xq = jnp.clip(jnp.round(x * scale), -128.0, 127.0) / scale
            return x + jax.lax.stop_gradient(xq - x)

        def _bitlinear(x, w):
            return jnp.einsum('bsi,oi->bso', _quant_act(x), _quant_weight(w))
        h = jax.nn.gelu(_bitlinear(x, w1), approximate=False)
        return _bitlinear(h, w2)
    edge_index = jnp.stack([src, dst])
    x = x + _L0_gnn_ref(_layernorm(x, axis=-1), edge_weight, L0_gnn_bias, edge_index)
    x = x + _L0_ffn_ref(_layernorm(x, axis=-1)[None], L0_ffn_wg, L0_ffn_w1, L0_ffn_b1, L0_ffn_w2, L0_ffn_b2)[0]
    x = x + _L1_gnn_ref(_layernorm(x, axis=-1), edge_index, L1_gnn_W, L1_gnn_b)
    x = x + _L1_ffn_ref(_layernorm(x, axis=-1)[None], L1_ffn_w1, L1_ffn_w2)[0]
    return x

_drawn_inputs = setup_inputs


def setup_inputs(seed=0):
    import zlib

    import numpy as np

    out = dict(_drawn_inputs(seed))
    spreads = {'L0_ffn_b1': (0.0, 0.1), 'L0_ffn_b2': (0.0, 0.1)}
    factors = {'L1_gnn_b': 4.77}
    for name, (base, spread) in spreads.items():
        noise = np.random.default_rng([zlib.crc32(name.encode()), seed]).standard_normal(out[name].shape)
        drawn = base * np.exp(spread * noise) if base else spread * noise
        out[name] = jnp.asarray(drawn.astype(out[name].dtype))
    for name, factor in factors.items():
        out[name] = (out[name] * factor).astype(out[name].dtype)
    return out
```

```python
from contextlib import ExitStack

import concourse.bass as bass
from concourse import mybir

F32 = mybir.dt.float32
F16 = mybir.dt.float16
F8 = mybir.dt.float8e4
I32 = mybir.dt.int32
U32 = mybir.dt.uint32
ALU = mybir.AluOpType
ACT = mybir.ActivationFunctionType
AX = mybir.AxisListType

P = 128
N = 1250
D = 1024
NT = (N + P - 1) // P
LAST = N - (NT - 1) * P
NP = NT * P
KD = D // P
E_EDGES = 41250
CH = (E_EDGES + P - 1) // P
CHP = 3 * P
WIN = 32
NW = NP // WIN
G = 10
RING = 5
NG_MAX = (CH + G - 1) // G
NE = 8
HID = 512
CAP = 2 * ((N + NE - 1) // NE)
SM = [P, P, CAP - 2 * P]
KH = HID // P
FH = 4096
KF = FH // P

SX = 1024.0
SW = 256.0
SH = 64.0
MAGIC = 12582912.0
LN_EPS = 1e-5
Q_EPS = 1e-5


class Steps:

    def __init__(self, eng, sem, base=0):
        self.eng, self.sem, self.base, self.n = eng, sem, base, 0

    def at(self, base):
        self.base, self.n = base, 0

    def inc(self, ins):
        ins.then_inc(self.sem, 1)
        self.n += 1

    def wait(self):
        self.eng.wait_ge(self.sem, self.base + self.n)


def build_kernel(nc, x_in, src_in, dst_in, ew_in, bias0_in, wg_in, w1_in, b1_in, w2_in, b2_in,
                 gw_in, gb_in, f1_in, f2_in, out):
    ctx = ExitStack()
    with ctx:
        OFF_X = (nc.sbuf_base + 31) // 32 * 32
        OFF_MISC = OFF_X + NT * D * 4
        OFF_LN = OFF_MISC + 14336
        OFF_AT = OFF_LN + 26624
        OFF_BIG = OFF_AT + 2 * NT * NP * 2
        END = nc.sbuf_usable_end

        cur = {"x": OFF_X, "misc": OFF_MISC, "ln": OFF_LN, "at": OFF_AT, "big": OFF_BIG}
        lim = {"x": OFF_MISC, "misc": OFF_LN, "ln": OFF_AT, "at": OFF_BIG, "big": END, "wide": END}

        def sb(area, name, shape, dt):
            n = 1
            for d in shape[1:]:
                n *= d
            size = (n * (2 if dt == F16 else 1 if dt == F8 else 4) + 31) // 32 * 32
            off = cur[area]
            cur[area] = off + size
            assert cur[area] <= lim[area], (area, name, cur[area] - lim[area])
            return nc.alloc_sbuf_tensor_at(name, shape, dt, offset=off)

        def restart(area, off):
            cur[area] = off

        def sem(name):
            return ctx.enter_context(nc.semaphore(name))

        x = sb("x", "x", [P, NT, D], F32)
        iota_r = sb("misc", "iota_r", [P, NP], F16)
        id16 = sb("misc", "id16", [P, P], F16)
        id32 = sb("misc", "id32", [P, P], F32)
        tri = sb("misc", "tri", [P, P], F16)
        ones16 = sb("misc", "ones16", [P, P], F16)
        zero16 = sb("misc", "zero16", [P, 96], F16)
        ones32 = sb("misc", "ones32", [P, P], F32)
        bias_b = sb("misc", "bias_b", [P, D], F32)
        stats = sb("misc", "stats", [P, 2, 6], F32)
        mv_one = sb("misc", "mv_one", [P, 2], F32)
        mv = sb("misc", "mv", [P, NT, 2], F32)
        rstd = sb("misc", "rstd", [P, NT], F32)
        rtmp = sb("misc", "rtmp", [P, 2], F32)
        consts = sb("misc", "consts", [P, 4], F32)
        rows_i = sb("misc", "rows_i", [1, 2, 48], I32)
        abs_acc = sb("misc", "abs_acc", [P, 32], F32)
        fwinv = sb("misc", "fwinv", [P, 16], F32)
        sw = sb("misc", "sw", [P, 8], F32)
        gates = sb("misc", "gates", [P, 2, NT], F32)
        slot_i = sb("misc", "slot_i", [P, 2 * NT], I32)
        tok_i = sb("misc", "tok_i", [P, 3 * NE], I32)
        b1c = sb("misc", "b1c", [P, NE, KH], F32)
        dinv = sb("misc", "dinv", [P, 3, NT], F32)
        fs = sb("misc", "fs", [P, 2, 16], F32)
        hm = sb("misc", "hm", [P, 2, 8], F32)

        wg32 = sb("misc", "wg32", [P, KD, NE], F32)
        wgs = sb("misc", "wgs", [P, KD, 2 * NE], F16)

        xn = sb("ln", "xn", [P, 2, D], F32)
        xh = sb("ln", "xh", [P, 2, D], F16)
        xl = sb("ln", "xl", [P, 2, D], F16)
        xth = sb("ln", "xth", [P, 2, KD, P], F16)
        xtl = sb("ln", "xtl", [P, 2, KD, P], F16)
        restart("ln", OFF_LN)
        st_a = sb("ln", "st_a", [P, 2, NP], F32)
        st_wh = sb("ln", "st_wh", [P, 2, D], F32)
        st_wl = sb("ln", "st_wl", [P, 2, D], F32)
        restart("ln", OFF_LN)
        gx = sb("ln", "gx", [P, 2, 2 * D], F16)
        eo = sb("ln", "eo", [P, 2, D], F32)
        b2b = sb("ln", "b2b", [P, D], F32)
        ht32 = sb("ln", "ht32", [P, 2, CAP], F32)
        htl = sb("ln", "htl", [P, KH, CAP], F16)

        at_h = sb("at", "at_h", [P, NT, NP], F16)
        at_l = sb("at", "at_l", [P, NT, NP], F16)

        wt_h = sb("big", "wt_h", [P, NT, D], F16)
        wt_l = sb("big", "wt_l", [P, NT, D], F16)
        src_t = sb("big", "src_t", [P, CHP], F32)
        dst_t = sb("big", "dst_t", [P, CHP], F32)
        ewh_t = sb("big", "ewh_t", [P, CHP], F16)
        ewl_t = sb("big", "ewl_t", [P, CHP], F16)
        src_g = sb("big", "src_g", [P, 2, RING], F32)
        st_e = sb("big", "st_e", [P, 2, RING, 96], F16)
        big_mark = cur["big"]
        oh = sb("big", "oh", [P, RING, NP], F16)
        abs_in = sb("big", "abs_in", [P, 2, 2048], F32)
        restart("big", big_mark)
        nat_i = sb("big", "nat_i", [P, 2, 3, P], I32)
        nat_f = sb("big", "nat_f", [P, 2, 3, P], F32)
        nat_w = sb("big", "nat_w", [P, 3, P], F32)
        ew32_t = sb("big", "ew32_t", [P, CHP], F32)
        cm = sb("big", "cm", [P, 2, 3], F32)
        cmb = sb("big", "cmb", [P, 6, 48], F16)
        q_iota = sb("big", "q_iota", [48, CHP], F32)
        w_lo = sb("big", "w_lo", [48, 2], F32)
        ov = sb("big", "ov", [48, 2, CHP], F32)
        j_iota = sb("big", "j_iota", [48, 40], F32)
        kk = sb("big", "kk", [48, 8], F32)
        kk16 = sb("big", "kk16", [48, 2], F16)
        restart("big", OFF_BIG)
        wstage = sb("big", "wstage", [P, 4, 2048], F32)
        w1h = sb("big", "w1h", [P, KD, HID], F16)
        w1l = sb("big", "w1l", [P, KD, HID], F16)
        w2h = sb("big", "w2h", [P, KH, D], F16)
        w2l = sb("big", "w2l", [P, KH, D], F16)
        xdh = sb("big", "xdh", [P, KD, CAP], F16)
        xdl = sb("big", "xdl", [P, KD, CAP], F16)
        hth = sb("big", "hth", [P, KH, CAP], F16)
        restart("big", OFF_BIG + 32768)
        logits = sb("big", "logits", [P, NT, NE], F32)
        lmax = sb("big", "lmax", [P, NT, 8], F32)
        lidx = sb("big", "lidx", [P, NT, 8], U32)
        lidf = sb("big", "lidf", [P, NT, 8], F32)
        mask = sb("big", "mask", [P, 2, NT, NE], F16)
        tot_e = sb("big", "tot_e", [P, NE, 2 * NT], F32)
        scan_m = sb("big", "scan_m", [P, NE, 2 * NT], F32)
        scan_o = sb("big", "scan_o", [P, NE, 2 * NT], F32)
        loc3 = sb("big", "loc3", [P, 2 * NT, NE], F32)
        loc3b = sb("big", "loc3b", [P, 2 * NT, NE], F32)
        rt = sb("big", "rt", [P, 12, 2 * NT], F32)
        iota_lo = sb("big", "iota_lo", [P, P], F32)
        tok_f = sb("big", "tok_f", [P, 2 * NT], F32)
        oh_lo = sb("big", "oh_lo", [P, 2 * NT, P], F16)
        oh_hi = sb("big", "oh_hi", [P, 2 * NT, 3 * NE], F16)
        oh_hi2 = sb("big", "oh_hi2", [P, 2 * NT, 3 * NE], F16)
        valid_m = sb("big", "valid_m", [P, 2, NT, NE], F16)
        restart("big", OFF_BIG + 57344)
        back = sb("big", "back", [P, 4, D], F32)
        restart("big", OFF_BIG)
        gwt_h = sb("big", "gwt_h", [P, KD, D], F16)
        gwt_l = sb("big", "gwt_l", [P, KD, D], F16)
        hs_mark = cur["big"]
        hs_h = sb("big", "hs_h", [P, NT, D], F16)
        hs_l = sb("big", "hs_l", [P, NT, D], F16)
        h32 = sb("big", "h32", [P, D], F32)
        restart("big", hs_mark + 8192)
        gnat = sb("big", "gnat", [P, 2, D], F32)
        gnh = sb("big", "gnh", [P, 2, D], F16)
        gnl = sb("big", "gnl", [P, 2, D], F16)
        cur["wide"] = OFF_AT
        w1q = sb("wide", "w1q", [P, KD, FH], F8)
        w2q = sb("wide", "w2q", [P, KF, D], F8)
        wide_mark = cur["wide"]
        hf = sb("wide", "hf", [P, 2, FH], F32)
        hq = sb("wide", "hq", [P, FH], F16)
        hqt = sb("wide", "hqt", [P, KF, P], F16)
        restart("wide", wide_mark)
        fnat = sb("wide", "fnat", [P, 4, D], F32)
        fy = sb("wide", "fy", [P, 2, D], F32)
        fq = sb("wide", "fq", [P, 2, D], F16)
        restart("ln", OFF_LN)
        xn_f = sb("ln", "xn_f", [P, 2, D], F32)
        out_t = sb("ln", "out_t", [P, 2, D], F32)
        xq = sb("ln", "xq", [P, 2, D], F16)
        xqt = sb("ln", "xqt", [P, 2, KD, P], F16)

        ps = ctx.enter_context(nc.psum_tensor("ps", [P, 8, 512], F32))

        def bank16(b):
            return ps[:, b, :].bitcast(F16)

        xs_d = nc.dram_tensor("xs_d", [NP, 2 * D], F16).ap()
        eo_d = nc.dram_tensor("eo_d", [NE * CAP, D], F32).ap()

        s_pad = sem("s_pad")
        s_edges = sem("s_edges")
        s_x = sem("s_x")
        s_bias = sem("s_bias")
        s_b1 = sem("s_b1")
        s_wg = sem("s_wg")
        s_absin = [sem(f"s_absin{u}") for u in range(2)]
        s_const = sem("s_const")
        s_dv = sem("s_dv")
        s_natf = sem("s_natf")
        s_cmb = sem("s_cmb")
        s_et = sem("s_et")
        s_cmw = sem("s_cmw")
        s_kk = sem("s_kk")
        s_kr = sem("s_kr")
        s_rows = sem("s_rows")
        s_small = sem("s_small")
        s_group = sem("s_group")
        s_st = sem("s_st")
        s_oh = sem("s_oh")
        s_chunk = sem("s_chunk")
        s_win = sem("s_win")
        s_winread = sem("s_winread")
        s_stage = sem("s_stage")
        s_blk = sem("s_blk")
        s_built = sem("s_built")
        s_abs = sem("s_abs")
        s_bn = sem("s_bn")
        s_stat = sem("s_stat")
        s_pl = sem("s_pl")
        s_rstd = sem("s_rstd")
        s_biased = sem("s_biased")
        s_xn = sem("s_xn")
        s_xh = sem("s_xh")
        s_xl = sem("s_xl")
        s_th, s_tl = sem("s_th"), sem("s_tl")
        s_xth, s_xtl = sem("s_xth"), sem("s_xtl")
        s_mm = sem("s_mm")
        s_mmread = sem("s_mmread")
        s_xstore = [sem(f"s_xstore{u}") for u in range(2)]
        s_mask = sem("s_mask")
        s_cum = sem("s_cum")
        s_gd = sem("s_gd")
        s_ex = sem("s_ex")
        s_ohr = sem("s_ohr")
        s_tok = sem("s_tok")
        s_toki = sem("s_toki")
        s_wst = [sem(f"s_wst{i}") for i in range(4)]
        s_wh = sem("s_wh")
        s_wl = sem("s_wl")
        s_g = [sem("s_gx0"), sem("s_gx1")]
        s_gth, s_gtl = sem("s_gth"), sem("s_gtl")
        s_gch, s_gcl = sem("s_gch"), sem("s_gcl")
        s_g1 = sem("s_g1")
        s_g1r = sem("s_g1r")
        s_hh = sem("s_hh")
        s_hl = sem("s_hl")
        s_g2 = sem("s_g2")
        s_g2r = sem("s_g2r")
        s_b2 = sem("s_b2")
        s_eout = [sem("s_eout0"), sem("s_eout1")]
        s_back = [sem(f"s_back{i}") for i in range(4)]
        s_mix = sem("s_mix")
        s_gn = [sem("s_gn0"), sem("s_gn1")]
        s_gnh, s_gnl = sem("s_gnh"), sem("s_gnl")
        s_wtp = sem("s_wtp")
        s_wth, s_wtl = sem("s_wth"), sem("s_wtl")
        s_deg = sem("s_deg")
        s_degp = sem("s_degp")
        s_dinv = sem("s_dinv")
        s_dinv2 = sem("s_dinv2")
        s_hsh, s_hsl = sem("s_hsh"), sem("s_hsl")
        s_agg = sem("s_agg")
        s_aggread = sem("s_aggread")
        s_swp = sem("s_swp")
        s_swm = sem("s_swm")
        s_sw = sem("s_sw")
        s_fn = [sem(f"s_fn{i}") for i in range(4)]
        s_fy = sem("s_fy")
        s_fq = sem("s_fq")
        s_ft = sem("s_ft")
        s_fc = sem("s_fc")
        s_dq = sem("s_dq")
        s_xq = sem("s_xq")
        s_xqt = sem("s_xqt")
        s_xqc = sem("s_xqc")
        s_f1 = sem("s_f1")
        s_ge = sem("s_ge")
        s_hq = sem("s_hq")
        s_hqt = sem("s_hqt")
        s_hqc = sem("s_hqc")
        s_f2 = sem("s_f2")
        s_f2r = sem("s_f2r")
        s_out = [sem("s_out0"), sem("s_out1")]

        s_held = sem("s_held")

        block = ctx.enter_context(nc.Block())

        R_GNN0, R_MOE, R_LIN1 = 0, NT, 2 * NT

        def last_of(i, n, k=1):
            return isinstance(i, int) and i >= n - k

        def hold(eng):
            eng.sem_inc(s_held, 1)

        def pairs(eng, body, n=NT):
            with eng.Fori(0, n // 2 - 1) as j:
                for u in range(2):
                    body(2 * j + u, u)
            for i in (n - 2, n - 1):
                body(i, i % 2)

        @block.sync
        def _(sp):
            for u in range(2):
                sp.sem_inc(s_eout[u], 16)
                sp.sem_inc(s_out[u], 16)
            sp.wait_ge(s_pad, 3)
            full, rest = CH - 1 - 2 * P, E_EDGES - (CH - 1) * P
            for v, edge in enumerate((src_in, dst_in, ew_in)):
                nat = nat_w[:, :, :] if v == 2 else nat_i[:, v, :, :]
                sp.dma_start(nat[:, 0:2, :], edge[0:2 * P * P].rearrange("(a q p) -> q a p", a=2, p=P)).then_inc(s_edges, 16)
                sp.dma_start(nat[0:full, 2, :], edge[2 * P * P:(CH - 1) * P].rearrange("(q p) -> q p", p=P)).then_inc(s_edges, 16)
                sp.dma_start(nat[full:full + 1, 2, 0:rest],
                             edge[(CH - 1) * P:E_EDGES].rearrange("(q p) -> q p", q=1)).then_inc(s_edges, 16)
            sp.wait_ge(s_const, 1)
            sp.dma_start(x[:, 0:NT - 1, :], x_in[0:(NT - 1) * P, :].rearrange("(t p) d -> p t d", p=P)).then_inc(s_x, 16)
            sp.dma_start(x[0:LAST, NT - 1, :], x_in[(NT - 1) * P:N, :]).then_inc(s_x, 16)
            sp.dma_start(bias_b[:, :], bias0_in.partition_broadcast(P)).then_inc(s_bias, 16)
            with nc.allow_non_contiguous_dma(reason="4096 words, once"):
                sp.dma_start(b1c[:, :, :], b1_in.rearrange("e (h p) -> p e h", p=P)).then_inc(s_b1, 16)
            sp.dma_start(wg32[:, :, :], wg_in.rearrange("(k p) e -> p k e", p=P)).then_inc(s_wg, 16)

            sp.wait_ge(s_rows, 1)
            for m, w in enumerate((f1_in, f2_in)):
                pieces = w.rearrange("a b -> (a b)").rearrange("(n p c) -> n p c", p=P, c=2048)
                with sp.Fori(0, 8) as j:
                    for u in range(2):
                        sp.wait_ge(s_abs, 16 * m + 2 * j + u + 1)
                        sp.dma_start(abs_in[:, u, :], pieces[2 * j + u]).then_inc(s_absin[u], 16)

            w1v = w1_in.rearrange("e (g k p) h -> e g p k h", g=2, p=P)
            w2v = w2_in.rearrange("e (g k p) d -> e g p k d", g=2, p=P)

            def expert_piece(e, q):
                piece = w1v[e, q] if q < 2 else w2v[e, q - 2]
                sp.dma_start(wstage[:, q, :].rearrange("p (k h) -> p k h", k=4 if q < 2 else 2), piece).then_inc(s_wst[q], 16)

            sp.wait_ge(s_mm, 1 + NT)
            for q in range(4):
                expert_piece(0, q)

            rows_d = xs_d.rearrange("(t p) c -> t p c", p=P)

            def store(i, u):
                sp.wait_ge(s_xh, R_MOE + i + 1)
                sp.dma_start(rows_d[i][:, 0:D], xh[:, u, :]).then_inc(s_xstore[u], 16)
                sp.wait_ge(s_xl, R_MOE + i + 1)
                sp.dma_start(rows_d[i][:, D:2 * D], xl[:, u, :]).then_inc(s_xstore[u], 16)

            pairs(sp, store)

            sp.wait_ge(s_toki, 1)
            for u in range(2):
                sp.wait_ge(s_xstore[u], 16 * NT)
            sp.dma_start(b2b[:, :], b2_in[0].partition_broadcast(P)).then_inc(s_b2, 16)
            expert_rows = eo_d.rearrange("(e s) d -> e s d", e=NE)

            def expert(e, ep):
                if not last_of(e, NE):
                    for q in range(4):
                        sp.wait_ge(s_wl, 4 * e + q + 1)
                        expert_piece(e + 1, q)
                for s in range(3):
                    u = (ep + s) % 2
                    sp.wait_ge(s_g2r, 3 + 6 * e + 2 * s + 2)
                    sp.dma_start(expert_rows[e][s * P:s * P + SM[s], :], eo[0:SM[s], u, :]).then_inc(s_eout[u], 16)
                if not last_of(e, NE):
                    sp.dma_start(b2b[:, :], b2_in[e + 1].partition_broadcast(P)).then_inc(s_b2, 16)

            pairs(sp, expert, NE)

            sp.dma_start(bias_b[:, :], gb_in.partition_broadcast(P)).then_inc(s_bias, 16)
            w1rows = gw_in.rearrange("(t p) d -> t p d", p=P)

            def w1_rows(i, u):
                sp.wait_ge(s_gnl, i + 1)
                sp.dma_start(gnat[:, u, :], w1rows[i]).then_inc(s_gn[u], 16)

            pairs(sp, w1_rows, KD)

            sp.wait_ge(s_agg, NT)
            f1v = f1_in.rearrange("(j u p) d -> j u p d", p=P, u=4)
            f2v = f2_in.rearrange("(j u p) (b d) -> b j u p d", p=P, u=4, b=4)
            with sp.Fori(0, KD) as j:
                for u in range(4):
                    sp.wait_ge(s_fy, 4 * j + u + 1)
                    sp.dma_start(fnat[:, u, :], f1v[j, u]).then_inc(s_fn[u], 16)
            for b in range(4):
                with sp.Fori(0, 2) as j:
                    for u in range(4):
                        sp.wait_ge(s_fy, 32 + 8 * b + 4 * j + u + 1)
                        sp.dma_start(fnat[:, u, :], f2v[b, j, u]).then_inc(s_fn[u], 16)

            res = out[0:(NT - 1) * P, :].rearrange("(t p) d -> t p d", p=P)

            def result(i, u):
                sp.wait_ge(s_f2r, i + 1)
                if last_of(i, NT):
                    sp.dma_start(out[(NT - 1) * P:N, :], out_t[0:LAST, u, :]).then_inc(s_out[u], 16)
                else:
                    sp.dma_start(res[i], out_t[:, u, :]).then_inc(s_out[u], 16)

            pairs(sp, result)
            for u in range(2):
                sp.wait_ge(s_eout[u], 16 + 16 * 3 * NE // 2)
                sp.wait_ge(s_out[u], 16 + 16 * NT // 2)

        @block.gpsimd
        def _(pool):
            g = nc.gpsimd
            ok = dict(allow_small_or_imprecise_dtypes=True)
            g.memset(x[:, NT - 1, :], 0.0).then_inc(s_const, 1)
            for k, v in enumerate((LN_EPS, -0.5, SX, 1.0)):
                g.memset(consts[:, k:k + 1], v).then_inc(s_const, 1)
            g.memset(zero16[:, :], 0.0).then_inc(s_const, 1)
            g.memset(ones16[:, :], 1.0).then_inc(s_const, 1)
            g.memset(ones32[:, :], 1.0).then_inc(s_const, 1)
            g.iota(iota_r[:, :], [[1, NP]], base=0, channel_multiplier=0, **ok).then_inc(s_const, 1)
            g.iota(q_iota[:, :], [[1, CHP]], base=0, channel_multiplier=0, **ok).then_inc(s_const, 1)
            g.iota(j_iota[:, 0:NG_MAX], [[G, NG_MAX]], base=G, channel_multiplier=0, **ok).then_inc(s_const, 1)
            for k in range(2):
                g.iota(w_lo[:, k:k + 1], [[1, 1]], base=(WIN - 1) * k, channel_multiplier=WIN, **ok).then_inc(s_const, 1)
            pool.wait_ge(s_const, 13)
            g.affine_select(out=id16[:, :], in_=ones16[:, :], pattern=[[-1, P]], compare_op=ALU.is_equal,
                            fill=0.0, base=0, channel_multiplier=1).then_inc(s_const, 1)
            g.affine_select(out=id32[:, :], in_=ones32[:, :], pattern=[[-1, P]], compare_op=ALU.is_equal,
                            fill=0.0, base=0, channel_multiplier=1).then_inc(s_const, 1)
            g.affine_select(out=tri[:, :], in_=ones16[:, :], pattern=[[1, P]], compare_op=ALU.is_ge,
                            fill=0.0, base=0, channel_multiplier=-1).then_inc(s_const, 1)

            def rstd_tile(r, i, k):
                n = NT * r + i
                one = bass.ds(i, 1)
                pool.wait_ge(s_stat, n + 1)
                g.tensor_tensor(rtmp[:, 0:1], mv[:, one, 1], consts[:, 0:1], ALU.add).then_inc(s_pl, 1)
                pool.wait_ge(s_pl, 2 * n + 1)
                g.tensor_tensor(rtmp[:, 1:2], rtmp[:, 0:1], consts[:, 1:2], ALU.pow).then_inc(s_pl, 1)
                pool.wait_ge(s_pl, 2 * n + 2)
                g.tensor_tensor(rstd[:, one], rtmp[:, 1:2], consts[:, k:k + 1], ALU.mult).then_inc(s_rstd, 1)

            with pool.Fori(0, NT) as i:
                rstd_tile(0, i, 2)
            pool.wait_ge(s_bias, 16)
            with pool.Fori(0, NT) as i:
                pool.wait_ge(s_xn, R_GNN0 + i + 1)
                g.tensor_tensor(x[:, i, :], x[:, i, :], bias_b[:, :], ALU.add).then_inc(s_biased, 1)
            with pool.Fori(0, NT) as i:
                rstd_tile(1, i, 2)

            pool.wait_ge(s_mm, 1 + NT)
            g.iota(iota_lo[:, :], [[1, P]], base=0, channel_multiplier=0, **ok).then_inc(s_const, 1)
            g.iota(tok_f[:, :], [[0, 2], [P, NT]], base=0, channel_multiplier=1, **ok).then_inc(s_const, 1)
            g.memset(valid_m[:, :, :, :], 1.0).then_inc(s_const, 1)
            g.memset(scan_m[:, :, :], 1.0).then_inc(s_const, 1)
            pool.wait_ge(s_const, 20)
            for k in range(2):
                g.affine_select(out=valid_m[:, k, NT - 1, :], in_=valid_m[:, k, NT - 1, :],
                                pattern=[[0, NE]], compare_op=ALU.is_ge, fill=0.0, base=LAST - 1,
                                channel_multiplier=-1).then_inc(s_const, 1)
            g.memset(scan_m[:, :, 0:1], 0.0).then_inc(s_const, 1)

            pool.wait_ge(s_toki, 1)
            for u in range(2):
                pool.wait_ge(s_xstore[u], 16 * NT)
            for n in range(3 * NE):
                m = SM[n % 3]
                if n >= 2:
                    pool.wait_ge(s_gtl, n - 1)
                pool.indirect_dma_start(out=gx[0:m, n % 2, :], out_offset=None, in_=xs_d[:, :],
                                        in_offset=bass.IndirectOffsetOnAxis(ap=tok_i[0:m, n:n + 1], axis=0)
                                        ).then_inc(s_g[n % 2], 16)
            for u in range(2):
                pool.wait_ge(s_eout[u], 16 + 16 * 3 * NE // 2)
            for n in range(2 * NT):
                col = (n % 2) * NT + n // 2
                if n >= 4:
                    pool.wait_ge(s_mix, n - 3)
                pool.indirect_dma_start(out=back[:, n % 4, :], out_offset=None, in_=eo_d[:, :],
                                        in_offset=bass.IndirectOffsetOnAxis(ap=slot_i[:, col:col + 1], axis=0)
                                        ).then_inc(s_back[n % 4], 16)
            with pool.Fori(0, NT) as i:
                rstd_tile(2, i, 2)
            pool.wait_ge(s_degp, 1)
            g.tensor_tensor(dinv[:, 0, :], dinv[:, 1, :], consts[:, 1:2].to_broadcast([P, NT]), ALU.pow).then_inc(s_dinv, 1)
            with pool.Fori(0, NT) as i:
                rstd_tile(3, i, 3)

        @block.tensor
        def _(pe):
            mm, tr = nc.tensor.matmul, nc.tensor.transpose
            pe.sem_inc(s_chunk, 10)
            pe.sem_inc(s_mm, 1)
            pe.sem_inc(s_g2, 1)
            pe.sem_inc(s_wtp, 1)

            pe.wait_ge(s_const, 16)
            pe.wait_ge(s_natf, 2)
            pe.wait_ge(s_edges, 16 * 9)
            for v in range(3):
                for a in range(3):
                    last = tr(ps[:, v, a * P:(a + 1) * P], nat_w[:, a, :] if v == 2 else nat_f[:, v, a, :], id32[:, :])
            last.then_inc(s_et, 1)
            pe.wait_ge(s_cmb, 1)
            for v in range(2):
                for a in range(3):
                    last = mm(ps[0:48, 3 + v, a * P:(a + 1) * P], cmb[:, 3 * v + a, :], id16[:, :], start=True, stop=True)
            last.then_inc(s_cmw, 1)
            pe.wait_ge(s_kk, 1)
            for v in range(2):
                last = mm(ps[0:1, 5, 48 * v:48 * v + 48], kk16[:, v:v + 1], id16[0:48, 0:48], start=True, stop=True)
            last.then_inc(s_kr, 1)
            pe.wait_ge(s_rows, 1)

            with pe.register("pe_chunks") as chunks:
                pe.reg_mov(chunks, 0)

                def window(w, u):
                    groups = pe.value_load(rows_i[0:1, 1, bass.ds(w, 1)], min_val=1, max_val=NG_MAX)
                    pe.wait_ge(s_winread, w + 1)
                    for r in range(3):
                        mm(ps[0:96, 3 * u + r, 0:2], zero16[:, :], zero16[:, 0:2], start=True, stop=False,
                           skip_group_check=True)
                    with pe.Fori(0, groups):
                        n = pe.snap(chunks, min_val=0, max_val=1 << 20)
                        for half in range(2):
                            pe.wait_ge(s_st, n + 5 * half + 5)
                            for c in range(RING):
                                pe.wait_ge(s_oh, n + 5 * half + c + 1)
                                for r in range(3):
                                    cols = slice(512 * r, min(512 * r + 512, NP))
                                    last = mm(ps[0:96, 3 * u + r, 0:cols.stop - cols.start], st_e[:, half, c, :],
                                              oh[:, c, cols], start=False, stop=False, skip_group_check=True)
                                last.then_inc(s_chunk, 1)
                        pe.reg_add(chunks, chunks, G)
                    for r in range(3):
                        last = mm(ps[0:96, 3 * u + r, 0:2], zero16[:, :], zero16[:, 0:2], start=False, stop=True,
                                  skip_group_check=True)
                    last.then_inc(s_win, 1)

                window(0, 0)
                with pe.Fori(0, NW // 8 - 1) as bb:
                    for v in range(1, 9):
                        window(8 * bb + v, v % 2)
                for w in range(NW - 7, NW):
                    window(w, w % 2)

            def transposes(n, u):
                pe.wait_ge(s_xh, n + 1)
                if not isinstance(n, int) or n > 0:
                    pe.wait_ge(s_xth, n)
                for k in range(KD):
                    last = tr(bank16(4)[:, k * P:(k + 1) * P], xh[:, u, k * P:(k + 1) * P], id16[:, :])
                last.then_inc(s_th, 1)
                pe.wait_ge(s_xl, n + 1)
                if not isinstance(n, int) or n > 0:
                    pe.wait_ge(s_xtl, n)
                for k in range(KD):
                    last = tr(bank16(5)[:, k * P:(k + 1) * P], xl[:, u, k * P:(k + 1) * P], id16[:, :])
                last.then_inc(s_tl, 1)

            def product(n, u, rh, rl):
                pe.wait_ge(s_xth, n + 1)
                pe.wait_ge(s_xtl, n + 1)
                pe.wait_ge(s_mmread, n + 1)
                for k in range(KD):
                    for a, (lhs, rhs) in enumerate(((xth, rh), (xth, rl), (xtl, rh))):
                        for h in range(2):
                            last = mm(ps[:, 2 * u + h, :], lhs[:, u, k, :], rhs[:, k, h * 512:(h + 1) * 512],
                                      start=(k == 0 and a == 0), stop=(k == KD - 1 and a == 2))
                last.then_inc(s_mm, 1)

            def normalised(r, body):
                transposes(r, 0)

                def step(i, u):
                    if not last_of(i, NT):
                        transposes(r + i + 1, 1 - u)
                    body(i, u)

                pairs(pe, step)

            pe.wait_ge(s_winread, 2 + NW)
            pe.wait_ge(s_built, 2 + NT)
            normalised(R_GNN0, lambda i, u: product(R_GNN0 + i, u, wt_h, wt_l))

            pe.wait_ge(s_small, 3)

            def logits_of(i, u):
                n = R_MOE + i
                pe.wait_ge(s_xth, n + 1)
                pe.wait_ge(s_xtl, n + 1)
                pe.wait_ge(s_mmread, n + 1)
                for k in range(KD):
                    for a, lhs in enumerate((xth, xtl)):
                        last = mm(ps[:, 6 + u, 0:2 * NE], lhs[:, u, k, :], wgs[:, k, :],
                                  start=(k == 0 and a == 0), stop=(k == KD - 1 and a == 1))
                last.then_inc(s_mm, 1)

            normalised(R_MOE, logits_of)
            pe.wait_ge(s_mask, 1)
            masks = mask[:, :, :, :].rearrange("p k t e -> p (k t e)")
            mm(ps[:, 0, 0:2 * NT * NE], tri[:, :], masks, start=True, stop=True)
            mm(ps[:, 1, 0:2 * NT * NE], ones16[:, :], masks, start=True, stop=True).then_inc(s_cum, 1)
            pe.wait_ge(s_ohr, 1)
            for n in range(2 * NT):
                last = mm(ps[:, 2, 0:3 * NE], oh_lo[:, n, :], oh_hi2[:, n, :], start=(n == 0), stop=(n == 2 * NT - 1))
            last.then_inc(s_tok, 1)
            pe.wait_ge(s_toki, 1)

            def gathered(e, ep):
                for s in range(3):
                    m, n, u = SM[s], 3 * e + s, (ep + s) % 2
                    pe.wait_ge(s_g[u], 8 * n - 8 * u + 16)
                    for part, (b, read, done) in enumerate(((4, s_gch, s_gth), (5, s_gcl, s_gtl))):
                        pe.wait_ge(read, n + 1)
                        hold(pe)
                        for k in range(KD):
                            c = part * D + k * P
                            last = tr(bank16(b)[:, k * P:k * P + m], gx[0:m, u, c:c + P], id16[0:m, 0:m])
                        last.then_inc(done, 1)

            def expert(e, ep):
                pe.wait_ge(s_gch, 1 + 3 * e + 3)
                pe.wait_ge(s_gcl, 1 + 3 * e + 3)
                pe.wait_ge(s_wl, 4 * e + 2)
                for hb in range(KH):
                    pe.wait_ge(s_g1r, 4 * e + hb + 1)
                    for k in range(KD):
                        for a, (lhs, rhs) in enumerate(((w1h, xdh), (w1h, xdl), (w1l, xdh))):
                            last = mm(ps[:, 6 + hb % 2, 0:CAP], lhs[:, k, hb * P:(hb + 1) * P], rhs[:, k, :],
                                      start=(k == 0 and a == 0), stop=(k == KD - 1 and a == 2))
                    last.then_inc(s_g1, 1)
                if not last_of(e, NE):
                    gathered(e + 1, 1 - ep)
                pe.wait_ge(s_hl, 2 + 4 * e + 4)
                pe.wait_ge(s_wl, 4 * e + 4)
                for s in range(3):
                    m = SM[s]
                    for h in range(2):
                        pe.wait_ge(s_g2r, 6 * e + 2 * s + h + 1)
                        for k in range(KH):
                            for a, (lhs, rhs) in enumerate(((hth, w2h), (hth, w2l), (htl, w2h))):
                                last = mm(ps[0:m, (2 * s + h) % 3, :], lhs[:, k, s * P:s * P + m],
                                          rhs[:, k, h * 512:(h + 1) * 512],
                                          start=(k == 0 and a == 0), stop=(k == KH - 1 and a == 2))
                        last.then_inc(s_g2, 1)

            gathered(0, 0)
            pairs(pe, expert, NE)

            def w1_t(i, u):
                pe.wait_ge(s_gnh, i + 1)
                pe.wait_ge(s_wth, i + 1)
                for k in range(KD):
                    tr(bank16(4)[:, k * P:(k + 1) * P], gnh[:, u, k * P:(k + 1) * P], id16[:, :])
                pe.wait_ge(s_gnl, 2 + i + 1)
                pe.wait_ge(s_wtl, i + 1)
                for k in range(KD):
                    last = tr(bank16(5)[:, k * P:(k + 1) * P], gnl[:, u, k * P:(k + 1) * P], id16[:, :])
                last.then_inc(s_wtp, 1)

            pairs(pe, w1_t, KD)
            for i in range(NT):
                for b in range(NT):
                    for a, t in enumerate((at_h, at_l)):
                        last = mm(ps[:, 6, i:i + 1], t[:, b, i * P:(i + 1) * P], ones16[:, 0:1],
                                  start=(b == 0 and a == 0), stop=(b == NT - 1 and a == 1))
            last.then_inc(s_deg, 1)
            pe.wait_ge(s_wth, 1 + KD)
            pe.wait_ge(s_wtl, 1 + KD)
            normalised(R_LIN1, lambda i, u: product(R_LIN1 + i, u, gwt_h, gwt_l))

            pe.wait_ge(s_hsh, NT)
            pe.wait_ge(s_hsl, 1 + NT)

            def agg(i, u):
                pe.wait_ge(s_aggread, i + 1)
                for b in range(NT):
                    for a, (lhs, rhs) in enumerate(((at_h, hs_h), (at_h, hs_l), (at_l, hs_h))):
                        for h in range(2):
                            mm(ps[:, 2 * u + h, :], lhs[:, b, bass.ds(i * P, P)], rhs[:, b, h * 512:(h + 1) * 512],
                               start=(b == 0 and a == 0), stop=False)
                for a, rhs in enumerate((hs_h, hs_l)):
                    flat = rhs[:, :, :].rearrange("p t d -> p (t d)")
                    for h in range(2):
                        last = mm(ps[:, 2 * u + h, :], id16[:, :], flat[:, bass.ds(i * D + h * 512, 512)],
                                  start=False, stop=(a == 1))
                last.then_inc(s_agg, 1)

            pairs(pe, agg)

            pe.wait_ge(s_swp, 1)
            mm(ps[:, 6, 0:2], ones32[:, :], sw[:, 0:2], start=True, stop=True).then_inc(s_swm, 1)
            with pe.Fori(0, 32) as j:
                for u in range(2):
                    pe.wait_ge(s_fq, 2 + 2 * j + u + 1)
                    pe.wait_ge(s_fc, 2 * j + u + 1)
                    for k in range(KD):
                        last = tr(bank16(4 + u)[:, k * P:(k + 1) * P], fq[:, u, k * P:(k + 1) * P], id16[:, :])
                    last.then_inc(s_ft, 1)

            def ffn_in(i, u):
                pe.wait_ge(s_xq, i + 1)
                for k in range(KD):
                    last = tr(bank16(6)[:, k * P:(k + 1) * P], xq[:, u, k * P:(k + 1) * P], id16[:, :])
                last.then_inc(s_xqt, 1)
                pe.wait_ge(s_xqc, i + 1)
                for n in range(8):
                    pe.wait_ge(s_ge, 8 * i + n + 1)
                    hold(pe)
                    for k in range(KD):
                        last = mm(ps[:, n % 4, :], xqt[:, u, k, :], w1q[:, k, n * 512:(n + 1) * 512],
                                  start=(k == 0), stop=(k == KD - 1))
                    last.then_inc(s_f1, 1)

            def ffn_out(i):
                def hidden_t(q):
                    for k in range(KD):
                        last = tr(bank16(7 - q % 2)[:, k * P:(k + 1) * P], hq[:, (8 * q + k) * P:(8 * q + k + 1) * P], id16[:, :])
                    last.then_inc(s_hqt, 1)

                pe.wait_ge(s_hq, 2 + i + 1)
                hidden_t(0)
                hidden_t(1)
                if not isinstance(i, int) or i > 0:
                    pe.wait_ge(s_f2r, i)
                for q in range(4):
                    pe.wait_ge(s_hqc, 4 * i + q + 1)
                    hold(pe)
                    if 1 <= q <= 2:
                        hidden_t(q + 1)
                    for k in range(8 * q, 8 * q + 8):
                        for h in range(2):
                            last = mm(ps[:, 4 + h, :], hqt[:, k, :], w2q[:, k, h * 512:(h + 1) * 512],
                                      start=(k == 0), stop=(k == KF - 1))
                last.then_inc(s_f2, 1)

            pe.wait_ge(s_fc, 2 + 64)
            ffn_in(0, 0)
            ffn_in(1, 1)
            ffn_out(0)

            def ffn(i, u):
                ffn_in(i + 1, 1 - u)
                ffn_out(i)

            with pe.Fori(0, NT // 2 - 1) as j:
                ffn(2 * j + 1, 1)
                ffn(2 * j + 2, 0)
            ffn_out(NT - 1)

        @block.scalar
        def _(act):
            cp = nc.scalar.activation
            act.sem_inc(s_winread, 2)
            act.sem_inc(s_abs, 2)
            act.sem_inc(s_gch, 1)
            act.sem_inc(s_g1r, 2)
            act.sem_inc(s_wth, 1)
            act.sem_inc(s_fy, 4)
            act.sem_inc(s_ge, 4)

            def window(w, u, j, blk, ub):
                act.wait_ge(s_win, w + 1)
                act.wait_ge(s_built, blk + 1)
                rows = slice(WIN * j, WIN * j + WIN)
                pw = ps[:, 3 * u:3 * u + 3, :].rearrange("p b c -> p (b c)")
                cp(st_a[rows, ub, :], pw[0:32, 0:NP], ACT.Copy).then_inc(s_stage, 1)
                cp(st_wh[rows, ub, :], pw[32:64, 0:D], ACT.Copy).then_inc(s_stage, 1)
                cp(st_wl[rows, ub, :], pw[64:96, 0:D], ACT.Copy).then_inc(s_stage, 1)
                act.wait_ge(s_stage, 3 * w + 3)
                act.sem_inc(s_winread, 1)

            def abs_piece(n, u):
                act.wait_ge(s_absin[u], 8 * n - 8 * u + 16)
                cp(abs_in[:, u, :], abs_in[:, u, :], ACT.Abs, accum_out=abs_acc[:, bass.ds(n, 1)]).then_inc(s_abs, 1)

            window(0, 0, 0, 0, 0)
            with act.Fori(0, NW // 8 - 1) as bb:
                for v in range(1, 9):
                    window(8 * bb + v, v % 2, v % 4, 2 * bb + v // 4, (v // 4) % 2)
                    abs_piece(8 * bb + v - 1, (v - 1) % 2)
            for w in range(NW - 7, NW):
                window(w, w % 2, w % 4, w // 4, (w // 4) % 2)

            def high(n, u):
                act.wait_ge(s_xn, n + 1)
                cp(xh[:, u, :], xn[:, u, :], ACT.Copy).then_inc(s_xh, 1)

            def copy_high(n, u):
                act.wait_ge(s_th, n + 1)
                cp(xth[:, u, :, :].rearrange("p k c -> p (k c)"), bank16(4), ACT.Copy).then_inc(s_xth, 1)

            def normalised(r, body, stored=False):
                high(r, 0)
                high(r + 1, 1)
                copy_high(r, 0)

                def step(i, u):
                    if not last_of(i, NT):
                        act.wait_ge(s_mm, r + i + 1)
                        copy_high(r + i + 1, 1 - u)
                    if not last_of(i, NT, 2):
                        act.wait_ge(s_tl, r + i + 1)
                        if stored:
                            act.wait_ge(s_xstore[u], 16 * i + 32 - 16 * u)
                        high(r + i + 2, u)
                    body(i, u)

                pairs(act, step)

            act.wait_ge(s_built, 2 + NT)
            normalised(R_GNN0, lambda i, u: None)
            act.wait_ge(s_tl, R_MOE)
            act.wait_ge(s_mm, 1 + R_MOE)
            normalised(R_MOE, lambda i, u: None, stored=True)
            act.wait_ge(s_gd, 1)
            cp(rt[:, 1, 0:NT], rt[:, 0, 0:NT], ACT.Exp).then_inc(s_ex, 1)

            b1s = b1c[:, :, :].rearrange("p e h -> p (e h)")

            def split_high(e, q):
                act.wait_ge(s_wst[q], 16 * e + 16)
                w = w1h[:, 4 * q:4 * q + 4, :] if q < 2 else w2h[:, 2 * q - 4:2 * q - 2, :]
                cp(w.rearrange("p k h -> p (k h)"), wstage[:, q, :], ACT.Copy, scale=SW).then_inc(s_wh, 1)

            def gathered(e):
                for s in range(3):
                    m = SM[s]
                    act.wait_ge(s_gth, 3 * e + s + 1)
                    cp(xdh[:, :, s * P:s * P + m], bank16(4).rearrange("p (k c) -> p k c", k=KD)[:, :, 0:m],
                       ACT.Copy).then_inc(s_gch, 1)

            def expert(e, ep):
                for hb in range(KH):
                    act.wait_ge(s_g1, 4 * e + hb + 1)
                    act.wait_ge(s_hl, 4 * e + hb + 1)
                    if hb == 0:
                        act.wait_ge(s_g2, 6 * e + 1)
                    cp(ht32[:, hb % 2, :], ps[:, 6 + hb % 2, 0:CAP], ACT.Relu, bias=b1s[:, bass.ds(4 * e + hb, 1)],
                       scale=SH / (SX * SW)).then_inc(s_g1r, 1)
                    act.wait_ge(s_g1r, 2 + 4 * e + hb + 1)
                    cp(hth[:, hb, :], ht32[:, hb % 2, :], ACT.Copy).then_inc(s_hh, 1)
                if not last_of(e, NE):
                    gathered(e + 1)
                    for q in range(2):
                        split_high(e + 1, q)
                    act.wait_ge(s_g2, 1 + 6 * e + 6)
                    for q in range(2, 4):
                        split_high(e + 1, q)

            act.wait_ge(s_toki, 1)
            act.wait_ge(s_small, 3)
            for q in range(4):
                split_high(0, q)
            gathered(0)
            pairs(act, expert, NE)

            act.wait_ge(s_g2, 1 + 6 * NE)

            def w1_part(i, u):
                act.wait_ge(s_gn[u], 8 * i - 8 * u + 16)
                act.wait_ge(s_wtp, i + 1)
                cp(gnh[:, u, :], gnat[:, u, :], ACT.Copy, scale=SW).then_inc(s_gnh, 1)
                act.wait_ge(s_wtp, 1 + i + 1)
                cp(gwt_h[:, :, bass.ds(i * P, P)], bank16(4).rearrange("p (k c) -> p k c", k=KD), ACT.Copy).then_inc(s_wth, 1)

            pairs(act, w1_part, KD)

            def h_high(i, u):
                act.wait_ge(s_mmread, 2 + R_LIN1 + i + 1)
                flat = hs_h[:, :, :].rearrange("p t d -> p (t d)")
                cp(flat[:, bass.ds(i * D, D)], h32[:, :], ACT.Copy, scale=dinv[:, 1, bass.ds(i, 1)]).then_inc(s_hsh, 1)

            act.wait_ge(s_dinv2, 2)
            normalised(R_LIN1, h_high)

            act.wait_ge(s_sw, 2)
            with act.Fori(0, 16) as j:
                for u in range(4):
                    n = 4 * j + u
                    act.wait_ge(s_fn[u], 16 * j + 16)
                    act.wait_ge(s_fq, n + 1)
                    hold(act)
                    cp(fy[:, u % 2, :], fnat[:, u, :], ACT.Identity, bias=sw[:, 6:7],
                       scale=fwinv[:, bass.ds(j, 1)]).then_inc(s_fy, 1)

            def ffn_in(i, u):
                act.wait_ge(s_xqt, i + 1)
                cp(xqt[:, u, :, :].rearrange("p k c -> p (k c)"), bank16(6), ACT.Copy).then_inc(s_xqc, 1)
                act.wait_ge(s_hq, i + 1)
                for n in range(8):
                    act.wait_ge(s_f1, 8 * i + n + 1)
                    cp(hf[:, u, n * 512:(n + 1) * 512], ps[:, n % 4, :], ACT.Gelu, scale=fs[:, u, 3:4]).then_inc(s_ge, 1)

            def ffn_out(i):
                for q in range(4):
                    act.wait_ge(s_hqt, 4 * i + q + 1)
                    cp(hqt[:, 8 * q:8 * q + 8, :].rearrange("p k c -> p (k c)"), bank16(7 - q % 2), ACT.Copy).then_inc(s_hqc, 1)

            act.wait_ge(s_fc, 2 + 64)
            ffn_in(0, 0)
            ffn_in(1, 1)
            ffn_out(0)
            with act.Fori(0, NT // 2 - 1) as j:
                ffn_in(2 * j + 2, 0)
                ffn_out(2 * j + 1)
                ffn_in(2 * j + 3, 1)
                ffn_out(2 * j + 2)
            ffn_out(NT - 1)

        @block.vector
        def _(dve):
            v = nc.vector
            steps = Steps(dve, s_dv)

            def do(ins):
                steps.inc(ins)
                steps.wait()

            dve.sem_inc(s_built, 2)
            dve.sem_inc(s_mmread, 2)
            dve.sem_inc(s_gcl, 1)
            dve.sem_inc(s_hl, 2)
            dve.sem_inc(s_g2r, 3)
            dve.sem_inc(s_gnl, 2)
            dve.sem_inc(s_hsl, 1)
            dve.sem_inc(s_wtl, 1)
            dve.sem_inc(s_aggread, 2)
            dve.sem_inc(s_fq, 2)
            dve.sem_inc(s_fc, 2)
            dve.sem_inc(s_hq, 2)

            v.memset(nat_i[:, 0, 2, :], -1).then_inc(s_pad, 1)
            v.memset(nat_i[:, 1, 2, :], NP - 1).then_inc(s_pad, 1)
            v.memset(nat_w[:, 2, :], 0.0).then_inc(s_pad, 1)
            v.memset(sw[:, 6:7], MAGIC).then_inc(s_small, 1)
            dve.wait_ge(s_edges, 16 * 9)
            for a in range(2):
                v.tensor_copy(nat_f[:, a, :, :], nat_i[:, a, :, :]).then_inc(s_natf, 1)
            dve.wait_ge(s_natf, 2)
            steps.inc(v.tensor_reduce(cm[:, 0, :], nat_f[:, 1, :, :], AX.X, ALU.min))
            do(v.tensor_reduce(cm[:, 1, :], nat_f[:, 1, :, :], AX.X, ALU.max))
            v.tensor_copy(cmb[:, :, :], cm[:, :, :].rearrange("p v a -> p (v a)").unsqueeze(2).to_broadcast([P, 6, 48])
                          ).then_inc(s_cmb, 1)
            dve.wait_ge(s_et, 1)
            steps.inc(v.tensor_copy(src_t[:, :], ps[:, 0, 0:CHP]))
            steps.inc(v.tensor_copy(dst_t[:, :], ps[:, 1, 0:CHP]))
            do(v.tensor_scalar(ew32_t[:, :], ps[:, 2, 0:CHP], SW, None, ALU.mult))
            do(v.tensor_copy(ewh_t[:, :], ew32_t[:, :]))
            do(v.tensor_tensor(ewl_t[:, :], ew32_t[:, :], ewh_t[:, :], ALU.subtract))
            dve.wait_ge(s_const, 16)
            dve.wait_ge(s_cmw, 1)
            do(v.tensor_scalar(ov[:, 0, 0:CH], ps[0:48, 4, 0:CH], w_lo[:, 0:1], None, ALU.is_ge))
            do(v.scalar_tensor_tensor(out=ov[:, 1, 0:CH], in0=ps[0:48, 3, 0:CH], scalar=w_lo[:, 1:2], in1=ov[:, 0, 0:CH],
                                      op0=ALU.is_le, op1=ALU.mult))
            do(v.scalar_tensor_tensor(out=ov[:, 0, 0:CH], in0=q_iota[:, 0:CH], scalar=-512.0, in1=ov[:, 1, 0:CH],
                                      op0=ALU.add, op1=ALU.mult))
            do(v.tensor_reduce(kk[:, 0:1], ov[:, 0, 0:CH], AX.X, ALU.min))
            do(v.tensor_scalar(kk[:, 1:2], kk[:, 0:1], 512.0, float(CH), ALU.add, ALU.min))
            do(v.scalar_tensor_tensor(out=ov[:, 0, 0:CH], in0=q_iota[:, 0:CH], scalar=1.0, in1=ov[:, 1, 0:CH],
                                      op0=ALU.add, op1=ALU.mult))
            do(v.tensor_reduce(kk[:, 2:3], ov[:, 0, 0:CH], AX.X, ALU.max))
            do(v.tensor_tensor(kk[:, 3:4], kk[:, 2:3], kk[:, 1:2], ALU.subtract))
            do(v.tensor_scalar(ov[:, 0, 0:NG_MAX], j_iota[:, 0:NG_MAX], kk[:, 3:4], None, ALU.is_lt))
            do(v.tensor_reduce(kk[:, 4:5], ov[:, 0, 0:NG_MAX], AX.X, ALU.add))
            steps.inc(v.tensor_copy(kk16[:, 0:1], kk[:, 1:2]))
            v.tensor_scalar(kk16[:, 1:2], kk[:, 4:5], 1.0, None, ALU.add).then_inc(s_kk, 1)
            dve.wait_ge(s_kr, 1)
            v.tensor_copy(rows_i[:, :, :].rearrange("p a w -> p (a w)"), ps[0:1, 5, 0:96]).then_inc(s_rows, 1)
            dve.wait_ge(s_rows, 1)

            dve.wait_ge(s_b1, 16)
            v.tensor_scalar(b1c[:, :, :], b1c[:, :, :], SH, None, ALU.mult).then_inc(s_small, 1)
            dve.wait_ge(s_wg, 16)
            do(v.tensor_scalar(wg32[:, :, :], wg32[:, :, :], SW, None, ALU.mult))
            do(v.tensor_copy(wgs[:, :, 0:NE], wg32[:, :, :]))
            v.tensor_tensor(wgs[:, :, NE:2 * NE], wg32[:, :, :], wgs[:, :, 0:NE], ALU.subtract).then_inc(s_small, 1)

            def statistics(n, i):
                hold(dve)
                for h in range(2):
                    v.bn_stats(stats[:, h, :], x[:, i, h * 512:(h + 1) * 512]).then_inc(s_bn, 1)
                dve.wait_ge(s_bn, 3 * n + 2)
                hold(dve)
                v.bn_aggr(mv_one[:, :], stats[:, :, :]).then_inc(s_bn, 1)
                dve.wait_ge(s_bn, 3 * n + 3)
                v.tensor_copy(mv[:, i, :], mv_one[:, :]).then_inc(s_stat, 1)

            dve.wait_ge(s_x, 32)
            with dve.Fori(0, NT) as i:
                statistics(i, i)

            with dve.register("dve_chunks") as chunks, dve.register("dve_first") as first:
                dve.reg_mov(chunks, 0)

                def window(w):
                    dve.reg_load(first, rows_i[0:1, 0, bass.ds(w, 1)])
                    groups = dve.value_load(rows_i[0:1, 1, bass.ds(w, 1)], min_val=1, max_val=NG_MAX)
                    with dve.Fori(0, groups):
                        n = dve.snap(chunks, min_val=0, max_val=1 << 20)
                        at = dve.snap(first, min_val=0, max_val=CHP - G)
                        for half in range(2):
                            five = bass.ds(at + 5 * half, RING)
                            dve.wait_ge(s_chunk, n + 5 * half + 5)
                            v.tensor_copy(src_g[:, half, :], src_t[:, five])
                            st = st_e[:, half, :, :]
                            v.tensor_tensor(st[:, :, 0:WIN], iota_r[:, bass.ds(w * WIN, WIN)].unsqueeze(1).to_broadcast([P, RING, WIN]),
                                            dst_t[:, five].unsqueeze(2).to_broadcast([P, RING, WIN]),
                                            ALU.is_equal).then_inc(s_group, 5)
                            dve.wait_ge(s_group, n + 5 * half + 5)
                            v.tensor_tensor(st[:, :, WIN:2 * WIN], st[:, :, 0:WIN],
                                            ewh_t[:, five].unsqueeze(2).to_broadcast([P, RING, WIN]), ALU.mult)
                            v.tensor_tensor(st[:, :, 2 * WIN:3 * WIN], st[:, :, 0:WIN],
                                            ewl_t[:, five].unsqueeze(2).to_broadcast([P, RING, WIN]),
                                            ALU.mult).then_inc(s_st, 5)
                            for c in range(RING):
                                dve.wait_ge(s_chunk, n + 5 * half + c + 6)
                                v.tensor_scalar(oh[:, c, :], iota_r[:, 0:NP], src_g[:, half, c:c + 1], None,
                                                ALU.is_equal).then_inc(s_oh, 1)
                        dve.reg_add(chunks, chunks, G)
                        dve.reg_add(first, first, G)

                def block_parts(b, ub):
                    dve.wait_ge(s_stage, 12 * b + 12)
                    v.tensor_copy(at_h[:, b, :], st_a[:, ub, :]).then_inc(s_blk, 1)
                    v.tensor_tensor(st_wh[:, ub, :], st_wh[:, ub, :], st_wl[:, ub, :], ALU.add).then_inc(s_blk, 1)
                    dve.wait_ge(s_blk, 3 * b + 2)
                    v.tensor_tensor(at_l[:, b, :], st_a[:, ub, :], at_h[:, b, :], ALU.subtract)
                    v.tensor_copy(wt_h[:, b, :], st_wh[:, ub, :]).then_inc(s_blk, 1)
                    dve.wait_ge(s_blk, 3 * b + 3)
                    v.tensor_tensor(wt_l[:, b, :], st_wh[:, ub, :], wt_h[:, b, :], ALU.subtract).then_inc(s_built, 1)

                window(0)
                with dve.Fori(0, NW // 8 - 1) as bb:
                    for k in range(1, 9):
                        window(8 * bb + k)
                        if k % 4 == 0:
                            block_parts(2 * bb + k // 4 - 1, k // 4 - 1)
                for w in range(NW - 7, NW):
                    window(w)
                    if w % 4 == 0:
                        block_parts(w // 4 - 1, (w // 4 - 1) % 2)
                block_parts(NT - 1, (NT - 1) % 2)

            def norm(r, i, u):
                dve.wait_ge(s_rstd, r + i + 1)
                v.tensor_scalar(xn[:, u, :], x[:, i, :], mv[:, i, 0:1], rstd[:, bass.ds(i, 1)], ALU.subtract, ALU.mult).then_inc(s_xn, 1)

            def low(n, u):
                dve.wait_ge(s_xh, n + 1)
                v.tensor_tensor(xl[:, u, :], xn[:, u, :], xh[:, u, :], ALU.subtract).then_inc(s_xl, 1)

            def copy_low(n, u):
                dve.wait_ge(s_tl, n + 1)
                v.tensor_copy(xtl[:, u, :, :].rearrange("p k c -> p (k c)"), bank16(5)).then_inc(s_xtl, 1)

            def normalised(r, body, stored=False):
                norm(r, 0, 0)
                norm(r, 1, 1)
                low(r, 0)
                low(r + 1, 1)
                copy_low(r, 0)

                def step(i, u):
                    if not last_of(i, NT):
                        dve.wait_ge(s_mm, r + i + 1)
                        copy_low(r + i + 1, 1 - u)
                    if not last_of(i, NT, 2):
                        norm(r, i + 2, u)
                        low(r + i + 2, u)
                    body(i, u)

                pairs(dve, step)

            def pair_banks(u):
                return ps[:, 2 * u:2 * u + 2, :].rearrange("p b c -> p (b c)")

            def gnn0(i, u):
                dve.wait_ge(s_biased, i + 1)
                dve.wait_ge(s_mm, 1 + R_GNN0 + i + 1)
                v.scalar_tensor_tensor(out=x[:, i, :], in0=pair_banks(u), scalar=1.0 / (SX * SW), in1=x[:, i, :],
                                       op0=ALU.mult, op1=ALU.add).then_inc(s_mmread, 1)
                dve.wait_ge(s_mmread, 2 + R_GNN0 + i + 1)
                statistics(NT + i, i)

            normalised(R_GNN0, gnn0)

            def logits_of(i, u):
                dve.wait_ge(s_mm, 1 + R_MOE + i + 1)
                v.tensor_reduce(logits[:, i, :], ps[:, 6 + u, 0:2 * NE].rearrange("p (a e) -> p e a", a=2), AX.X,
                                ALU.add).then_inc(s_mmread, 1)

            normalised(R_MOE, logits_of)
            dve.wait_ge(s_mmread, 2 + R_MOE + NT)
            dve.wait_ge(s_const, 23)
            do(v.tensor_scalar(logits[:, :, :], logits[:, :, :], 1.0 / (SX * SW), None, ALU.mult))
            for t in range(NT):
                steps.inc(v.max(lmax[:, t, :], logits[:, t, :]))
            steps.wait()
            for t in range(NT):
                steps.inc(v.max_index(lidx[:, t, :], lmax[:, t, :], logits[:, t, :]))
            v.tensor_tensor(rt[:, 0, 0:NT], lmax[:, :, 1], lmax[:, :, 0], ALU.subtract).then_inc(s_gd, 1)
            steps.wait()
            do(v.tensor_copy(lidf[:, :, :], lidx[:, :, :]))
            for k in range(2):
                steps.inc(v.tensor_tensor(mask[:, k, :, :], iota_lo[:, 0:NE].unsqueeze(1).to_broadcast([P, NT, NE]),
                                          lidf[:, :, k:k + 1].to_broadcast([P, NT, NE]), ALU.is_equal))
                steps.inc(v.tensor_copy(rt[:, 5, k * NT:(k + 1) * NT], lidf[:, :, k]))
            steps.wait()
            v.tensor_tensor(mask[:, :, :, :], mask[:, :, :, :], valid_m[:, :, :, :], ALU.mult).then_inc(s_mask, 1)
            dve.wait_ge(s_ex, 1)
            do(v.tensor_scalar(rt[:, 2, 0:NT], rt[:, 1, 0:NT], 1.0, None, ALU.add))
            do(v.reciprocal(gates[:, 0, :], rt[:, 2, 0:NT]))
            do(v.tensor_tensor(gates[:, 1, :], rt[:, 1, 0:NT], gates[:, 0, :], ALU.mult))
            dve.wait_ge(s_cum, 1)
            dve.wait_ge(s_mask, 1)
            by_e = "p (n e) -> p e n"
            do(v.tensor_copy(tot_e[:, :, :], ps[:, 1, 0:2 * NT * NE].rearrange(by_e, e=NE)))
            do(v.tensor_tensor_scan(scan_o[:, :, :].rearrange("p e n -> p (e n)"), scan_m[:, :, :].rearrange("p e n -> p (e n)"),
                                    tot_e[:, :, :].rearrange("p e n -> p (e n)"), 0.0, ALU.mult, ALU.add))
            do(v.tensor_tensor(scan_o[:, :, :], scan_o[:, :, :], tot_e[:, :, :], ALU.subtract))
            do(v.scalar_tensor_tensor(out=loc3[:, :, :], in0=ps[:, 0, 0:2 * NT * NE].rearrange("p (n e) -> p n e", e=NE),
                                      scalar=-1.0, in1=scan_o[:, :, :].rearrange("p e n -> p n e"), op0=ALU.add, op1=ALU.add))
            do(v.tensor_tensor(loc3[:, :, :], loc3[:, :, :], mask[:, :, :, :].rearrange("p k t e -> p (k t) e"), ALU.mult))
            do(v.tensor_reduce(rt[:, 2, :], loc3[:, :, :], AX.X, ALU.add))
            do(v.tensor_scalar(rt[:, 3, :], rt[:, 2, :], float(CAP), None, ALU.is_lt))
            steps.inc(v.tensor_tensor(gates[:, :, :].rearrange("p k t -> p (k t)"), gates[:, :, :].rearrange("p k t -> p (k t)"),
                                      rt[:, 3, :], ALU.mult))
            do(v.tensor_tensor(rt[:, 4, :], rt[:, 3, :], valid_m[:, :, :, 0].rearrange("p k t -> p (k t)"), ALU.mult))
            do(v.tensor_scalar(rt[:, 6, :], rt[:, 2, :], float(CAP - 1), None, ALU.min))
            do(v.scalar_tensor_tensor(out=rt[:, 7, :], in0=rt[:, 5, :], scalar=float(CAP), in1=rt[:, 6, :],
                                      op0=ALU.mult, op1=ALU.add))
            steps.inc(v.tensor_copy(slot_i[:, :], rt[:, 7, :]))
            steps.inc(v.tensor_scalar(rt[:, 8, :], rt[:, 2, :], float(P), None, ALU.is_ge))
            do(v.tensor_scalar(rt[:, 9, :], rt[:, 2, :], float(2 * P), None, ALU.is_ge))
            do(v.tensor_tensor(rt[:, 8, :], rt[:, 8, :], rt[:, 9, :], ALU.add))
            steps.inc(v.scalar_tensor_tensor(out=rt[:, 10, :], in0=rt[:, 8, :], scalar=-float(P), in1=rt[:, 2, :],
                                             op0=ALU.mult, op1=ALU.add))
            do(v.scalar_tensor_tensor(out=rt[:, 11, :], in0=rt[:, 5, :], scalar=3.0, in1=rt[:, 8, :],
                                      op0=ALU.mult, op1=ALU.add))
            do(v.scalar_tensor_tensor(out=rt[:, 9, :], in0=rt[:, 11, :], scalar=1.0, in1=rt[:, 4, :],
                                      op0=ALU.add, op1=ALU.mult))
            do(v.tensor_scalar(rt[:, 11, :], rt[:, 9, :], -1.0, None, ALU.add))
            steps.inc(v.tensor_tensor(oh_lo[:, :, :], iota_lo[:, :].unsqueeze(1).to_broadcast([P, 2 * NT, P]),
                                      rt[:, 10, :].unsqueeze(2).to_broadcast([P, 2 * NT, P]), ALU.is_equal))
            do(v.tensor_tensor(oh_hi[:, :, :], iota_lo[:, 0:3 * NE].unsqueeze(1).to_broadcast([P, 2 * NT, 3 * NE]),
                               rt[:, 11, :].unsqueeze(2).to_broadcast([P, 2 * NT, 3 * NE]), ALU.is_equal))
            v.tensor_tensor(oh_hi2[:, :, :], oh_hi[:, :, :], tok_f[:, :].unsqueeze(2).to_broadcast([P, 2 * NT, 3 * NE]),
                            ALU.mult).then_inc(s_ohr, 1)
            dve.wait_ge(s_tok, 1)
            v.tensor_copy(tok_i[:, :], ps[:, 2, 0:3 * NE]).then_inc(s_toki, 1)

            def split_low(e, q):
                dve.wait_ge(s_wh, 4 * e + q + 1)
                hi, lo = (w1h, w1l) if q < 2 else (w2h, w2l)
                part = slice(4 * q, 4 * q + 4) if q < 2 else slice(2 * q - 4, 2 * q - 2)
                flat = "p k h -> p (k h)"
                v.scalar_tensor_tensor(out=lo[:, part, :].rearrange(flat), in0=wstage[:, q, :], scalar=SW,
                                       in1=hi[:, part, :].rearrange(flat), op0=ALU.mult, op1=ALU.subtract).then_inc(s_wl, 1)

            def gathered(e):
                for s in range(3):
                    m = SM[s]
                    dve.wait_ge(s_gtl, 3 * e + s + 1)
                    v.tensor_copy(xdl[:, :, s * P:s * P + m],
                                  bank16(5).rearrange("p (k c) -> p k c", k=KD)[:, :, 0:m]).then_inc(s_gcl, 1)

            def expert(e, ep):
                for hb in range(KH):
                    dve.wait_ge(s_hh, 4 * e + hb + 1)
                    v.tensor_tensor(htl[:, hb, :], ht32[:, hb % 2, :], hth[:, hb, :], ALU.subtract).then_inc(s_hl, 1)
                if not last_of(e, NE):
                    gathered(e + 1)
                    for q in range(2):
                        split_low(e + 1, q)
                dve.wait_ge(s_b2, 16 * e + 16)
                for s in range(3):
                    m, u = SM[s], (ep + s) % 2
                    dve.wait_ge(s_eout[u], 24 * e + 8 * s - 8 * u + 16)
                    for h in range(2):
                        dve.wait_ge(s_g2, 1 + 6 * e + 2 * s + h + 1)
                        cols = slice(h * 512, (h + 1) * 512)
                        v.scalar_tensor_tensor(out=eo[0:m, u, cols], in0=ps[0:m, (2 * s + h) % 3, :], scalar=1.0 / (SH * SW),
                                               in1=b2b[0:m, cols], op0=ALU.mult, op1=ALU.add).then_inc(s_g2r, 1)
                if not last_of(e, NE):
                    for q in range(2, 4):
                        split_low(e + 1, q)

            dve.wait_ge(s_toki, 1)
            for q in range(4):
                split_low(0, q)
            gathered(0)
            pairs(dve, expert, NE)

            def w1_part(i, u):
                dve.wait_ge(s_gnh, i + 1)
                dve.wait_ge(s_wtp, i + 1)
                v.scalar_tensor_tensor(out=gnl[:, u, :], in0=gnat[:, u, :], scalar=SW, in1=gnh[:, u, :],
                                       op0=ALU.mult, op1=ALU.subtract).then_inc(s_gnl, 1)
                dve.wait_ge(s_wtp, 1 + i + 1)
                v.tensor_copy(gwt_l[:, :, bass.ds(i * P, P)], bank16(5).rearrange("p (k c) -> p k c", k=KD)).then_inc(s_wtl, 1)

            pairs(dve, w1_part, KD)

            for i in range(NT):
                for k in range(2):
                    n = 2 * i + k
                    dve.wait_ge(s_back[n % 4], 16 * (n // 4) + 16)
                    v.scalar_tensor_tensor(out=x[:, i, :], in0=back[:, n % 4, :], scalar=gates[:, k, i:i + 1],
                                           in1=x[:, i, :], op0=ALU.mult, op1=ALU.add).then_inc(s_mix, 1)
                    dve.wait_ge(s_mix, n + 1)
                statistics(2 * NT + i, i)
            dve.wait_ge(s_deg, 1)
            v.tensor_scalar(dinv[:, 1, :], ps[:, 6, 0:NT], 1.0, None, ALU.add).then_inc(s_degp, 1)
            dve.wait_ge(s_dinv, 1)
            v.tensor_scalar(dinv[:, 1, :], dinv[:, 0, :], SH, None, ALU.mult).then_inc(s_dinv2, 1)
            v.tensor_scalar(dinv[:, 2, :], dinv[:, 0, :], 1.0 / SH, None, ALU.mult).then_inc(s_dinv2, 1)
            dve.wait_ge(s_dinv2, 2)
            dve.wait_ge(s_bias, 32)

            def lin1(i, u):
                dve.wait_ge(s_hsl, i + 1)
                dve.wait_ge(s_mm, 1 + R_LIN1 + i + 1)
                v.scalar_tensor_tensor(out=h32[:, :], in0=pair_banks(u), scalar=1.0 / (SX * SW), in1=bias_b[:, :],
                                       op0=ALU.mult, op1=ALU.add).then_inc(s_mmread, 1)
                dve.wait_ge(s_hsh, i + 1)
                v.scalar_tensor_tensor(out=hs_l[:, i, :], in0=h32[:, :], scalar=dinv[:, 1, bass.ds(i, 1)],
                                       in1=hs_h[:, i, :], op0=ALU.mult, op1=ALU.subtract).then_inc(s_hsl, 1)

            normalised(R_LIN1, lin1)

            def agg(i, u):
                dve.wait_ge(s_agg, i + 1)
                v.scalar_tensor_tensor(out=x[:, i, :], in0=pair_banks(u), scalar=dinv[:, 2, bass.ds(i, 1)], in1=x[:, i, :],
                                       op0=ALU.mult, op1=ALU.add).then_inc(s_aggread, 1)
                dve.wait_ge(s_aggread, 2 + i + 1)
                statistics(3 * NT + i, i)

            pairs(dve, agg)

            dve.wait_ge(s_abs, 2 + 32)
            v.tensor_reduce(sw[:, 0:2], abs_acc[:, :].rearrange("p (m n) -> p m n", m=2), AX.X, ALU.add).then_inc(s_swp, 1)
            dve.wait_ge(s_swm, 1)
            do(v.tensor_scalar(sw[:, 2:4], ps[:, 6, 0:2], 1.0 / (D * FH), Q_EPS, ALU.mult, ALU.max))
            do(v.reciprocal(sw[:, 4:6], sw[:, 2:4]))
            v.tensor_copy(fwinv[:, 0:8], sw[:, 4:5].to_broadcast([P, 8])).then_inc(s_sw, 1)
            v.tensor_copy(fwinv[:, 8:16], sw[:, 5:6].to_broadcast([P, 8])).then_inc(s_sw, 1)

            def clip_high(n):
                dve.wait_ge(s_fy, 4 + n + 1)
                v.tensor_scalar(fq[:, n % 2, :], fy[:, n % 2, :], -MAGIC, 1.0, ALU.add, ALU.min).then_inc(s_fq, 1)

            def clip_low(n):
                dve.wait_ge(s_ft, n + 1)
                if n < 32:
                    dst = w1q[:, :, n * P:(n + 1) * P]
                else:
                    b, o = (n - 32) // 8, (n - 32) % 8
                    dst = w2q[:, 8 * b:8 * b + 8, o * P:(o + 1) * P]
                v.tensor_scalar(dst, bank16(4 + n % 2).rearrange("p (k c) -> p k c", k=KD), -1.0, None,
                                ALU.max, saturate=False).then_inc(s_fc, 1)

            clip_high(0)
            for n in range(64):
                if n < 63:
                    clip_high(n + 1)
                clip_low(n)

            qsteps = Steps(dve, s_dq)

            def dq(ins):
                qsteps.inc(ins)
                qsteps.wait()

            def quantise(i, u):
                qsteps.at(0 if isinstance(i, int) and i == 0 else 10 * i - 5)
                dve.wait_ge(s_rstd, 3 * NT + i + 1)
                one = bass.ds(i, 1)
                dq(v.tensor_scalar(xn_f[:, u, :], x[:, i, :], mv[:, i, 0:1], rstd[:, one], ALU.subtract, ALU.mult))
                dq(v.tensor_reduce(fs[:, u, 0:1], xn_f[:, u, :], AX.X, ALU.max, apply_absolute_value=True))
                dq(v.tensor_scalar(fs[:, u, 1:2], fs[:, u, 0:1], Q_EPS, 1.0 / 127.0, ALU.max, ALU.mult))
                v.tensor_tensor(fs[:, u, 3:4], fs[:, u, 1:2], sw[:, 2:3], ALU.mult)
                dq(v.reciprocal(fs[:, u, 2:3], fs[:, u, 1:2]))
                dq(v.tensor_scalar(xn_f[:, u, :], xn_f[:, u, :], fs[:, u, 2:3], MAGIC, ALU.mult, ALU.add))
                v.tensor_scalar(xq[:, u, :], xn_f[:, u, :], -MAGIC, 127.0, ALU.add, ALU.min).then_inc(s_xq, 1)

            def quantise_hidden(i, u):
                qsteps.at(10 * i + 5 if last_of(i, NT) else 10 * i + 10)
                for n in range(8):
                    dve.wait_ge(s_ge, 4 + 8 * i + n + 1)
                    last = v.tensor_reduce(hm[:, u, n:n + 1], hf[:, u, n * 512:(n + 1) * 512], AX.X, ALU.max,
                                           apply_absolute_value=True)
                dq(last)
                dq(v.tensor_reduce(fs[:, u, 8:9], hm[:, u, :], AX.X, ALU.max))
                dq(v.tensor_scalar(fs[:, u, 9:10], fs[:, u, 8:9], Q_EPS, 1.0 / 127.0, ALU.max, ALU.mult))
                v.tensor_tensor(fs[:, u, 11:12], fs[:, u, 9:10], sw[:, 3:4], ALU.mult)
                dq(v.reciprocal(fs[:, u, 10:11], fs[:, u, 9:10]))
                dq(v.tensor_scalar(hf[:, u, :], hf[:, u, :], fs[:, u, 10:11], MAGIC, ALU.mult, ALU.add))
                v.tensor_scalar(hq[:, :], hf[:, u, :], -MAGIC, 127.0, ALU.add, ALU.min).then_inc(s_hq, 1)

            def result(i, u):
                dve.wait_ge(s_f2, i + 1)
                dve.wait_ge(s_out[u], 8 * i - 8 * u + 16)
                v.scalar_tensor_tensor(out=out_t[:, u, :], in0=ps[:, 4:6, :].rearrange("p b c -> p (b c)"),
                                       scalar=fs[:, u, 11:12], in1=x[:, i, :], op0=ALU.mult, op1=ALU.add).then_inc(s_f2r, 1)

            def ffn(i, u):
                quantise_hidden(i, u)
                if not last_of(i, NT, 2):
                    quantise(i + 2, u)
                result(i, u)

            quantise(0, 0)
            quantise(1, 1)
            pairs(dve, ffn)


_INS = ["x", "src", "dst", "edge_weight", "L0_gnn_bias", "L0_ffn_wg", "L0_ffn_w1", "L0_ffn_b1", "L0_ffn_w2", "L0_ffn_b2",
        "L1_gnn_W", "L1_gnn_b", "L1_ffn_w1", "L1_ffn_w2"]


def kernel(**inputs):
    import numpy as np
    import concourse.bacc as bacc
    from concourse.bass_utils import run_bass_kernel_spmd

    nc = bacc.Bacc("TRN2", target_bir_lowering=False, num_devices=1)
    arrays, args = {}, []
    for name in _INS:
        a = np.ascontiguousarray(inputs[name])
        arrays[f"in_{name}"] = a
        args.append(nc.dram_tensor(f"in_{name}", a.shape, mybir.dt.from_np(a.dtype), kind="ExternalInput").ap())
    out = nc.dram_tensor("out_x", (N, D), F32, kind="ExternalOutput").ap()
    build_kernel(nc, *args, out)
    r = run_bass_kernel_spmd(nc, [arrays], core_ids=[0])
    return r.results[0]["out_x"]
```

```python
from contextlib import ExitStack

import concourse.bass as bass
from concourse import mybir

F32 = mybir.dt.float32
F16 = mybir.dt.float16
F8 = mybir.dt.float8e4
I32 = mybir.dt.int32
I16 = mybir.dt.int16
U32 = mybir.dt.uint32
ALU = mybir.AluOpType
ACT = mybir.ActivationFunctionType
AX = mybir.AxisListType

P = 128
N = 1250
D = 1024
NT = (N + P - 1) // P
LAST = N - (NT - 1) * P
NP = NT * P
KD = D // P
E_EDGES = 41250
CH = (E_EDGES + P - 1) // P
CHP = 3 * P
WIN = 32
NW = NP // WIN
G = 10
RING = 5
NG_MAX = (CH + G - 1) // G
NE = 8
HID = 512
CAP = 2 * ((N + NE - 1) // NE)
SM = [P, P, CAP - 2 * P]
KH = HID // P
FH = 4096
KF = FH // P

SX = 1024.0
SW = 256.0
SH = 64.0
MAGIC = 12582912.0
LN_EPS = 1e-5
Q_EPS = 1e-5


class Steps:

    def __init__(self, eng, sem, base=0):
        self.eng, self.sem, self.base, self.n = eng, sem, base, 0

    def at(self, base):
        self.base, self.n = base, 0

    def inc(self, ins):
        ins.then_inc(self.sem, 1)
        self.n += 1

    def wait(self):
        self.eng.wait_ge(self.sem, self.base + self.n)


def build_kernel(nc, x_in, src_in, dst_in, ew_in, bias0_in, wg_in, w1_in, b1_in, w2_in, b2_in,
                 gw_in, gb_in, f1_in, f2_in, out):
    ctx = ExitStack()
    with ctx:
        OFF_X = (nc.sbuf_base + 31) // 32 * 32
        OFF_MISC = OFF_X + NT * D * 4
        OFF_AT = OFF_MISC + 14336
        OFF_LN = OFF_AT + NT * NP * 3
        OFF_BIG = OFF_LN + 26624
        END = nc.sbuf_usable_end // 32 * 32
        OFF_HS = END - 2 * NT * D * 2

        cur = {"x": OFF_X, "misc": OFF_MISC, "ln": OFF_LN, "at": OFF_AT, "big": OFF_BIG}
        lim = {"x": OFF_MISC, "misc": OFF_AT, "at": OFF_LN, "ln": OFF_BIG, "big": END, "wide": OFF_HS, "late": OFF_LN}

        def sb(area, name, shape, dt):
            n = 1
            for d in shape[1:]:
                n *= d
            size = (n * (2 if dt == F16 else 1 if dt == F8 else 4) + 31) // 32 * 32
            off = cur[area]
            cur[area] = off + size
            assert cur[area] <= lim[area], (area, name, cur[area] - lim[area])
            return nc.alloc_sbuf_tensor_at(name, shape, dt, offset=off)

        def restart(area, off):
            cur[area] = off

        def sem(name):
            return ctx.enter_context(nc.semaphore(name))

        x = sb("x", "x", [P, NT, D], F32)
        id16 = sb("misc", "id16", [P, P], F16)
        id32 = sb("misc", "id32", [P, P], F32)
        tri = sb("misc", "tri", [P, P], F16)
        ones16 = sb("misc", "ones16", [P, P], F16)
        zero16 = sb("misc", "zero16", [P, 96], F16)
        ones32 = sb("misc", "ones32", [P, P], F32)
        bias_b = sb("misc", "bias_b", [P, D], F32)
        stats = sb("misc", "stats", [P, 2, 6], F32)
        mv_one = sb("misc", "mv_one", [P, 2], F32)
        mv = sb("misc", "mv", [P, NT, 2], F32)
        rstd = sb("misc", "rstd", [P, NT], F32)
        rtmp = sb("misc", "rtmp", [P, 2], F32)
        consts = sb("misc", "consts", [P, 4], F32)
        rows_i = sb("misc", "rows_i", [1, 2, 48], I32)
        abs_acc = sb("misc", "abs_acc", [P, 32], F32)
        sw = sb("misc", "sw", [P, 8], F32)
        gates = sb("misc", "gates", [P, 2, NT], F32)
        slot_i = sb("misc", "slot_i", [P, 2 * NT], I32)
        tok_i = sb("misc", "tok_i", [P, 3 * NE], I32)
        b1c = sb("misc", "b1c", [P, NE, KH], F32)
        dinv = sb("misc", "dinv", [P, 3, NT], F32)
        fs = sb("misc", "fs", [P, 2, 16], F32)
        hm = sb("misc", "hm", [P, 2, 8], F32)

        wg32 = sb("misc", "wg32", [P, KD, NE], F32)
        wgs = sb("misc", "wgs", [P, KD, 2 * NE], F16)

        misc_mark = cur["misc"]
        iota_r = sb("misc", "iota_r", [P, NP], F16)

        xn = sb("ln", "xn", [P, 2, D], F32)
        xh = sb("ln", "xh", [P, 2, D], F16)
        xl = sb("ln", "xl", [P, 2, D], F16)
        xth = sb("ln", "xth", [P, 2, KD, P], F16)
        xtl = sb("ln", "xtl", [P, 2, KD, P], F16)
        restart("ln", OFF_LN)
        st_a = sb("ln", "st_a", [P, 2, NP], F32)
        st_wh = sb("ln", "st_wh", [P, 2, D], F32)
        st_wl = sb("ln", "st_wl", [P, 2, D], F32)
        restart("ln", OFF_LN)
        gx = sb("ln", "gx", [P, 2, 2 * D], F16)
        eo = sb("ln", "eo", [P, 2, D], F32)
        b2b = sb("ln", "b2b", [P, D], F32)
        ht32 = sb("ln", "ht32", [P, 2, CAP], F32)
        htl = sb("ln", "htl", [P, KH, CAP], F16)

        at_h = sb("at", "at_h", [P, NT, NP], F16)
        at_l = sb("at", "at_l", [P, NT, NP], F8)

        wt_h = sb("big", "wt_h", [P, NT, D], F16)
        wt_l = sb("big", "wt_l", [P, NT, D], F16)
        src_t = sb("big", "src_t", [P, CHP], F32)
        dst_t = sb("big", "dst_t", [P, CHP], F32)
        ewh_t = sb("big", "ewh_t", [P, CHP], F16)
        ewl_t = sb("big", "ewl_t", [P, CHP], F16)
        src_g = sb("big", "src_g", [P, 2, RING], F32)
        st_e = sb("big", "st_e", [P, 2, RING, 96], F16)
        big_mark = cur["big"]
        oh = sb("big", "oh", [P, RING, NP], F16)
        at_lo16 = sb("big", "at_lo16", [P, NP], F16)
        at_lo = sb("big", "at_lo", [P, NP], F8)
        abs_in = sb("big", "abs_in", [P, 2, 2048], F32)
        restart("big", big_mark)
        nat_i = sb("big", "nat_i", [P, 2, 3, P], I32)
        nat_f = sb("big", "nat_f", [P, 2, 3, P], F32)
        nat_w = sb("big", "nat_w", [P, 3, P], F32)
        ew32_t = sb("big", "ew32_t", [P, CHP], F32)
        cm = sb("big", "cm", [P, 2, 3], F32)
        cmb = sb("big", "cmb", [P, 6, 48], F16)
        q_iota = sb("big", "q_iota", [48, CHP], F32)
        w_lo = sb("big", "w_lo", [48, 2], F32)
        ov = sb("big", "ov", [48, 2, CHP], F32)
        j_iota = sb("big", "j_iota", [48, 40], F32)
        kk = sb("big", "kk", [48, 8], F32)
        kk16 = sb("big", "kk16", [48, 2], F16)
        restart("big", OFF_BIG)
        wstage = sb("big", "wstage", [P, 4, 2048], F32)
        w1h = sb("big", "w1h", [P, KD, HID], F16)
        w1l = sb("big", "w1l", [P, KD, HID], F16)
        w2h = sb("big", "w2h", [P, KH, D], F16)
        w2l = sb("big", "w2l", [P, KH, D], F16)
        xdh = sb("big", "xdh", [P, KD, CAP], F16)
        xdl = sb("big", "xdl", [P, KD, CAP], F16)
        hth = sb("big", "hth", [P, KH, CAP], F16)
        restart("big", OFF_BIG + 32768)
        logits = sb("big", "logits", [P, NT, NE], F32)
        lmax = sb("big", "lmax", [P, NT, 8], F32)
        lidx = sb("big", "lidx", [P, NT, 8], U32)
        lidf = sb("big", "lidf", [P, NT, 8], F32)
        mask = sb("big", "mask", [P, 2, NT, NE], F16)
        tot_e = sb("big", "tot_e", [P, NE, 2 * NT], F32)
        scan_m = sb("big", "scan_m", [P, NE, 2 * NT], F32)
        scan_o = sb("big", "scan_o", [P, NE, 2 * NT], F32)
        loc3 = sb("big", "loc3", [P, 2 * NT, NE], F32)
        loc3b = sb("big", "loc3b", [P, 2 * NT, NE], F32)
        rt = sb("big", "rt", [P, 12, 2 * NT], F32)
        iota_lo = sb("big", "iota_lo", [P, P], F32)
        tok_f = sb("big", "tok_f", [P, 2 * NT], F32)
        oh_lo = sb("big", "oh_lo", [P, 2 * NT, P], F16)
        oh_hi = sb("big", "oh_hi", [P, 2 * NT, 3 * NE], F16)
        oh_hi2 = sb("big", "oh_hi2", [P, 2 * NT, 3 * NE], F16)
        valid_m = sb("big", "valid_m", [P, 2, NT, NE], F16)
        restart("big", OFF_BIG)
        gwt_h = sb("big", "gwt_h", [P, KD, D], F16)
        gwt_l = sb("big", "gwt_l", [P, KD, D], F16)
        h32 = sb("big", "h32", [P, D], F32)
        back = sb("big", "back", [P, 3, D], F32)
        restart("big", OFF_HS)
        hs_h = sb("big", "hs_h", [P, NT, D], F16)
        hs_l = sb("big", "hs_l", [P, NT, D], F16)
        restart("big", OFF_HS)
        gnat = sb("big", "gnat", [P, 2, D], F32)
        gnh = sb("big", "gnh", [P, 2, D], F16)
        gnl = sb("big", "gnl", [P, 2, D], F16)
        cur["wide"] = OFF_LN
        w1q = sb("wide", "w1q", [P, KD, FH], F8)
        w2q = sb("wide", "w2q", [P, KF, D], F8)
        stage_mark = cur["wide"]
        fnat_a = sb("wide", "fnat_a", [P, 3, D], F32)
        fnat = [fnat_a[:, 0, :], fnat_a[:, 1, :], fnat_a[:, 2, :], bias_b[:, :]]
        restart("misc", misc_mark)
        fq = sb("misc", "fq", [P, 2, D], F16)
        fneg = sb("misc", "fneg", [P, 2, D], F8)
        restart("wide", stage_mark)
        xn_f = sb("wide", "xn_f", [P, 2, D], F32)
        xq = sb("wide", "xq", [P, 2, D], F16)
        cur["late"] = OFF_AT
        hf = sb("late", "hf", [P, 2, FH], F32)
        restart("big", OFF_HS)
        hq = sb("big", "hq", [P, FH], F16)
        hqt = sb("big", "hqt", [P, KF, P], F16)
        out_t = sb("big", "out_t", [P, 2, D], F32)
        xqt = sb("big", "xqt", [P, 2, KD, P], F16)

        ps = ctx.enter_context(nc.psum_tensor("ps", [P, 8, 512], F32))

        def bank16(b):
            return ps[:, b, :].bitcast(F16)

        xs_d = nc.dram_tensor("xs_d", [NP, 2 * D], F16).ap()
        eo_d = nc.dram_tensor("eo_d", [NE * CAP, D], F32).ap()

        s_pad = sem("s_pad")
        s_edges = sem("s_edges")
        s_x = sem("s_x")
        s_bias = sem("s_bias")
        s_b1 = sem("s_b1")
        s_wg = sem("s_wg")
        s_absin = [sem(f"s_absin{u}") for u in range(2)]
        s_const = sem("s_const")
        s_dv = sem("s_dv")
        s_natf = sem("s_natf")
        s_cmb = sem("s_cmb")
        s_et = sem("s_et")
        s_cmw = sem("s_cmw")
        s_kk = sem("s_kk")
        s_kr = sem("s_kr")
        s_rows = sem("s_rows")
        s_small = sem("s_small")
        s_srcg = sem("s_srcg")
        s_onehot = sem("s_onehot")
        s_st = sem("s_st")
        s_oh = sem("s_oh")
        s_chunk = sem("s_chunk")
        s_win = sem("s_win")
        s_winread = sem("s_winread")
        s_stage = sem("s_stage")
        s_wsum = sem("s_wsum")
        s_blk = sem("s_blk")
        s_built = sem("s_built")
        s_abs = sem("s_abs")
        s_bn = sem("s_bn")
        s_stat = sem("s_stat")
        s_pl = sem("s_pl")
        s_rstd = sem("s_rstd")
        s_biased = sem("s_biased")
        s_xn = sem("s_xn")
        s_xh = sem("s_xh")
        s_xl = sem("s_xl")
        s_th, s_tl = sem("s_th"), sem("s_tl")
        s_xth, s_xtl = sem("s_xth"), sem("s_xtl")
        s_mm = sem("s_mm")
        s_mmread = sem("s_mmread")
        s_xstore = [sem(f"s_xstore{u}") for u in range(2)]
        s_mask = sem("s_mask")
        s_cum = sem("s_cum")
        s_gd = sem("s_gd")
        s_ex = sem("s_ex")
        s_ohr = sem("s_ohr")
        s_tok = sem("s_tok")
        s_toki = sem("s_toki")
        s_wst = [sem(f"s_wst{i}") for i in range(4)]
        s_wh = sem("s_wh")
        s_wl = sem("s_wl")
        s_g = [sem("s_gx0"), sem("s_gx1")]
        s_gth, s_gtl = sem("s_gth"), sem("s_gtl")
        s_gch, s_gcl = sem("s_gch"), sem("s_gcl")
        s_g1 = sem("s_g1")
        s_g1r = sem("s_g1r")
        s_hh = sem("s_hh")
        s_hl = sem("s_hl")
        s_g2 = sem("s_g2")
        s_g2r = sem("s_g2r")
        s_b2 = sem("s_b2")
        s_eout = [sem("s_eout0"), sem("s_eout1")]
        s_back = [sem(f"s_back{i}") for i in range(3)]
        s_mix = sem("s_mix")
        s_gn = [sem("s_gn0"), sem("s_gn1")]
        s_gnh, s_gnl = sem("s_gnh"), sem("s_gnl")
        s_wtp = sem("s_wtp")
        s_wth, s_wtl = sem("s_wth"), sem("s_wtl")
        s_deg = sem("s_deg")
        s_degp = sem("s_degp")
        s_dinv = sem("s_dinv")
        s_dinv2 = sem("s_dinv2")
        s_hsh, s_hsl = sem("s_hsh"), sem("s_hsl")
        s_agg = sem("s_agg")
        s_aggread = sem("s_aggread")
        s_swp = sem("s_swp")
        s_swm = sem("s_swm")
        s_fn = [sem(f"s_fn{i}") for i in range(4)]
        s_fneg = sem("s_fneg")
        s_fq = sem("s_fq")
        s_ft = sem("s_ft")
        s_fc = sem("s_fc")
        s_dq = sem("s_dq")
        s_xq = sem("s_xq")
        s_xqt = sem("s_xqt")
        s_xqc = sem("s_xqc")
        s_f1 = sem("s_f1")
        s_ge = sem("s_ge")
        s_hq = sem("s_hq")
        s_hqt = sem("s_hqt")
        s_hqc = sem("s_hqc")
        s_f2 = sem("s_f2")
        s_f2r = sem("s_f2r")
        s_out = [sem("s_out0"), sem("s_out1")]

        s_held = sem("s_held")

        block = ctx.enter_context(nc.Block())

        R_GNN0, R_MOE, R_LIN1 = 0, NT, 2 * NT

        def last_of(i, n, k=1):
            return isinstance(i, int) and i >= n - k

        def hold(eng):
            eng.sem_inc(s_held, 1)

        def pairs(eng, body, n=NT):
            with eng.Fori(0, n // 2 - 1) as j:
                for u in range(2):
                    body(2 * j + u, u)
            for i in (n - 2, n - 1):
                body(i, i % 2)

        @block.sync
        def _(sp):
            for u in range(2):
                sp.sem_inc(s_eout[u], 16)
                sp.sem_inc(s_out[u], 16)
            sp.wait_ge(s_pad, 3)
            full, rest = CH - 1 - 2 * P, E_EDGES - (CH - 1) * P
            for v, edge in enumerate((src_in, dst_in, ew_in)):
                nat = nat_w[:, :, :] if v == 2 else nat_i[:, v, :, :]
                sp.dma_start(nat[:, 0:2, :], edge[0:2 * P * P].rearrange("(a q p) -> q a p", a=2, p=P)).then_inc(s_edges, 16)
                sp.dma_start(nat[0:full, 2, :], edge[2 * P * P:(CH - 1) * P].rearrange("(q p) -> q p", p=P)).then_inc(s_edges, 16)
                sp.dma_start(nat[full:full + 1, 2, 0:rest],
                             edge[(CH - 1) * P:E_EDGES].rearrange("(q p) -> q p", q=1)).then_inc(s_edges, 16)
            sp.wait_ge(s_const, 1)
            sp.dma_start(x[:, 0:NT - 1, :], x_in[0:(NT - 1) * P, :].rearrange("(t p) d -> p t d", p=P)).then_inc(s_x, 16)
            sp.dma_start(x[0:LAST, NT - 1, :], x_in[(NT - 1) * P:N, :]).then_inc(s_x, 16)
            sp.dma_start(bias_b[:, :], bias0_in.partition_broadcast(P)).then_inc(s_bias, 16)
            with nc.allow_non_contiguous_dma(reason="4096 words, once"):
                sp.dma_start(b1c[:, :, :], b1_in.rearrange("e (h p) -> p e h", p=P)).then_inc(s_b1, 16)
            sp.dma_start(wg32[:, :, :], wg_in.rearrange("(k p) e -> p k e", p=P)).then_inc(s_wg, 16)

            sp.wait_ge(s_rows, 1)
            for m, w in enumerate((f1_in, f2_in)):
                pieces = w.rearrange("a b -> (a b)").rearrange("(n p c) -> n p c", p=P, c=2048)
                with sp.Fori(0, 8) as j:
                    for u in range(2):
                        sp.wait_ge(s_abs, 16 * m + 2 * j + u + 1)
                        sp.dma_start(abs_in[:, u, :], pieces[2 * j + u]).then_inc(s_absin[u], 16)

            w1v = w1_in.rearrange("e (g k p) h -> e g p k h", g=2, p=P)
            w2v = w2_in.rearrange("e (g k p) d -> e g p k d", g=2, p=P)

            def expert_piece(e, q):
                piece = w1v[e, q] if q < 2 else w2v[e, q - 2]
                sp.dma_start(wstage[:, q, :].rearrange("p (k h) -> p k h", k=4 if q < 2 else 2), piece).then_inc(s_wst[q], 16)

            sp.wait_ge(s_mm, 1 + NT)
            for q in range(4):
                expert_piece(0, q)

            rows_d = xs_d.rearrange("(t p) c -> t p c", p=P)

            def store(i, u):
                sp.wait_ge(s_xh, R_MOE + i + 1)
                sp.dma_start(rows_d[i][:, 0:D], xh[:, u, :]).then_inc(s_xstore[u], 16)
                sp.wait_ge(s_xl, R_MOE + i + 1)
                sp.dma_start(rows_d[i][:, D:2 * D], xl[:, u, :]).then_inc(s_xstore[u], 16)

            pairs(sp, store)

            sp.wait_ge(s_toki, 1)
            for u in range(2):
                sp.wait_ge(s_xstore[u], 16 * NT)
            sp.dma_start(b2b[:, :], b2_in[0].partition_broadcast(P)).then_inc(s_b2, 16)
            expert_rows = eo_d.rearrange("(e s) d -> e s d", e=NE)

            def expert(e, ep):
                if not last_of(e, NE):
                    for q in range(4):
                        sp.wait_ge(s_wl, 4 * e + q + 1)
                        expert_piece(e + 1, q)
                for s in range(3):
                    u = (ep + s) % 2
                    sp.wait_ge(s_g2r, 3 + 6 * e + 2 * s + 2)
                    sp.dma_start(expert_rows[e][s * P:s * P + SM[s], :], eo[0:SM[s], u, :]).then_inc(s_eout[u], 16)
                if not last_of(e, NE):
                    sp.dma_start(b2b[:, :], b2_in[e + 1].partition_broadcast(P)).then_inc(s_b2, 16)

            pairs(sp, expert, NE)

            sp.dma_start(bias_b[:, :], gb_in.partition_broadcast(P)).then_inc(s_bias, 16)
            w1rows = gw_in.rearrange("(t p) d -> t p d", p=P)

            def w1_rows(i, u):
                sp.wait_ge(s_gnl, i + 1)
                sp.dma_start(gnat[:, u, :], w1rows[i]).then_inc(s_gn[u], 16)

            pairs(sp, w1_rows, KD)

            sp.wait_ge(s_mix, 2 * NT)
            sp.wait_ge(s_mmread, 2 + R_LIN1 + NT)
            f1v = f1_in.rearrange("(j u p) d -> j u p d", p=P, u=4)
            f2v = f2_in.rearrange("(j u p) (b d) -> b j u p d", p=P, u=4, b=4)
            with sp.Fori(0, KD) as j:
                for u in range(4):
                    sp.wait_ge(s_fq, 4 * j + u + 1)
                    sp.dma_start(fnat[u], f1v[j, u]).then_inc(s_fn[u], 16)
            for b in range(4):
                with sp.Fori(0, 2) as j:
                    for u in range(4):
                        sp.wait_ge(s_fq, 32 + 8 * b + 4 * j + u + 1)
                        sp.dma_start(fnat[u], f2v[b, j, u]).then_inc(s_fn[u], 16)

            res = out[0:(NT - 1) * P, :].rearrange("(t p) d -> t p d", p=P)

            def result(i, u):
                sp.wait_ge(s_f2r, i + 1)
                if last_of(i, NT):
                    sp.dma_start(out[(NT - 1) * P:N, :], out_t[0:LAST, u, :]).then_inc(s_out[u], 16)
                else:
                    sp.dma_start(res[i], out_t[:, u, :]).then_inc(s_out[u], 16)

            pairs(sp, result)
            for u in range(2):
                sp.wait_ge(s_eout[u], 16 + 16 * 3 * NE // 2)
                sp.wait_ge(s_out[u], 16 + 16 * NT // 2)

        @block.gpsimd
        def _(pool):
            g = nc.gpsimd
            ok = dict(allow_small_or_imprecise_dtypes=True)
            g.memset(x[:, NT - 1, :], 0.0).then_inc(s_const, 1)
            for k, v in enumerate((LN_EPS, -0.5, SX, 1.0)):
                g.memset(consts[:, k:k + 1], v).then_inc(s_const, 1)
            g.memset(zero16[:, :], 0.0).then_inc(s_const, 1)
            g.memset(ones16[:, :], 1.0).then_inc(s_const, 1)
            g.memset(ones32[:, :], 1.0).then_inc(s_const, 1)
            g.iota(iota_r[:, :], [[1, NP]], base=0, channel_multiplier=0, **ok).then_inc(s_const, 1)
            g.iota(q_iota[:, :], [[1, CHP]], base=0, channel_multiplier=0, **ok).then_inc(s_const, 1)
            g.iota(j_iota[:, 0:NG_MAX], [[G, NG_MAX]], base=G, channel_multiplier=0, **ok).then_inc(s_const, 1)
            for k in range(2):
                g.iota(w_lo[:, k:k + 1], [[1, 1]], base=(WIN - 1) * k, channel_multiplier=WIN, **ok).then_inc(s_const, 1)
            pool.wait_ge(s_const, 13)
            g.affine_select(out=id16[:, :], in_=ones16[:, :], pattern=[[-1, P]], compare_op=ALU.is_equal,
                            fill=0.0, base=0, channel_multiplier=1).then_inc(s_const, 1)
            g.affine_select(out=id32[:, :], in_=ones32[:, :], pattern=[[-1, P]], compare_op=ALU.is_equal,
                            fill=0.0, base=0, channel_multiplier=1).then_inc(s_const, 1)
            g.affine_select(out=tri[:, :], in_=ones16[:, :], pattern=[[1, P]], compare_op=ALU.is_ge,
                            fill=0.0, base=0, channel_multiplier=-1).then_inc(s_const, 1)

            def rstd_tile(r, i, k):
                n = NT * r + i
                one = bass.ds(i, 1)
                pool.wait_ge(s_stat, n + 1)
                g.tensor_tensor(rtmp[:, 0:1], mv[:, one, 1], consts[:, 0:1], ALU.add).then_inc(s_pl, 1)
                pool.wait_ge(s_pl, 2 * n + 1)
                g.tensor_tensor(rtmp[:, 1:2], rtmp[:, 0:1], consts[:, 1:2], ALU.pow).then_inc(s_pl, 1)
                pool.wait_ge(s_pl, 2 * n + 2)
                g.tensor_tensor(rstd[:, one], rtmp[:, 1:2], consts[:, k:k + 1], ALU.mult).then_inc(s_rstd, 1)

            with pool.Fori(0, NT) as i:
                rstd_tile(0, i, 2)

            pool.wait_ge(s_rows, 1)
            with pool.register("pool_chunks") as chunks, pool.register("pool_first") as first:
                pool.reg_mov(chunks, 0)

                def window(w):
                    pool.reg_load(first, rows_i[0:1, 0, bass.ds(w, 1)])
                    groups = pool.value_load(rows_i[0:1, 1, bass.ds(w, 1)], min_val=1, max_val=NG_MAX)
                    with pool.Fori(0, groups):
                        n = pool.snap(chunks, min_val=0, max_val=1 << 20)
                        at = pool.snap(first, min_val=0, max_val=CHP - G)
                        for half in range(2):
                            five = bass.ds(at + 5 * half, RING)
                            st = st_e[:, half, :, :]
                            pool.wait_ge(s_onehot, n + 5 * half + 5)
                            g.tensor_tensor(st[:, :, WIN:2 * WIN], st[:, :, 0:WIN],
                                            ewh_t[:, five].unsqueeze(2).to_broadcast([P, RING, WIN]), ALU.mult)
                            g.tensor_tensor(st[:, :, 2 * WIN:3 * WIN], st[:, :, 0:WIN],
                                            ewl_t[:, five].unsqueeze(2).to_broadcast([P, RING, WIN]),
                                            ALU.mult).then_inc(s_st, 5)
                        pool.reg_add(chunks, chunks, G)
                        pool.reg_add(first, first, G)

                def block_sums(b, ub):
                    pool.wait_ge(s_stage, 12 * b + 12)
                    g.tensor_tensor(st_wh[:, ub, :], st_wh[:, ub, :], st_wl[:, ub, :], ALU.add).then_inc(s_wsum, 1)

                window(0)
                with pool.Fori(0, NW // 8 - 1) as bb:
                    for k in range(1, 9):
                        window(8 * bb + k)
                        if k % 4 == 0:
                            block_sums(2 * bb + k // 4 - 1, k // 4 - 1)
                for w in range(NW - 7, NW):
                    window(w)
                    if w % 4 == 0:
                        block_sums(w // 4 - 1, (w // 4 - 1) % 2)
                block_sums(NT - 1, (NT - 1) % 2)

            pool.wait_ge(s_bias, 16)
            with pool.Fori(0, NT) as i:
                pool.wait_ge(s_xn, R_GNN0 + i + 1)
                g.tensor_tensor(x[:, i, :], x[:, i, :], bias_b[:, :], ALU.add).then_inc(s_biased, 1)
            with pool.Fori(0, NT) as i:
                rstd_tile(1, i, 2)

            pool.wait_ge(s_mm, 1 + NT)
            g.iota(iota_lo[:, :], [[1, P]], base=0, channel_multiplier=0, **ok).then_inc(s_const, 1)
            g.iota(tok_f[:, :], [[0, 2], [P, NT]], base=0, channel_multiplier=1, **ok).then_inc(s_const, 1)
            g.memset(valid_m[:, :, :, :], 1.0).then_inc(s_const, 1)
            g.memset(scan_m[:, :, :], 1.0).then_inc(s_const, 1)
            pool.wait_ge(s_const, 20)
            for k in range(2):
                g.affine_select(out=valid_m[:, k, NT - 1, :], in_=valid_m[:, k, NT - 1, :],
                                pattern=[[0, NE]], compare_op=ALU.is_ge, fill=0.0, base=LAST - 1,
                                channel_multiplier=-1).then_inc(s_const, 1)
            g.memset(scan_m[:, :, 0:1], 0.0).then_inc(s_const, 1)

            pool.wait_ge(s_toki, 1)
            for u in range(2):
                pool.wait_ge(s_xstore[u], 16 * NT)
            for n in range(3 * NE):
                m = SM[n % 3]
                if n >= 2:
                    pool.wait_ge(s_gtl, n - 1)
                pool.indirect_dma_start(out=gx[0:m, n % 2, :], out_offset=None, in_=xs_d[:, :],
                                        in_offset=bass.IndirectOffsetOnAxis(ap=tok_i[0:m, n:n + 1], axis=0)
                                        ).then_inc(s_g[n % 2], 16)
            for u in range(2):
                pool.wait_ge(s_eout[u], 16 + 16 * 3 * NE // 2)
            for n in range(2 * NT):
                col = (n % 2) * NT + n // 2
                if n >= 3:
                    pool.wait_ge(s_mix, n - 2)
                pool.indirect_dma_start(out=back[:, n % 3, :], out_offset=None, in_=eo_d[:, :],
                                        in_offset=bass.IndirectOffsetOnAxis(ap=slot_i[:, col:col + 1], axis=0)
                                        ).then_inc(s_back[n % 3], 16)
            with pool.Fori(0, NT) as i:
                rstd_tile(2, i, 2)
            pool.wait_ge(s_degp, 1)
            g.tensor_tensor(dinv[:, 0, :], dinv[:, 1, :], consts[:, 1:2].to_broadcast([P, NT]), ALU.pow).then_inc(s_dinv, 1)
            with pool.Fori(0, NT) as i:
                rstd_tile(3, i, 3)

        @block.tensor
        def _(pe):
            mm, tr = nc.tensor.matmul, nc.tensor.transpose
            pe.sem_inc(s_chunk, 10)
            pe.sem_inc(s_mm, 1)
            pe.sem_inc(s_g2, 1)
            pe.sem_inc(s_wtp, 1)
            pe.sem_inc(s_ft, 2)

            pe.wait_ge(s_const, 16)
            pe.wait_ge(s_natf, 2)
            pe.wait_ge(s_edges, 16 * 9)
            for v in range(3):
                for a in range(3):
                    last = tr(ps[:, v, a * P:(a + 1) * P], nat_w[:, a, :] if v == 2 else nat_f[:, v, a, :], id32[:, :])
            last.then_inc(s_et, 1)
            pe.wait_ge(s_cmb, 1)
            for v in range(2):
                for a in range(3):
                    last = mm(ps[0:48, 3 + v, a * P:(a + 1) * P], cmb[:, 3 * v + a, :], id16[:, :], start=True, stop=True)
            last.then_inc(s_cmw, 1)
            pe.wait_ge(s_kk, 1)
            for v in range(2):
                last = mm(ps[0:1, 5, 48 * v:48 * v + 48], kk16[:, v:v + 1], id16[0:48, 0:48], start=True, stop=True)
            last.then_inc(s_kr, 1)
            pe.wait_ge(s_rows, 1)

            with pe.register("pe_chunks") as chunks:
                pe.reg_mov(chunks, 0)

                def window(w, u):
                    groups = pe.value_load(rows_i[0:1, 1, bass.ds(w, 1)], min_val=1, max_val=NG_MAX)
                    pe.wait_ge(s_winread, w + 1)
                    for r in range(3):
                        mm(ps[0:96, 3 * u + r, 0:2], zero16[:, :], zero16[:, 0:2], start=True, stop=False,
                           skip_group_check=True)
                    with pe.Fori(0, groups):
                        n = pe.snap(chunks, min_val=0, max_val=1 << 20)
                        for half in range(2):
                            pe.wait_ge(s_st, n + 5 * half + 5)
                            for c in range(RING):
                                pe.wait_ge(s_oh, n + 5 * half + c + 1)
                                for r in range(3):
                                    cols = slice(512 * r, min(512 * r + 512, NP))
                                    last = mm(ps[0:96, 3 * u + r, 0:cols.stop - cols.start], st_e[:, half, c, :],
                                              oh[:, c, cols], start=False, stop=False, skip_group_check=True)
                                last.then_inc(s_chunk, 1)
                        pe.reg_add(chunks, chunks, G)
                    for r in range(3):
                        last = mm(ps[0:96, 3 * u + r, 0:2], zero16[:, :], zero16[:, 0:2], start=False, stop=True,
                                  skip_group_check=True)
                    last.then_inc(s_win, 1)

                window(0, 0)
                with pe.Fori(0, NW // 8 - 1) as bb:
                    for v in range(1, 9):
                        window(8 * bb + v, v % 2)
                for w in range(NW - 7, NW):
                    window(w, w % 2)

            def transposes(n, u):
                pe.wait_ge(s_xh, n + 1)
                if not isinstance(n, int) or n > 0:
                    pe.wait_ge(s_xth, n)
                for k in range(KD):
                    last = tr(bank16(4)[:, k * P:(k + 1) * P], xh[:, u, k * P:(k + 1) * P], id16[:, :])
                last.then_inc(s_th, 1)
                pe.wait_ge(s_xl, n + 1)
                if not isinstance(n, int) or n > 0:
                    pe.wait_ge(s_xtl, n)
                for k in range(KD):
                    last = tr(bank16(5)[:, k * P:(k + 1) * P], xl[:, u, k * P:(k + 1) * P], id16[:, :])
                last.then_inc(s_tl, 1)

            def product(n, u, rh, rl):
                pe.wait_ge(s_xth, n + 1)
                pe.wait_ge(s_xtl, n + 1)
                pe.wait_ge(s_mmread, n + 1)
                for k in range(KD):
                    for a, (lhs, rhs) in enumerate(((xth, rh), (xth, rl), (xtl, rh))):
                        for h in range(2):
                            last = mm(ps[:, 2 * u + h, :], lhs[:, u, k, :], rhs[:, k, h * 512:(h + 1) * 512],
                                      start=(k == 0 and a == 0), stop=(k == KD - 1 and a == 2))
                last.then_inc(s_mm, 1)

            def normalised(r, body):
                transposes(r, 0)

                def step(i, u):
                    if not last_of(i, NT):
                        transposes(r + i + 1, 1 - u)
                    body(i, u)

                pairs(pe, step)

            pe.wait_ge(s_winread, 2 + NW)
            pe.wait_ge(s_built, 2 + NT)
            normalised(R_GNN0, lambda i, u: product(R_GNN0 + i, u, wt_h, wt_l))

            pe.wait_ge(s_small, 2)

            def logits_of(i, u):
                n = R_MOE + i
                pe.wait_ge(s_xth, n + 1)
                pe.wait_ge(s_xtl, n + 1)
                pe.wait_ge(s_mmread, n + 1)
                for k in range(KD):
                    for a, lhs in enumerate((xth, xtl)):
                        last = mm(ps[:, 6 + u, 0:2 * NE], lhs[:, u, k, :], wgs[:, k, :],
                                  start=(k == 0 and a == 0), stop=(k == KD - 1 and a == 1))
                last.then_inc(s_mm, 1)

            normalised(R_MOE, logits_of)
            pe.wait_ge(s_mask, 1)
            masks = mask[:, :, :, :].rearrange("p k t e -> p (k t e)")
            mm(ps[:, 0, 0:2 * NT * NE], tri[:, :], masks, start=True, stop=True)
            mm(ps[:, 1, 0:2 * NT * NE], ones16[:, :], masks, start=True, stop=True).then_inc(s_cum, 1)
            pe.wait_ge(s_ohr, 1)
            for n in range(2 * NT):
                last = mm(ps[:, 2, 0:3 * NE], oh_lo[:, n, :], oh_hi2[:, n, :], start=(n == 0), stop=(n == 2 * NT - 1))
            last.then_inc(s_tok, 1)
            pe.wait_ge(s_toki, 1)

            def gathered(e, ep):
                for s in range(3):
                    m, n, u = SM[s], 3 * e + s, (ep + s) % 2
                    pe.wait_ge(s_g[u], 8 * n - 8 * u + 16)
                    for part, (b, read, done) in enumerate(((4, s_gch, s_gth), (5, s_gcl, s_gtl))):
                        pe.wait_ge(read, n + 1)
                        hold(pe)
                        for k in range(KD):
                            c = part * D + k * P
                            last = tr(bank16(b)[:, k * P:k * P + m], gx[0:m, u, c:c + P], id16[0:m, 0:m])
                        last.then_inc(done, 1)

            def expert(e, ep):
                pe.wait_ge(s_gch, 1 + 3 * e + 3)
                pe.wait_ge(s_gcl, 1 + 3 * e + 3)
                pe.wait_ge(s_wl, 4 * e + 2)
                for hb in range(KH):
                    pe.wait_ge(s_g1r, 4 * e + hb + 1)
                    for k in range(KD):
                        for a, (lhs, rhs) in enumerate(((w1h, xdh), (w1h, xdl), (w1l, xdh))):
                            last = mm(ps[:, 6 + hb % 2, 0:CAP], lhs[:, k, hb * P:(hb + 1) * P], rhs[:, k, :],
                                      start=(k == 0 and a == 0), stop=(k == KD - 1 and a == 2))
                    last.then_inc(s_g1, 1)
                if not last_of(e, NE):
                    gathered(e + 1, 1 - ep)
                pe.wait_ge(s_hl, 2 + 4 * e + 4)
                pe.wait_ge(s_wl, 4 * e + 4)
                for s in range(3):
                    m = SM[s]
                    for h in range(2):
                        pe.wait_ge(s_g2r, 6 * e + 2 * s + h + 1)
                        for k in range(KH):
                            for a, (lhs, rhs) in enumerate(((hth, w2h), (hth, w2l), (htl, w2h))):
                                last = mm(ps[0:m, (2 * s + h) % 3, :], lhs[:, k, s * P:s * P + m],
                                          rhs[:, k, h * 512:(h + 1) * 512],
                                          start=(k == 0 and a == 0), stop=(k == KH - 1 and a == 2))
                        last.then_inc(s_g2, 1)

            gathered(0, 0)
            pairs(pe, expert, NE)

            def w1_t(i, u):
                pe.wait_ge(s_gnh, i + 1)
                pe.wait_ge(s_wth, i + 1)
                for k in range(KD):
                    tr(bank16(4)[:, k * P:(k + 1) * P], gnh[:, u, k * P:(k + 1) * P], id16[:, :])
                pe.wait_ge(s_gnl, 2 + i + 1)
                pe.wait_ge(s_wtl, i + 1)
                for k in range(KD):
                    last = tr(bank16(5)[:, k * P:(k + 1) * P], gnl[:, u, k * P:(k + 1) * P], id16[:, :])
                last.then_inc(s_wtp, 1)

            pairs(pe, w1_t, KD)
            for i in range(NT):
                for b in range(NT):
                    for a, t in enumerate((at_h, at_l)):
                        last = mm(ps[:, 6, i:i + 1], t[:, b, i * P:(i + 1) * P], ones16[:, 0:1],
                                  start=(b == 0 and a == 0), stop=(b == NT - 1 and a == 1))
            last.then_inc(s_deg, 1)
            pe.wait_ge(s_swp, 1)
            mm(ps[:, 7, 0:2], ones32[:, :], sw[:, 0:2], start=True, stop=True).then_inc(s_swm, 1)
            pe.wait_ge(s_wth, 1 + KD)
            pe.wait_ge(s_wtl, 1 + KD)
            normalised(R_LIN1, lambda i, u: product(R_LIN1 + i, u, gwt_h, gwt_l))

            pe.wait_ge(s_hsh, NT)
            pe.wait_ge(s_hsl, 1 + NT)

            def weight_piece(n):
                pe.wait_ge(s_fq, 4 + n + 1)
                pe.wait_ge(s_fc, n + 1)
                for k in range(KD):
                    last = tr(bank16(4 + n % 4)[:, k * P:(k + 1) * P], fq[:, n % 2, k * P:(k + 1) * P], id16[:, :])
                last.then_inc(s_ft, 1)

            for i in range(NT):
                u = i % 2
                pe.wait_ge(s_aggread, i + 1)
                for a, rhs in enumerate((hs_h, hs_l)):
                    for h in range(2):
                        mm(ps[:, 2 * u + h, :], id16[:, :], rhs[:, i, h * 512:(h + 1) * 512], start=(a == 0), stop=False)
                for b in range(NT):
                    for a, (lhs, rhs) in enumerate(((at_h, hs_h), (at_h, hs_l), (at_l, hs_h))):
                        for h in range(2):
                            last = mm(ps[:, 2 * u + h, :], lhs[:, b, i * P:(i + 1) * P], rhs[:, b, h * 512:(h + 1) * 512],
                                      start=False, stop=(b == NT - 1 and a == 2))
                    if i < 8 and b >= 2:
                        weight_piece(8 * i + b - 2)
                last.then_inc(s_agg, 1)

            def ffn_in(i, u):
                pe.wait_ge(s_xq, i + 1)
                for k in range(KD):
                    last = tr(bank16(6)[:, k * P:(k + 1) * P], xq[:, u, k * P:(k + 1) * P], id16[:, :])
                last.then_inc(s_xqt, 1)
                pe.wait_ge(s_xqc, i + 1)
                for n in range(8):
                    pe.wait_ge(s_ge, 8 * i + n + 1)
                    hold(pe)
                    for k in range(KD):
                        last = mm(ps[:, n % 4, :], xqt[:, u, k, :], w1q[:, k, n * 512:(n + 1) * 512],
                                  start=(k == 0), stop=(k == KD - 1))
                    last.then_inc(s_f1, 1)

            def ffn_out(i):
                def hidden_t(q):
                    for k in range(KD):
                        last = tr(bank16(7 - q % 2)[:, k * P:(k + 1) * P], hq[:, (8 * q + k) * P:(8 * q + k + 1) * P], id16[:, :])
                    last.then_inc(s_hqt, 1)

                pe.wait_ge(s_hq, 2 + i + 1)
                hidden_t(0)
                hidden_t(1)
                if not isinstance(i, int) or i > 0:
                    pe.wait_ge(s_f2r, i)
                for q in range(4):
                    pe.wait_ge(s_hqc, 4 * i + q + 1)
                    hold(pe)
                    if 1 <= q <= 2:
                        hidden_t(q + 1)
                    for k in range(8 * q, 8 * q + 8):
                        for h in range(2):
                            last = mm(ps[:, 4 + h, :], hqt[:, k, :], w2q[:, k, h * 512:(h + 1) * 512],
                                      start=(k == 0), stop=(k == KF - 1))
                last.then_inc(s_f2, 1)

            pe.wait_ge(s_fc, 4 + 64)
            pe.wait_ge(s_aggread, 2 + NT)
            ffn_in(0, 0)
            ffn_in(1, 1)
            ffn_out(0)

            def ffn(i, u):
                ffn_in(i + 1, 1 - u)
                ffn_out(i)

            with pe.Fori(0, NT // 2 - 1) as j:
                ffn(2 * j + 1, 1)
                ffn(2 * j + 2, 0)
            ffn_out(NT - 1)

        @block.scalar
        def _(act):
            cp = nc.scalar.activation
            act.sem_inc(s_winread, 2)
            act.sem_inc(s_abs, 2)
            act.sem_inc(s_gch, 1)
            act.sem_inc(s_g1r, 2)
            act.sem_inc(s_wth, 1)
            act.sem_inc(s_fc, 4)
            act.sem_inc(s_ge, 4)

            def window(w, u, j, blk, ub):
                act.wait_ge(s_win, w + 1)
                act.wait_ge(s_built, blk + 1)
                rows = slice(WIN * j, WIN * j + WIN)
                pw = ps[:, 3 * u:3 * u + 3, :].rearrange("p b c -> p (b c)")
                cp(st_a[rows, ub, :], pw[0:32, 0:NP], ACT.Copy).then_inc(s_stage, 1)
                cp(st_wh[rows, ub, :], pw[32:64, 0:D], ACT.Copy).then_inc(s_stage, 1)
                cp(st_wl[rows, ub, :], pw[64:96, 0:D], ACT.Copy).then_inc(s_stage, 1)
                act.wait_ge(s_stage, 3 * w + 3)
                act.sem_inc(s_winread, 1)

            def abs_piece(n, u):
                act.wait_ge(s_absin[u], 8 * n - 8 * u + 16)
                cp(abs_in[:, u, :], abs_in[:, u, :], ACT.Abs, accum_out=abs_acc[:, bass.ds(n, 1)]).then_inc(s_abs, 1)

            window(0, 0, 0, 0, 0)
            with act.Fori(0, NW // 8 - 1) as bb:
                for v in range(1, 9):
                    window(8 * bb + v, v % 2, v % 4, 2 * bb + v // 4, (v // 4) % 2)
                    abs_piece(8 * bb + v - 1, (v - 1) % 2)
            for w in range(NW - 7, NW):
                window(w, w % 2, w % 4, w // 4, (w // 4) % 2)

            def high(n, u):
                act.wait_ge(s_xn, n + 1)
                cp(xh[:, u, :], xn[:, u, :], ACT.Copy).then_inc(s_xh, 1)

            def copy_high(n, u):
                act.wait_ge(s_th, n + 1)
                cp(xth[:, u, :, :].rearrange("p k c -> p (k c)"), bank16(4), ACT.Copy).then_inc(s_xth, 1)

            def normalised(r, body, stored=False):
                high(r, 0)
                high(r + 1, 1)
                copy_high(r, 0)

                def step(i, u):
                    if not last_of(i, NT):
                        act.wait_ge(s_mm, r + i + 1)
                        copy_high(r + i + 1, 1 - u)
                    if not last_of(i, NT, 2):
                        act.wait_ge(s_tl, r + i + 1)
                        if stored:
                            act.wait_ge(s_xstore[u], 16 * i + 32 - 16 * u)
                        high(r + i + 2, u)
                    body(i, u)

                pairs(act, step)

            act.wait_ge(s_built, 2 + NT)
            normalised(R_GNN0, lambda i, u: None)
            act.wait_ge(s_tl, R_MOE)
            act.wait_ge(s_mm, 1 + R_MOE)
            normalised(R_MOE, lambda i, u: None, stored=True)
            act.wait_ge(s_gd, 1)
            cp(rt[:, 1, 0:NT], rt[:, 0, 0:NT], ACT.Exp).then_inc(s_ex, 1)

            b1s = b1c[:, :, :].rearrange("p e h -> p (e h)")

            def split_high(e, q):
                act.wait_ge(s_wst[q], 16 * e + 16)
                w = w1h[:, 4 * q:4 * q + 4, :] if q < 2 else w2h[:, 2 * q - 4:2 * q - 2, :]
                cp(w.rearrange("p k h -> p (k h)"), wstage[:, q, :], ACT.Copy, scale=SW).then_inc(s_wh, 1)

            def gathered(e):
                for s in range(3):
                    m = SM[s]
                    act.wait_ge(s_gth, 3 * e + s + 1)
                    cp(xdh[:, :, s * P:s * P + m], bank16(4).rearrange("p (k c) -> p k c", k=KD)[:, :, 0:m],
                       ACT.Copy).then_inc(s_gch, 1)

            def expert(e, ep):
                for hb in range(KH):
                    act.wait_ge(s_g1, 4 * e + hb + 1)
                    act.wait_ge(s_hl, 4 * e + hb + 1)
                    if hb == 0:
                        act.wait_ge(s_g2, 6 * e + 1)
                    cp(ht32[:, hb % 2, :], ps[:, 6 + hb % 2, 0:CAP], ACT.Relu, bias=b1s[:, bass.ds(4 * e + hb, 1)],
                       scale=SH / (SX * SW)).then_inc(s_g1r, 1)
                    act.wait_ge(s_g1r, 2 + 4 * e + hb + 1)
                    cp(hth[:, hb, :], ht32[:, hb % 2, :], ACT.Copy).then_inc(s_hh, 1)
                if not last_of(e, NE):
                    gathered(e + 1)
                    for q in range(2):
                        split_high(e + 1, q)
                    act.wait_ge(s_g2, 1 + 6 * e + 6)
                    for q in range(2, 4):
                        split_high(e + 1, q)

            act.wait_ge(s_toki, 1)
            act.wait_ge(s_small, 2)
            for q in range(4):
                split_high(0, q)
            gathered(0)
            pairs(act, expert, NE)

            act.wait_ge(s_g2, 1 + 6 * NE)

            def w1_part(i, u):
                act.wait_ge(s_gn[u], 8 * i - 8 * u + 16)
                act.wait_ge(s_wtp, i + 1)
                cp(gnh[:, u, :], gnat[:, u, :], ACT.Copy, scale=SW).then_inc(s_gnh, 1)
                act.wait_ge(s_wtp, 1 + i + 1)
                cp(gwt_h[:, :, bass.ds(i * P, P)], bank16(4).rearrange("p (k c) -> p k c", k=KD), ACT.Copy).then_inc(s_wth, 1)

            pairs(act, w1_part, KD)

            def h_high(i, u):
                act.wait_ge(s_mmread, 2 + R_LIN1 + i + 1)
                flat = hs_h[:, :, :].rearrange("p t d -> p (t d)")
                cp(flat[:, bass.ds(i * D, D)], h32[:, :], ACT.Copy, scale=dinv[:, 1, bass.ds(i, 1)]).then_inc(s_hsh, 1)

            act.wait_ge(s_dinv2, 2)
            normalised(R_LIN1, h_high)

            act.wait_ge(s_mm, 1 + R_LIN1 + NT)
            act.wait_ge(s_hsl, 1 + NT)
            for n in range(64):
                act.wait_ge(s_ft, 2 + n + 1)
                if n < 32:
                    part = w1q[:, :, n * P:(n + 1) * P]
                else:
                    b, o = (n - 32) // 8, (n - 32) % 8
                    part = w2q[:, 8 * b:8 * b + 8, o * P:(o + 1) * P]
                cp(part, bank16(4 + n % 4).rearrange("p (k c) -> p k c", k=KD), ACT.Copy, saturate=False).then_inc(s_fc, 1)

            def ffn_in(i, u):
                act.wait_ge(s_xqt, i + 1)
                cp(xqt[:, u, :, :].rearrange("p k c -> p (k c)"), bank16(6), ACT.Copy).then_inc(s_xqc, 1)
                act.wait_ge(s_hq, i + 1)
                for n in range(8):
                    act.wait_ge(s_f1, 8 * i + n + 1)
                    cp(hf[:, u, n * 512:(n + 1) * 512], ps[:, n % 4, :], ACT.Gelu, scale=fs[:, u, 3:4]).then_inc(s_ge, 1)

            def ffn_out(i):
                for q in range(4):
                    act.wait_ge(s_hqt, 4 * i + q + 1)
                    cp(hqt[:, 8 * q:8 * q + 8, :].rearrange("p k c -> p (k c)"), bank16(7 - q % 2), ACT.Copy).then_inc(s_hqc, 1)

            act.wait_ge(s_fc, 4 + 64)
            act.wait_ge(s_agg, NT)
            ffn_in(0, 0)
            ffn_in(1, 1)
            ffn_out(0)
            with act.Fori(0, NT // 2 - 1) as j:
                ffn_in(2 * j + 2, 0)
                ffn_out(2 * j + 1)
                ffn_in(2 * j + 3, 1)
                ffn_out(2 * j + 2)
            ffn_out(NT - 1)

        @block.vector
        def _(dve):
            v = nc.vector
            steps = Steps(dve, s_dv)

            def do(ins):
                steps.inc(ins)
                steps.wait()

            dve.sem_inc(s_built, 2)
            dve.sem_inc(s_mmread, 2)
            dve.sem_inc(s_gcl, 1)
            dve.sem_inc(s_hl, 2)
            dve.sem_inc(s_g2r, 3)
            dve.sem_inc(s_gnl, 2)
            dve.sem_inc(s_hsl, 1)
            dve.sem_inc(s_wtl, 1)
            dve.sem_inc(s_aggread, 2)
            dve.sem_inc(s_fq, 4)
            dve.sem_inc(s_hq, 2)

            v.memset(nat_i[:, 0, 2, :], -1).then_inc(s_pad, 1)
            v.memset(nat_i[:, 1, 2, :], NP - 1).then_inc(s_pad, 1)
            v.memset(nat_w[:, 2, :], 0.0).then_inc(s_pad, 1)
            dve.wait_ge(s_edges, 16 * 9)
            for a in range(2):
                v.tensor_copy(nat_f[:, a, :, :], nat_i[:, a, :, :]).then_inc(s_natf, 1)
            dve.wait_ge(s_natf, 2)
            steps.inc(v.tensor_reduce(cm[:, 0, :], nat_f[:, 1, :, :], AX.X, ALU.min))
            do(v.tensor_reduce(cm[:, 1, :], nat_f[:, 1, :, :], AX.X, ALU.max))
            v.tensor_copy(cmb[:, :, :], cm[:, :, :].rearrange("p v a -> p (v a)").unsqueeze(2).to_broadcast([P, 6, 48])
                          ).then_inc(s_cmb, 1)
            dve.wait_ge(s_et, 1)
            steps.inc(v.tensor_copy(src_t[:, :], ps[:, 0, 0:CHP]))
            steps.inc(v.tensor_copy(dst_t[:, :], ps[:, 1, 0:CHP]))
            do(v.tensor_scalar(ew32_t[:, :], ps[:, 2, 0:CHP], SW, None, ALU.mult))
            do(v.tensor_copy(ewh_t[:, :], ew32_t[:, :]))
            do(v.tensor_tensor(ewl_t[:, :], ew32_t[:, :], ewh_t[:, :], ALU.subtract))
            dve.wait_ge(s_const, 16)
            dve.wait_ge(s_cmw, 1)
            do(v.tensor_scalar(ov[:, 0, 0:CH], ps[0:48, 4, 0:CH], w_lo[:, 0:1], None, ALU.is_ge))
            do(v.scalar_tensor_tensor(out=ov[:, 1, 0:CH], in0=ps[0:48, 3, 0:CH], scalar=w_lo[:, 1:2], in1=ov[:, 0, 0:CH],
                                      op0=ALU.is_le, op1=ALU.mult))
            do(v.scalar_tensor_tensor(out=ov[:, 0, 0:CH], in0=q_iota[:, 0:CH], scalar=-512.0, in1=ov[:, 1, 0:CH],
                                      op0=ALU.add, op1=ALU.mult))
            do(v.tensor_reduce(kk[:, 0:1], ov[:, 0, 0:CH], AX.X, ALU.min))
            do(v.tensor_scalar(kk[:, 1:2], kk[:, 0:1], 512.0, float(CH), ALU.add, ALU.min))
            do(v.scalar_tensor_tensor(out=ov[:, 0, 0:CH], in0=q_iota[:, 0:CH], scalar=1.0, in1=ov[:, 1, 0:CH],
                                      op0=ALU.add, op1=ALU.mult))
            do(v.tensor_reduce(kk[:, 2:3], ov[:, 0, 0:CH], AX.X, ALU.max))
            do(v.tensor_tensor(kk[:, 3:4], kk[:, 2:3], kk[:, 1:2], ALU.subtract))
            do(v.tensor_scalar(ov[:, 0, 0:NG_MAX], j_iota[:, 0:NG_MAX], kk[:, 3:4], None, ALU.is_lt))
            do(v.tensor_reduce(kk[:, 4:5], ov[:, 0, 0:NG_MAX], AX.X, ALU.add))
            steps.inc(v.tensor_copy(kk16[:, 0:1], kk[:, 1:2]))
            v.tensor_scalar(kk16[:, 1:2], kk[:, 4:5], 1.0, None, ALU.add).then_inc(s_kk, 1)
            dve.wait_ge(s_kr, 1)
            v.tensor_copy(rows_i[:, :, :].rearrange("p a w -> p (a w)"), ps[0:1, 5, 0:96]).then_inc(s_rows, 1)
            dve.wait_ge(s_rows, 1)

            dve.wait_ge(s_b1, 16)
            v.tensor_scalar(b1c[:, :, :], b1c[:, :, :], SH, None, ALU.mult).then_inc(s_small, 1)
            dve.wait_ge(s_wg, 16)
            do(v.tensor_scalar(wg32[:, :, :], wg32[:, :, :], SW, None, ALU.mult))
            do(v.tensor_copy(wgs[:, :, 0:NE], wg32[:, :, :]))
            v.tensor_tensor(wgs[:, :, NE:2 * NE], wg32[:, :, :], wgs[:, :, 0:NE], ALU.subtract).then_inc(s_small, 1)

            def statistics(n, i):
                hold(dve)
                for h in range(2):
                    v.bn_stats(stats[:, h, :], x[:, i, h * 512:(h + 1) * 512]).then_inc(s_bn, 1)
                dve.wait_ge(s_bn, 3 * n + 2)
                hold(dve)
                v.bn_aggr(mv_one[:, :], stats[:, :, :]).then_inc(s_bn, 1)
                dve.wait_ge(s_bn, 3 * n + 3)
                v.tensor_copy(mv[:, i, :], mv_one[:, :]).then_inc(s_stat, 1)

            dve.wait_ge(s_x, 32)
            with dve.Fori(0, NT) as i:
                statistics(i, i)

            with dve.register("dve_chunks") as chunks, dve.register("dve_first") as first:
                dve.reg_mov(chunks, 0)

                def window(w):
                    dve.reg_load(first, rows_i[0:1, 0, bass.ds(w, 1)])
                    groups = dve.value_load(rows_i[0:1, 1, bass.ds(w, 1)], min_val=1, max_val=NG_MAX)
                    with dve.Fori(0, groups):
                        n = dve.snap(chunks, min_val=0, max_val=1 << 20)
                        at = dve.snap(first, min_val=0, max_val=CHP - G)
                        for half in range(2):
                            dve.wait_ge(s_chunk, n + 5 * half + 5)
                            v.tensor_copy(src_g[:, half, :], src_t[:, bass.ds(at + 5 * half, RING)]).then_inc(s_srcg, 5)
                            v.tensor_tensor(st_e[:, half, :, 0:WIN],
                                            iota_r[:, bass.ds(w * WIN, WIN)].unsqueeze(1).to_broadcast([P, RING, WIN]),
                                            dst_t[:, bass.ds(at + 5 * half, RING)].unsqueeze(2).to_broadcast([P, RING, WIN]),
                                            ALU.is_equal).then_inc(s_onehot, 5)
                            dve.wait_ge(s_srcg, n + 5 * half + 5)
                            for c in range(RING):
                                dve.wait_ge(s_chunk, n + 5 * half + c + 6)
                                v.tensor_scalar(oh[:, c, :], iota_r[:, 0:NP], src_g[:, half, c:c + 1], None,
                                                ALU.is_equal).then_inc(s_oh, 1)
                        dve.reg_add(chunks, chunks, G)
                        dve.reg_add(first, first, G)

                def block_parts(b, ub):
                    dve.wait_ge(s_stage, 12 * b + 12)
                    v.tensor_copy(at_h[:, b, :], st_a[:, ub, :]).then_inc(s_blk, 1)
                    dve.wait_ge(s_wsum, b + 1)
                    v.tensor_copy(wt_h[:, b, :], st_wh[:, ub, :]).then_inc(s_blk, 1)
                    dve.wait_ge(s_blk, 4 * b + 2)
                    v.tensor_tensor(at_lo16[:, :], st_a[:, ub, :], at_h[:, b, :], ALU.subtract).then_inc(s_blk, 1)
                    dve.wait_ge(s_blk, 4 * b + 3)
                    hold(dve)
                    v.tensor_copy(at_lo[:, :], at_lo16[:, :], saturate=False).then_inc(s_blk, 1)
                    dve.wait_ge(s_blk, 4 * b + 4)
                    v.tensor_copy(at_l[:, b, :].bitcast(I16), at_lo[:, :].bitcast(I16))
                    v.tensor_tensor(wt_l[:, b, :], st_wh[:, ub, :], wt_h[:, b, :], ALU.subtract).then_inc(s_built, 1)

                window(0)
                with dve.Fori(0, NW // 8 - 1) as bb:
                    for k in range(1, 9):
                        window(8 * bb + k)
                        if k % 4 == 0:
                            block_parts(2 * bb + k // 4 - 1, k // 4 - 1)
                for w in range(NW - 7, NW):
                    window(w)
                    if w % 4 == 0:
                        block_parts(w // 4 - 1, (w // 4 - 1) % 2)
                block_parts(NT - 1, (NT - 1) % 2)

            def norm(r, i, u):
                dve.wait_ge(s_rstd, r + i + 1)
                v.tensor_scalar(xn[:, u, :], x[:, i, :], mv[:, i, 0:1], rstd[:, bass.ds(i, 1)], ALU.subtract, ALU.mult).then_inc(s_xn, 1)

            def low(n, u):
                dve.wait_ge(s_xh, n + 1)
                v.tensor_tensor(xl[:, u, :], xn[:, u, :], xh[:, u, :], ALU.subtract).then_inc(s_xl, 1)

            def copy_low(n, u):
                dve.wait_ge(s_tl, n + 1)
                v.tensor_copy(xtl[:, u, :, :].rearrange("p k c -> p (k c)"), bank16(5)).then_inc(s_xtl, 1)

            def normalised(r, body, stored=False):
                norm(r, 0, 0)
                norm(r, 1, 1)
                low(r, 0)
                low(r + 1, 1)
                copy_low(r, 0)

                def step(i, u):
                    if not last_of(i, NT):
                        dve.wait_ge(s_mm, r + i + 1)
                        copy_low(r + i + 1, 1 - u)
                    if not last_of(i, NT, 2):
                        norm(r, i + 2, u)
                        low(r + i + 2, u)
                    body(i, u)

                pairs(dve, step)

            def pair_banks(u):
                return ps[:, 2 * u:2 * u + 2, :].rearrange("p b c -> p (b c)")

            def gnn0(i, u):
                dve.wait_ge(s_biased, i + 1)
                dve.wait_ge(s_mm, 1 + R_GNN0 + i + 1)
                v.scalar_tensor_tensor(out=x[:, i, :], in0=pair_banks(u), scalar=1.0 / (SX * SW), in1=x[:, i, :],
                                       op0=ALU.mult, op1=ALU.add).then_inc(s_mmread, 1)
                dve.wait_ge(s_mmread, 2 + R_GNN0 + i + 1)
                statistics(NT + i, i)

            dve.wait_ge(s_built, 2 + NT)
            normalised(R_GNN0, gnn0)

            def logits_of(i, u):
                dve.wait_ge(s_mm, 1 + R_MOE + i + 1)
                v.tensor_reduce(logits[:, i, :], ps[:, 6 + u, 0:2 * NE].rearrange("p (a e) -> p e a", a=2), AX.X,
                                ALU.add).then_inc(s_mmread, 1)

            normalised(R_MOE, logits_of)
            dve.wait_ge(s_mmread, 2 + R_MOE + NT)
            dve.wait_ge(s_const, 23)
            do(v.tensor_scalar(logits[:, :, :], logits[:, :, :], 1.0 / (SX * SW), None, ALU.mult))
            for t in range(NT):
                steps.inc(v.max(lmax[:, t, :], logits[:, t, :]))
            steps.wait()
            for t in range(NT):
                steps.inc(v.max_index(lidx[:, t, :], lmax[:, t, :], logits[:, t, :]))
            v.tensor_tensor(rt[:, 0, 0:NT], lmax[:, :, 1], lmax[:, :, 0], ALU.subtract).then_inc(s_gd, 1)
            steps.wait()
            do(v.tensor_copy(lidf[:, :, :], lidx[:, :, :]))
            for k in range(2):
                steps.inc(v.tensor_tensor(mask[:, k, :, :], iota_lo[:, 0:NE].unsqueeze(1).to_broadcast([P, NT, NE]),
                                          lidf[:, :, k:k + 1].to_broadcast([P, NT, NE]), ALU.is_equal))
                steps.inc(v.tensor_copy(rt[:, 5, k * NT:(k + 1) * NT], lidf[:, :, k]))
            steps.wait()
            v.tensor_tensor(mask[:, :, :, :], mask[:, :, :, :], valid_m[:, :, :, :], ALU.mult).then_inc(s_mask, 1)
            dve.wait_ge(s_ex, 1)
            do(v.tensor_scalar(rt[:, 2, 0:NT], rt[:, 1, 0:NT], 1.0, None, ALU.add))
            do(v.reciprocal(gates[:, 0, :], rt[:, 2, 0:NT]))
            do(v.tensor_tensor(gates[:, 1, :], rt[:, 1, 0:NT], gates[:, 0, :], ALU.mult))
            dve.wait_ge(s_cum, 1)
            dve.wait_ge(s_mask, 1)
            by_e = "p (n e) -> p e n"
            do(v.tensor_copy(tot_e[:, :, :], ps[:, 1, 0:2 * NT * NE].rearrange(by_e, e=NE)))
            do(v.tensor_tensor_scan(scan_o[:, :, :].rearrange("p e n -> p (e n)"), scan_m[:, :, :].rearrange("p e n -> p (e n)"),
                                    tot_e[:, :, :].rearrange("p e n -> p (e n)"), 0.0, ALU.mult, ALU.add))
            do(v.tensor_tensor(scan_o[:, :, :], scan_o[:, :, :], tot_e[:, :, :], ALU.subtract))
            do(v.scalar_tensor_tensor(out=loc3[:, :, :], in0=ps[:, 0, 0:2 * NT * NE].rearrange("p (n e) -> p n e", e=NE),
                                      scalar=-1.0, in1=scan_o[:, :, :].rearrange("p e n -> p n e"), op0=ALU.add, op1=ALU.add))
            do(v.tensor_tensor(loc3[:, :, :], loc3[:, :, :], mask[:, :, :, :].rearrange("p k t e -> p (k t) e"), ALU.mult))
            do(v.tensor_reduce(rt[:, 2, :], loc3[:, :, :], AX.X, ALU.add))
            do(v.tensor_scalar(rt[:, 3, :], rt[:, 2, :], float(CAP), None, ALU.is_lt))
            steps.inc(v.tensor_tensor(gates[:, :, :].rearrange("p k t -> p (k t)"), gates[:, :, :].rearrange("p k t -> p (k t)"),
                                      rt[:, 3, :], ALU.mult))
            do(v.tensor_tensor(rt[:, 4, :], rt[:, 3, :], valid_m[:, :, :, 0].rearrange("p k t -> p (k t)"), ALU.mult))
            do(v.tensor_scalar(rt[:, 6, :], rt[:, 2, :], float(CAP - 1), None, ALU.min))
            do(v.scalar_tensor_tensor(out=rt[:, 7, :], in0=rt[:, 5, :], scalar=float(CAP), in1=rt[:, 6, :],
                                      op0=ALU.mult, op1=ALU.add))
            steps.inc(v.tensor_copy(slot_i[:, :], rt[:, 7, :]))
            steps.inc(v.tensor_scalar(rt[:, 8, :], rt[:, 2, :], float(P), None, ALU.is_ge))
            do(v.tensor_scalar(rt[:, 9, :], rt[:, 2, :], float(2 * P), None, ALU.is_ge))
            do(v.tensor_tensor(rt[:, 8, :], rt[:, 8, :], rt[:, 9, :], ALU.add))
            steps.inc(v.scalar_tensor_tensor(out=rt[:, 10, :], in0=rt[:, 8, :], scalar=-float(P), in1=rt[:, 2, :],
                                             op0=ALU.mult, op1=ALU.add))
            do(v.scalar_tensor_tensor(out=rt[:, 11, :], in0=rt[:, 5, :], scalar=3.0, in1=rt[:, 8, :],
                                      op0=ALU.mult, op1=ALU.add))
            do(v.scalar_tensor_tensor(out=rt[:, 9, :], in0=rt[:, 11, :], scalar=1.0, in1=rt[:, 4, :],
                                      op0=ALU.add, op1=ALU.mult))
            do(v.tensor_scalar(rt[:, 11, :], rt[:, 9, :], -1.0, None, ALU.add))
            steps.inc(v.tensor_tensor(oh_lo[:, :, :], iota_lo[:, :].unsqueeze(1).to_broadcast([P, 2 * NT, P]),
                                      rt[:, 10, :].unsqueeze(2).to_broadcast([P, 2 * NT, P]), ALU.is_equal))
            do(v.tensor_tensor(oh_hi[:, :, :], iota_lo[:, 0:3 * NE].unsqueeze(1).to_broadcast([P, 2 * NT, 3 * NE]),
                               rt[:, 11, :].unsqueeze(2).to_broadcast([P, 2 * NT, 3 * NE]), ALU.is_equal))
            v.tensor_tensor(oh_hi2[:, :, :], oh_hi[:, :, :], tok_f[:, :].unsqueeze(2).to_broadcast([P, 2 * NT, 3 * NE]),
                            ALU.mult).then_inc(s_ohr, 1)
            dve.wait_ge(s_tok, 1)
            v.tensor_copy(tok_i[:, :], ps[:, 2, 0:3 * NE]).then_inc(s_toki, 1)

            def split_low(e, q):
                dve.wait_ge(s_wh, 4 * e + q + 1)
                hi, lo = (w1h, w1l) if q < 2 else (w2h, w2l)
                part = slice(4 * q, 4 * q + 4) if q < 2 else slice(2 * q - 4, 2 * q - 2)
                flat = "p k h -> p (k h)"
                v.scalar_tensor_tensor(out=lo[:, part, :].rearrange(flat), in0=wstage[:, q, :], scalar=SW,
                                       in1=hi[:, part, :].rearrange(flat), op0=ALU.mult, op1=ALU.subtract).then_inc(s_wl, 1)

            def gathered(e):
                for s in range(3):
                    m = SM[s]
                    dve.wait_ge(s_gtl, 3 * e + s + 1)
                    v.tensor_copy(xdl[:, :, s * P:s * P + m],
                                  bank16(5).rearrange("p (k c) -> p k c", k=KD)[:, :, 0:m]).then_inc(s_gcl, 1)

            def expert(e, ep):
                for hb in range(KH):
                    dve.wait_ge(s_hh, 4 * e + hb + 1)
                    v.tensor_tensor(htl[:, hb, :], ht32[:, hb % 2, :], hth[:, hb, :], ALU.subtract).then_inc(s_hl, 1)
                if not last_of(e, NE):
                    gathered(e + 1)
                    for q in range(2):
                        split_low(e + 1, q)
                dve.wait_ge(s_b2, 16 * e + 16)
                for s in range(3):
                    m, u = SM[s], (ep + s) % 2
                    dve.wait_ge(s_eout[u], 24 * e + 8 * s - 8 * u + 16)
                    for h in range(2):
                        dve.wait_ge(s_g2, 1 + 6 * e + 2 * s + h + 1)
                        cols = slice(h * 512, (h + 1) * 512)
                        v.scalar_tensor_tensor(out=eo[0:m, u, cols], in0=ps[0:m, (2 * s + h) % 3, :], scalar=1.0 / (SH * SW),
                                               in1=b2b[0:m, cols], op0=ALU.mult, op1=ALU.add).then_inc(s_g2r, 1)
                if not last_of(e, NE):
                    for q in range(2, 4):
                        split_low(e + 1, q)

            dve.wait_ge(s_toki, 1)
            for q in range(4):
                split_low(0, q)
            gathered(0)
            pairs(dve, expert, NE)

            def w1_part(i, u):
                dve.wait_ge(s_gnh, i + 1)
                dve.wait_ge(s_wtp, i + 1)
                v.scalar_tensor_tensor(out=gnl[:, u, :], in0=gnat[:, u, :], scalar=SW, in1=gnh[:, u, :],
                                       op0=ALU.mult, op1=ALU.subtract).then_inc(s_gnl, 1)
                dve.wait_ge(s_wtp, 1 + i + 1)
                v.tensor_copy(gwt_l[:, :, bass.ds(i * P, P)], bank16(5).rearrange("p (k c) -> p k c", k=KD)).then_inc(s_wtl, 1)

            pairs(dve, w1_part, KD)

            for i in range(NT):
                for k in range(2):
                    n = 2 * i + k
                    dve.wait_ge(s_back[n % 3], 16 * (n // 3) + 16)
                    v.scalar_tensor_tensor(out=x[:, i, :], in0=back[:, n % 3, :], scalar=gates[:, k, i:i + 1],
                                           in1=x[:, i, :], op0=ALU.mult, op1=ALU.add).then_inc(s_mix, 1)
                    dve.wait_ge(s_mix, n + 1)
                statistics(2 * NT + i, i)
            dve.wait_ge(s_deg, 1)
            v.tensor_scalar(dinv[:, 1, :], ps[:, 6, 0:NT], 1.0, None, ALU.add).then_inc(s_degp, 1)
            dve.wait_ge(s_dinv, 1)
            v.tensor_scalar(dinv[:, 1, :], dinv[:, 0, :], SH, None, ALU.mult).then_inc(s_dinv2, 1)
            v.tensor_scalar(dinv[:, 2, :], dinv[:, 0, :], 1.0 / SH, None, ALU.mult).then_inc(s_dinv2, 1)
            dve.wait_ge(s_dinv2, 2)
            dve.wait_ge(s_abs, 2 + 32)
            v.tensor_reduce(sw[:, 0:2], abs_acc[:, :].rearrange("p (m n) -> p m n", m=2), AX.X, ALU.add).then_inc(s_swp, 1)
            dve.wait_ge(s_swm, 1)
            do(v.tensor_scalar(sw[:, 2:4], ps[:, 7, 0:2], 1.0 / (D * FH), Q_EPS, ALU.mult, ALU.max))
            steps.inc(v.tensor_scalar(sw[:, 4:6], sw[:, 2:4], 0.5, None, ALU.mult))
            do(v.tensor_scalar(sw[:, 6:8], sw[:, 2:4], -0.5, None, ALU.mult))
            dve.wait_ge(s_bias, 32)

            def lin1(i, u):
                dve.wait_ge(s_hsl, i + 1)
                dve.wait_ge(s_mm, 1 + R_LIN1 + i + 1)
                v.scalar_tensor_tensor(out=h32[:, :], in0=pair_banks(u), scalar=1.0 / (SX * SW), in1=bias_b[:, :],
                                       op0=ALU.mult, op1=ALU.add).then_inc(s_mmread, 1)
                dve.wait_ge(s_hsh, i + 1)
                v.scalar_tensor_tensor(out=hs_l[:, i, :], in0=h32[:, :], scalar=dinv[:, 1, bass.ds(i, 1)],
                                       in1=hs_h[:, i, :], op0=ALU.mult, op1=ALU.subtract).then_inc(s_hsl, 1)

            normalised(R_LIN1, lin1)

            def agg(i, u):
                dve.wait_ge(s_agg, i + 1)
                v.scalar_tensor_tensor(out=x[:, i, :], in0=pair_banks(u), scalar=dinv[:, 2, bass.ds(i, 1)], in1=x[:, i, :],
                                       op0=ALU.mult, op1=ALU.add).then_inc(s_aggread, 1)
                dve.wait_ge(s_aggread, 2 + i + 1)
                statistics(3 * NT + i, i)

            def below(n):
                if n >= 2:
                    dve.wait_ge(s_fq, 4 + n - 1)
                dve.wait_ge(s_fn[n % 4], 16 * (n // 4) + 16)
                m = n // 32
                v.tensor_scalar(fneg[:, n % 2, :], fnat[n % 4], sw[:, 6 + m:7 + m], None, ALU.is_lt,
                                saturate=False).then_inc(s_fneg, 1)

            def weight_piece(n):
                m = n // 32
                if n < 63:
                    below(n + 1)
                dve.wait_ge(s_fneg, n + 1)
                dve.wait_ge(s_ft, n + 1)
                v.scalar_tensor_tensor(out=fq[:, n % 2, :], in0=fnat[n % 4], scalar=sw[:, 4 + m:5 + m],
                                       in1=fneg[:, n % 2, :], op0=ALU.is_gt, op1=ALU.subtract).then_inc(s_fq, 1)

            below(0)
            for i in range(8):
                for k in range(8):
                    weight_piece(8 * i + k)
                    if k == 2 and i > 0:
                        agg(i - 1, (i - 1) % 2)

            qsteps = Steps(dve, s_dq)

            def dq(ins):
                qsteps.inc(ins)
                qsteps.wait()

            def quantise(i, u):
                qsteps.at(0 if isinstance(i, int) and i == 0 else 10 * i - 5)
                dve.wait_ge(s_rstd, 3 * NT + i + 1)
                one = bass.ds(i, 1)
                dq(v.tensor_scalar(xn_f[:, u, :], x[:, i, :], mv[:, i, 0:1], rstd[:, one], ALU.subtract, ALU.mult))
                dq(v.tensor_reduce(fs[:, u, 0:1], xn_f[:, u, :], AX.X, ALU.max, apply_absolute_value=True))
                dq(v.tensor_scalar(fs[:, u, 1:2], fs[:, u, 0:1], Q_EPS, 1.0 / 127.0, ALU.max, ALU.mult))
                v.tensor_tensor(fs[:, u, 3:4], fs[:, u, 1:2], sw[:, 2:3], ALU.mult)
                dq(v.reciprocal(fs[:, u, 2:3], fs[:, u, 1:2]))
                dq(v.tensor_scalar(xn_f[:, u, :], xn_f[:, u, :], fs[:, u, 2:3], MAGIC, ALU.mult, ALU.add))
                v.tensor_scalar(xq[:, u, :], xn_f[:, u, :], -MAGIC, 127.0, ALU.add, ALU.min).then_inc(s_xq, 1)

            def quantise_hidden(i, u):
                qsteps.at(10 * i + 5 if last_of(i, NT) else 10 * i + 10)
                for n in range(8):
                    dve.wait_ge(s_ge, 4 + 8 * i + n + 1)
                    last = v.tensor_reduce(hm[:, u, n:n + 1], hf[:, u, n * 512:(n + 1) * 512], AX.X, ALU.max,
                                           apply_absolute_value=True)
                dq(last)
                dq(v.tensor_reduce(fs[:, u, 8:9], hm[:, u, :], AX.X, ALU.max))
                dq(v.tensor_scalar(fs[:, u, 9:10], fs[:, u, 8:9], Q_EPS, 1.0 / 127.0, ALU.max, ALU.mult))
                v.tensor_tensor(fs[:, u, 11:12], fs[:, u, 9:10], sw[:, 3:4], ALU.mult)
                dq(v.reciprocal(fs[:, u, 10:11], fs[:, u, 9:10]))
                dq(v.tensor_scalar(hf[:, u, :], hf[:, u, :], fs[:, u, 10:11], MAGIC, ALU.mult, ALU.add))
                if not isinstance(i, int) or i > 0:
                    dve.wait_ge(s_hqt, 4 * i)
                v.tensor_scalar(hq[:, :], hf[:, u, :], -MAGIC, 127.0, ALU.add, ALU.min).then_inc(s_hq, 1)

            def result(i, u):
                dve.wait_ge(s_f2, i + 1)
                dve.wait_ge(s_out[u], 8 * i - 8 * u + 16)
                v.scalar_tensor_tensor(out=out_t[:, u, :], in0=ps[:, 4:6, :].rearrange("p b c -> p (b c)"),
                                       scalar=fs[:, u, 11:12], in1=x[:, i, :], op0=ALU.mult, op1=ALU.add).then_inc(s_f2r, 1)

            def ffn(i, u):
                quantise_hidden(i + 1, 1 - u)
                if not last_of(i, NT, 3):
                    quantise(i + 3, 1 - u)
                result(i, u)

            dve.wait_ge(s_ft, 2 + 64)
            agg(NT - 3, 1)
            quantise(0, 0)
            quantise(1, 1)
            agg(NT - 2, 0)
            agg(NT - 1, 1)
            quantise_hidden(0, 0)
            quantise(2, 0)
            with dve.Fori(0, NT // 2 - 2) as j:
                for u in range(2):
                    ffn(2 * j + u, u)
            for i in range(NT - 4, NT - 1):
                ffn(i, i % 2)
            result(NT - 1, (NT - 1) % 2)


_INS = ["x", "src", "dst", "edge_weight", "L0_gnn_bias", "L0_ffn_wg", "L0_ffn_w1", "L0_ffn_b1", "L0_ffn_w2", "L0_ffn_b2",
        "L1_gnn_W", "L1_gnn_b", "L1_ffn_w1", "L1_ffn_w2"]


def kernel(**inputs):
    import numpy as np
    import concourse.bacc as bacc
    from concourse.bass_utils import run_bass_kernel_spmd

    nc = bacc.Bacc("TRN2", target_bir_lowering=False, num_devices=1)
    arrays, args = {}, []
    for name in _INS:
        a = np.ascontiguousarray(inputs[name])
        arrays[f"in_{name}"] = a
        args.append(nc.dram_tensor(f"in_{name}", a.shape, mybir.dt.from_np(a.dtype), kind="ExternalInput").ap())
    out = nc.dram_tensor("out_x", (N, D), F32, kind="ExternalOutput").ap()
    build_kernel(nc, *args, out)
    r = run_bass_kernel_spmd(nc, [arrays], core_ids=[0])
    return r.results[0]["out_x"]
```

```python
from contextlib import ExitStack

import concourse.bass as bass
from concourse import mybir

F32 = mybir.dt.float32
F16 = mybir.dt.float16
F8 = mybir.dt.float8e4
I32 = mybir.dt.int32
I16 = mybir.dt.int16
U32 = mybir.dt.uint32
ALU = mybir.AluOpType
ACT = mybir.ActivationFunctionType
AX = mybir.AxisListType

P = 128
N = 1250
D = 1024
NT = (N + P - 1) // P
LAST = N - (NT - 1) * P
NP = NT * P
KD = D // P
E_EDGES = 41250
CH = (E_EDGES + P - 1) // P
CHP = 3 * P
WIN = 32
NW = NP // WIN
G = 10
RING = 5
NG_MAX = (CH + G - 1) // G
NE = 8
HID = 512
CAP = 2 * ((N + NE - 1) // NE)
SM = [P, P, CAP - 2 * P]
KH = HID // P
FH = 4096
KF = FH // P

SX = 1024.0
SW = 256.0
SH = 64.0
MAGIC = 12582912.0
LN_EPS = 1e-5
Q_EPS = 1e-5


class Steps:

    def __init__(self, eng, sem, base=0):
        self.eng, self.sem, self.base, self.n = eng, sem, base, 0

    def at(self, base):
        self.base, self.n = base, 0

    def inc(self, ins):
        ins.then_inc(self.sem, 1)
        self.n += 1

    def wait(self):
        self.eng.wait_ge(self.sem, self.base + self.n)


def build_kernel(nc, x_in, src_in, dst_in, ew_in, bias0_in, wg_in, w1_in, b1_in, w2_in, b2_in,
                 gw_in, gb_in, f1_in, f2_in, out):
    ctx = ExitStack()
    with ctx:
        OFF_X = (nc.sbuf_base + 31) // 32 * 32
        OFF_MISC = OFF_X + NT * D * 4
        OFF_AT = OFF_MISC + 14336
        OFF_LN = OFF_AT + NT * NP * 3
        OFF_BIG = OFF_LN + 26624
        END = nc.sbuf_usable_end // 32 * 32
        OFF_HS = END - 2 * NT * D * 2

        cur = {"x": OFF_X, "misc": OFF_MISC, "ln": OFF_LN, "at": OFF_AT, "big": OFF_BIG}
        lim = {"x": OFF_MISC, "misc": OFF_AT, "at": OFF_LN, "ln": OFF_BIG, "big": END, "wide": OFF_HS, "late": OFF_LN,
               "route": OFF_HS}

        def sb(area, name, shape, dt):
            n = 1
            for d in shape[1:]:
                n *= d
            size = (n * (2 if dt == F16 else 1 if dt == F8 else 4) + 31) // 32 * 32
            off = cur[area]
            cur[area] = off + size
            assert cur[area] <= lim[area], (area, name, cur[area] - lim[area])
            return nc.alloc_sbuf_tensor_at(name, shape, dt, offset=off)

        def restart(area, off):
            cur[area] = off

        def sem(name):
            return ctx.enter_context(nc.semaphore(name))

        x = sb("x", "x", [P, NT, D], F32)
        id16 = sb("misc", "id16", [P, P], F16)
        id32 = sb("misc", "id32", [P, P], F32)
        tri = sb("misc", "tri", [P, P], F16)
        ones16 = sb("misc", "ones16", [P, P], F16)
        zero16 = sb("misc", "zero16", [P, 96], F16)
        ones32 = sb("misc", "ones32", [P, P], F32)
        bias_b = sb("misc", "bias_b", [P, D], F32)
        stats = sb("misc", "stats", [P, 2, 6], F32)
        mv_one = sb("misc", "mv_one", [P, 2], F32)
        mv = sb("misc", "mv", [P, NT, 2], F32)
        rstd = sb("misc", "rstd", [P, NT], F32)
        rtmp = sb("misc", "rtmp", [P, 2], F32)
        consts = sb("misc", "consts", [P, 4], F32)
        rows_i = sb("misc", "rows_i", [1, 2, 48], I32)
        abs_acc = sb("misc", "abs_acc", [P, 32], F32)
        sw = sb("misc", "sw", [P, 8], F32)
        gates = sb("misc", "gates", [P, 2, NT], F32)
        slot_i = sb("misc", "slot_i", [P, 2 * NT], I32)
        tok_i = sb("misc", "tok_i", [P, 3 * NE], I32)
        b1c = sb("misc", "b1c", [P, NE, KH], F32)
        dinv = sb("misc", "dinv", [P, 3, NT], F32)
        fs = sb("misc", "fs", [P, 2, 16], F32)
        hm = sb("misc", "hm", [P, 2, 8], F32)

        wg32 = sb("misc", "wg32", [P, KD, NE], F32)
        wgs = sb("misc", "wgs", [P, KD, 2 * NE], F16)

        misc_mark = cur["misc"]
        iota_r = sb("misc", "iota_r", [P, NP], F16)

        xn = sb("ln", "xn", [P, 2, D], F32)
        xh = sb("ln", "xh", [P, 2, D], F16)
        xl = sb("ln", "xl", [P, 2, D], F16)
        xth = sb("ln", "xth", [P, 2, KD, P], F16)
        xtl = sb("ln", "xtl", [P, 2, KD, P], F16)
        restart("ln", OFF_LN)
        st_a = sb("ln", "st_a", [P, 2, NP], F32)
        st_wh = sb("ln", "st_wh", [P, 2, D], F32)
        st_wl = sb("ln", "st_wl", [P, 2, D], F32)
        restart("ln", OFF_LN)
        gx = sb("ln", "gx", [P, 2, 2 * D], F16)
        eo = sb("ln", "eo", [P, 2, D], F32)
        b2b = sb("ln", "b2b", [P, D], F32)
        ht32 = sb("ln", "ht32", [P, 2, CAP], F32)
        htl = sb("ln", "htl", [P, KH, CAP], F16)

        at_h = sb("at", "at_h", [P, NT, NP], F16)
        at_l = sb("at", "at_l", [P, NT, NP], F8)

        wt_h = sb("big", "wt_h", [P, NT, D], F16)
        wt_l = sb("big", "wt_l", [P, NT, D], F16)
        src_t = sb("big", "src_t", [P, CHP], F32)
        dst_t = sb("big", "dst_t", [P, CHP], F32)
        ewh_t = sb("big", "ewh_t", [P, CHP], F16)
        ewl_t = sb("big", "ewl_t", [P, CHP], F16)
        src_g = sb("big", "src_g", [P, 2, RING], F32)
        st_e = sb("big", "st_e", [P, 2, RING, 96], F16)
        big_mark = cur["big"]
        oh = sb("big", "oh", [P, RING, NP], F16)
        at_lo16 = sb("big", "at_lo16", [P, NP], F16)
        at_lo = sb("big", "at_lo", [P, NP], F8)
        abs_in = sb("big", "abs_in", [P, 2, 2048], F32)
        restart("big", big_mark)
        nat_i = sb("big", "nat_i", [P, 2, 3, P], I32)
        nat_f = sb("big", "nat_f", [P, 2, 3, P], F32)
        nat_w = sb("big", "nat_w", [P, 3, P], F32)
        ew32_t = sb("big", "ew32_t", [P, CHP], F32)
        cm = sb("big", "cm", [P, 2, 3], F32)
        cmb = sb("big", "cmb", [P, 6, 48], F16)
        q_iota = sb("big", "q_iota", [48, CHP], F32)
        w_lo = sb("big", "w_lo", [48, 2], F32)
        ov = sb("big", "ov", [48, 2, CHP], F32)
        j_iota = sb("big", "j_iota", [48, 40], F32)
        kk = sb("big", "kk", [48, 8], F32)
        kk16 = sb("big", "kk16", [48, 2], F16)
        restart("big", OFF_BIG)
        wstage = sb("big", "wstage", [P, 4, 2048], F32)
        w1h = sb("big", "w1h", [P, KD, HID], F16)
        w1l = sb("big", "w1l", [P, KD, HID], F16)
        w2h = sb("big", "w2h", [P, KH, D], F16)
        w2l = sb("big", "w2l", [P, KH, D], F16)
        xdh = sb("big", "xdh", [P, KD, CAP], F16)
        xdl = sb("big", "xdl", [P, KD, CAP], F16)
        hth = sb("big", "hth", [P, KH, CAP], F16)
        cur["route"] = OFF_BIG + 49152
        logits = sb("route", "logits", [P, NT, NE], F32)
        scan_m = sb("route", "scan_m", [P, NE, 2 * NT], F32)
        iota_lo = sb("route", "iota_lo", [P, P], F32)
        tok_f = sb("route", "tok_f", [P, 2 * NT], F32)
        valid_m = sb("route", "valid_m", [P, 2, NT, NE], F16)
        restart("ln", OFF_LN)
        lmax = sb("ln", "lmax", [P, NT, 8], F32)
        lidx = sb("ln", "lidx", [P, NT, 8], U32)
        lidf = sb("ln", "lidf", [P, NT, 8], F32)
        mask = sb("ln", "mask", [P, 2, NT, NE], F16)
        tot_e = sb("ln", "tot_e", [P, NE, 2 * NT], F32)
        scan_o = sb("ln", "scan_o", [P, NE, 2 * NT], F32)
        loc3 = sb("ln", "loc3", [P, 2 * NT, NE], F32)
        rt = sb("ln", "rt", [P, 12, 2 * NT], F32)
        oh_lo = sb("ln", "oh_lo", [P, 2 * NT, P], F16)
        oh_hi = sb("ln", "oh_hi", [P, 2 * NT, 3 * NE], F16)
        oh_hi2 = sb("ln", "oh_hi2", [P, 2 * NT, 3 * NE], F16)
        restart("big", OFF_HS)
        xs_all = sb("big", "xs_all", [P, NT, 2 * D], F16)
        restart("big", OFF_BIG)
        gwt_h = sb("big", "gwt_h", [P, KD, D], F16)
        gwt_l = sb("big", "gwt_l", [P, KD, D], F16)
        h32 = sb("big", "h32", [P, D], F32)
        back_a = sb("big", "back_a", [P, 3, D], F32)
        restart("big", END - 4 * D)
        back_b = sb("big", "back_b", [P, D], F32)
        back = [back_a[:, 0, :], back_a[:, 1, :], back_a[:, 2, :], back_b[:, :]]
        restart("big", OFF_HS)
        hs_h = sb("big", "hs_h", [P, NT, D], F16)
        hs_l = sb("big", "hs_l", [P, NT, D], F16)
        restart("big", OFF_HS)
        gnat = sb("big", "gnat", [P, 2, D], F32)
        gnh = sb("big", "gnh", [P, 2, D], F16)
        gnl = sb("big", "gnl", [P, 2, D], F16)
        cur["wide"] = OFF_LN
        w1q = sb("wide", "w1q", [P, KD, FH], F8)
        w2q = sb("wide", "w2q", [P, KF, D], F8)
        stage_mark = cur["wide"]
        fnat_a = sb("wide", "fnat_a", [P, 3, D], F32)
        fnat = [fnat_a[:, 0, :], fnat_a[:, 1, :], fnat_a[:, 2, :], bias_b[:, :]]
        restart("misc", misc_mark)
        fq = sb("misc", "fq", [P, 2, D], F16)
        fneg = sb("misc", "fneg", [P, 2, D], F8)
        restart("wide", stage_mark)
        xn_f = sb("wide", "xn_f", [P, 2, D], F32)
        xq = sb("wide", "xq", [P, 2, D], F16)
        cur["late"] = OFF_AT
        hf = sb("late", "hf", [P, 2, FH], F32)
        restart("big", OFF_HS)
        hq = sb("big", "hq", [P, FH], F16)
        hqt = sb("big", "hqt", [P, KF, P], F16)
        out_t = sb("big", "out_t", [P, 2, D], F32)
        xqt = sb("big", "xqt", [P, 2, KD, P], F16)

        ps = ctx.enter_context(nc.psum_tensor("ps", [P, 8, 512], F32))

        def bank16(b):
            return ps[:, b, :].bitcast(F16)

        xs_d = nc.dram_tensor("xs_d", [NP, 2 * D], F16).ap()
        eo_d = nc.dram_tensor("eo_d", [NE * CAP, D], F32).ap()

        s_pad = sem("s_pad")
        s_edges = sem("s_edges")
        s_x = sem("s_x")
        s_bias = sem("s_bias")
        s_b1 = sem("s_b1")
        s_wg = sem("s_wg")
        s_absin = [sem(f"s_absin{u}") for u in range(2)]
        s_const = sem("s_const")
        s_dv = sem("s_dv")
        s_natf = sem("s_natf")
        s_cmb = sem("s_cmb")
        s_et = sem("s_et")
        s_cmw = sem("s_cmw")
        s_kk = sem("s_kk")
        s_kr = sem("s_kr")
        s_rows = sem("s_rows")
        s_small = sem("s_small")
        s_srcg = sem("s_srcg")
        s_onehot = sem("s_onehot")
        s_st = sem("s_st")
        s_oh = sem("s_oh")
        s_chunk = sem("s_chunk")
        s_win = sem("s_win")
        s_winread = sem("s_winread")
        s_stage = sem("s_stage")
        s_ath = sem("s_ath")
        s_wtb = sem("s_wtb")
        s_atlo = sem("s_atlo")
        s_wsum = sem("s_wsum")
        s_blk = sem("s_blk")
        s_built = sem("s_built")
        s_abs = sem("s_abs")
        s_bn = sem("s_bn")
        s_stat = sem("s_stat")
        s_pl = sem("s_pl")
        s_rstd = sem("s_rstd")
        s_biased = sem("s_biased")
        s_xn = sem("s_xn")
        s_xh = sem("s_xh")
        s_xl = sem("s_xl")
        s_th, s_tl = sem("s_th"), sem("s_tl")
        s_xth, s_xtl = sem("s_xth"), sem("s_xtl")
        s_mm = sem("s_mm")
        s_mmread = sem("s_mmread")
        s_xstore = sem("s_xstore")
        s_mask = sem("s_mask")
        s_cum = sem("s_cum")
        s_gd = sem("s_gd")
        s_ex = sem("s_ex")
        s_ohr = sem("s_ohr")
        s_tok = sem("s_tok")
        s_toki = sem("s_toki")
        s_wst = [sem(f"s_wst{i}") for i in range(4)]
        s_wh = sem("s_wh")
        s_wl = sem("s_wl")
        s_g = [sem("s_gx0"), sem("s_gx1")]
        s_gth, s_gtl = sem("s_gth"), sem("s_gtl")
        s_gch, s_gcl = sem("s_gch"), sem("s_gcl")
        s_g1 = sem("s_g1")
        s_g1r = sem("s_g1r")
        s_hh = sem("s_hh")
        s_hl = sem("s_hl")
        s_g2 = sem("s_g2")
        s_g2r = sem("s_g2r")
        s_b2 = sem("s_b2")
        s_eout = [sem("s_eout0"), sem("s_eout1")]
        s_back = [sem(f"s_back{i}") for i in range(4)]
        s_mix = sem("s_mix")
        s_gn = [sem("s_gn0"), sem("s_gn1")]
        s_gnh, s_gnl = sem("s_gnh"), sem("s_gnl")
        s_wtp = sem("s_wtp")
        s_wth, s_wtl = sem("s_wth"), sem("s_wtl")
        s_deg = sem("s_deg")
        s_degp = sem("s_degp")
        s_dinv = sem("s_dinv")
        s_dinv2 = sem("s_dinv2")
        s_hsh, s_hsl = sem("s_hsh"), sem("s_hsl")
        s_agg = sem("s_agg")
        s_aggread = sem("s_aggread")
        s_swp = sem("s_swp")
        s_swm = sem("s_swm")
        s_fn = [sem(f"s_fn{i}") for i in range(4)]
        s_fneg = sem("s_fneg")
        s_fq = sem("s_fq")
        s_ft = sem("s_ft")
        s_fc = sem("s_fc")
        s_dq = sem("s_dq")
        s_xq = sem("s_xq")
        s_xqt = sem("s_xqt")
        s_xqc = sem("s_xqc")
        s_f1 = sem("s_f1")
        s_ge = sem("s_ge")
        s_hq = sem("s_hq")
        s_hqt = sem("s_hqt")
        s_hqc = sem("s_hqc")
        s_f2 = sem("s_f2")
        s_f2r = sem("s_f2r")
        s_out = [sem("s_out0"), sem("s_out1")]

        s_held = sem("s_held")

        block = ctx.enter_context(nc.Block())

        R_GNN0, R_MOE, R_LIN1 = 0, NT, 2 * NT

        def parts(n, u):
            if isinstance(n, int) and R_MOE <= n < R_LIN1:
                return xs_all[:, n - R_MOE, 0:D], xs_all[:, n - R_MOE, D:2 * D]
            return xh[:, u, :], xl[:, u, :]

        def last_of(i, n, k=1):
            return isinstance(i, int) and i >= n - k

        def hold(eng):
            eng.sem_inc(s_held, 1)

        def pairs(eng, body, n=NT, peeled=2):
            if peeled < n:
                with eng.Fori(0, (n - peeled) // 2) as j:
                    for u in range(2):
                        body(2 * j + u, u)
            for i in range(n - peeled, n):
                body(i, i % 2)

        @block.sync
        def _(sp):
            for u in range(2):
                sp.sem_inc(s_eout[u], 16)
                sp.sem_inc(s_out[u], 16)
            sp.wait_ge(s_pad, 3)
            full, rest = CH - 1 - 2 * P, E_EDGES - (CH - 1) * P
            for v, edge in enumerate((src_in, dst_in, ew_in)):
                nat = nat_w[:, :, :] if v == 2 else nat_i[:, v, :, :]
                sp.dma_start(nat[:, 0:2, :], edge[0:2 * P * P].rearrange("(a q p) -> q a p", a=2, p=P)).then_inc(s_edges, 16)
                sp.dma_start(nat[0:full, 2, :], edge[2 * P * P:(CH - 1) * P].rearrange("(q p) -> q p", p=P)).then_inc(s_edges, 16)
                sp.dma_start(nat[full:full + 1, 2, 0:rest],
                             edge[(CH - 1) * P:E_EDGES].rearrange("(q p) -> q p", q=1)).then_inc(s_edges, 16)
            sp.wait_ge(s_const, 1)
            sp.dma_start(x[:, 0:NT - 1, :], x_in[0:(NT - 1) * P, :].rearrange("(t p) d -> p t d", p=P)).then_inc(s_x, 16)
            sp.dma_start(x[0:LAST, NT - 1, :], x_in[(NT - 1) * P:N, :]).then_inc(s_x, 16)
            sp.dma_start(bias_b[:, :], bias0_in.partition_broadcast(P)).then_inc(s_bias, 16)
            with nc.allow_non_contiguous_dma(reason="4096 words, once"):
                sp.dma_start(b1c[:, :, :], b1_in.rearrange("e (h p) -> p e h", p=P)).then_inc(s_b1, 16)
            sp.dma_start(wg32[:, :, :], wg_in.rearrange("(k p) e -> p k e", p=P)).then_inc(s_wg, 16)

            sp.wait_ge(s_rows, 1)
            for m, w in enumerate((f1_in, f2_in)):
                pieces = w.rearrange("a b -> (a b)").rearrange("(n p c) -> n p c", p=P, c=2048)
                with sp.Fori(0, 8) as j:
                    for u in range(2):
                        sp.wait_ge(s_abs, 16 * m + 2 * j + u + 1)
                        sp.dma_start(abs_in[:, u, :], pieces[2 * j + u]).then_inc(s_absin[u], 16)

            w1v = w1_in.rearrange("e (g k p) h -> e g p k h", g=2, p=P)
            w2v = w2_in.rearrange("e (g k p) d -> e g p k d", g=2, p=P)

            def expert_piece(e, q):
                piece = w1v[e, q] if q < 2 else w2v[e, q - 2]
                sp.dma_start(wstage[:, q, :].rearrange("p (k h) -> p k h", k=4 if q < 2 else 2), piece).then_inc(s_wst[q], 16)

            sp.wait_ge(s_mm, 1 + NT)
            for q in range(4):
                expert_piece(0, q)

            rows_d = xs_d.rearrange("(t p) c -> t p c", p=P)

            for i in range(NT):
                sp.wait_ge(s_xh, R_MOE + i + 1)
                sp.wait_ge(s_xl, R_MOE + i + 1)
                sp.dma_start(rows_d[i], xs_all[:, i, :]).then_inc(s_xstore, 16)

            sp.wait_ge(s_toki, 1)
            sp.wait_ge(s_xstore, 16 * NT)
            sp.dma_start(b2b[:, :], b2_in[0].partition_broadcast(P)).then_inc(s_b2, 16)
            expert_rows = eo_d.rearrange("(e s) d -> e s d", e=NE)

            def expert(e, ep):
                if not last_of(e, NE):
                    for q in range(4):
                        sp.wait_ge(s_wl, 4 * e + q + 1)
                        expert_piece(e + 1, q)
                for s in range(3):
                    u = (ep + s) % 2
                    sp.wait_ge(s_g2r, 3 + 6 * e + 2 * s + 2)
                    sp.dma_start(expert_rows[e][s * P:s * P + SM[s], :], eo[0:SM[s], u, :]).then_inc(s_eout[u], 16)
                if not last_of(e, NE):
                    sp.dma_start(b2b[:, :], b2_in[e + 1].partition_broadcast(P)).then_inc(s_b2, 16)

            pairs(sp, expert, NE)

            sp.dma_start(bias_b[:, :], gb_in.partition_broadcast(P)).then_inc(s_bias, 16)
            w1rows = gw_in.rearrange("(t p) d -> t p d", p=P)

            def w1_rows(i, u):
                sp.wait_ge(s_gnl, i + 1)
                sp.dma_start(gnat[:, u, :], w1rows[i]).then_inc(s_gn[u], 16)

            pairs(sp, w1_rows, KD)

            sp.wait_ge(s_mix, 2 * NT)
            sp.wait_ge(s_mmread, 2 + R_LIN1 + NT)
            f1v = f1_in.rearrange("(j u p) d -> j u p d", p=P, u=4)
            f2v = f2_in.rearrange("(j u p) (b d) -> b j u p d", p=P, u=4, b=4)
            with sp.Fori(0, KD) as j:
                for u in range(4):
                    sp.wait_ge(s_fq, 4 * j + u + 1)
                    sp.dma_start(fnat[u], f1v[j, u]).then_inc(s_fn[u], 16)
            for b in range(4):
                with sp.Fori(0, 2) as j:
                    for u in range(4):
                        sp.wait_ge(s_fq, 32 + 8 * b + 4 * j + u + 1)
                        sp.dma_start(fnat[u], f2v[b, j, u]).then_inc(s_fn[u], 16)

            res = out[0:(NT - 1) * P, :].rearrange("(t p) d -> t p d", p=P)

            def result(i, u):
                sp.wait_ge(s_f2r, i + 1)
                if last_of(i, NT):
                    sp.dma_start(out[(NT - 1) * P:N, :], out_t[0:LAST, u, :]).then_inc(s_out[u], 16)
                else:
                    sp.dma_start(res[i], out_t[:, u, :]).then_inc(s_out[u], 16)

            pairs(sp, result)
            for u in range(2):
                sp.wait_ge(s_eout[u], 16 + 16 * 3 * NE // 2)
                sp.wait_ge(s_out[u], 16 + 16 * NT // 2)

        @block.gpsimd
        def _(pool):
            g = nc.gpsimd
            ok = dict(allow_small_or_imprecise_dtypes=True)
            g.memset(x[:, NT - 1, :], 0.0).then_inc(s_const, 1)
            for k, v in enumerate((LN_EPS, -0.5, SX, 1.0)):
                g.memset(consts[:, k:k + 1], v).then_inc(s_const, 1)
            g.memset(zero16[:, :], 0.0).then_inc(s_const, 1)
            g.memset(ones16[:, :], 1.0).then_inc(s_const, 1)
            g.memset(ones32[:, :], 1.0).then_inc(s_const, 1)
            g.iota(iota_r[:, :], [[1, NP]], base=0, channel_multiplier=0, **ok).then_inc(s_const, 1)
            g.iota(q_iota[:, :], [[1, CHP]], base=0, channel_multiplier=0, **ok).then_inc(s_const, 1)
            g.iota(j_iota[:, 0:NG_MAX], [[G, NG_MAX]], base=G, channel_multiplier=0, **ok).then_inc(s_const, 1)
            for k in range(2):
                g.iota(w_lo[:, k:k + 1], [[1, 1]], base=(WIN - 1) * k, channel_multiplier=WIN, **ok).then_inc(s_const, 1)
            pool.wait_ge(s_const, 13)
            g.affine_select(out=id16[:, :], in_=ones16[:, :], pattern=[[-1, P]], compare_op=ALU.is_equal,
                            fill=0.0, base=0, channel_multiplier=1).then_inc(s_const, 1)
            g.affine_select(out=id32[:, :], in_=ones32[:, :], pattern=[[-1, P]], compare_op=ALU.is_equal,
                            fill=0.0, base=0, channel_multiplier=1).then_inc(s_const, 1)
            g.affine_select(out=tri[:, :], in_=ones16[:, :], pattern=[[1, P]], compare_op=ALU.is_ge,
                            fill=0.0, base=0, channel_multiplier=-1).then_inc(s_const, 1)

            def rstd_tile(r, i, k):
                n = NT * r + i
                one = bass.ds(i, 1)
                pool.wait_ge(s_stat, n + 1)
                g.tensor_tensor(rtmp[:, 0:1], mv[:, one, 1], consts[:, 0:1], ALU.add).then_inc(s_pl, 1)
                pool.wait_ge(s_pl, 2 * n + 1)
                g.tensor_tensor(rtmp[:, 1:2], rtmp[:, 0:1], consts[:, 1:2], ALU.pow).then_inc(s_pl, 1)
                pool.wait_ge(s_pl, 2 * n + 2)
                g.tensor_tensor(rstd[:, one], rtmp[:, 1:2], consts[:, k:k + 1], ALU.mult).then_inc(s_rstd, 1)

            with pool.Fori(0, NT) as i:
                rstd_tile(0, i, 2)

            pool.wait_ge(s_rows, 1)
            with pool.register("pool_chunks") as chunks, pool.register("pool_first") as first:
                pool.reg_mov(chunks, 0)

                def window(w):
                    pool.reg_load(first, rows_i[0:1, 0, bass.ds(w, 1)])
                    groups = pool.value_load(rows_i[0:1, 1, bass.ds(w, 1)], min_val=1, max_val=NG_MAX)
                    with pool.Fori(0, groups):
                        n = pool.snap(chunks, min_val=0, max_val=1 << 20)
                        at = pool.snap(first, min_val=0, max_val=CHP - G)
                        for half in range(2):
                            five = bass.ds(at + 5 * half, RING)
                            st = st_e[:, half, :, :]
                            pool.wait_ge(s_onehot, n + 5 * half + 5)
                            g.tensor_tensor(st[:, :, WIN:2 * WIN], st[:, :, 0:WIN],
                                            ewh_t[:, five].unsqueeze(2).to_broadcast([P, RING, WIN]), ALU.mult)
                            g.tensor_tensor(st[:, :, 2 * WIN:3 * WIN], st[:, :, 0:WIN],
                                            ewl_t[:, five].unsqueeze(2).to_broadcast([P, RING, WIN]),
                                            ALU.mult).then_inc(s_st, 5)
                        pool.reg_add(chunks, chunks, G)
                        pool.reg_add(first, first, G)

                def weight_sums(b, ub):
                    pool.wait_ge(s_stage, 12 * b + 12)
                    g.tensor_tensor(st_wh[:, ub, :], st_wh[:, ub, :], st_wl[:, ub, :], ALU.add).then_inc(s_wsum, 1)

                def count_rest(b, ub):
                    pool.wait_ge(s_ath, b + 1)
                    pool.wait_ge(s_built, 2 + b)
                    hold(pool)
                    g.tensor_tensor(at_lo16[:, :], st_a[:, ub, :], at_h[:, b, :], ALU.subtract).then_inc(s_atlo, 1)

                for w in range(3):
                    window(w)
                with pool.Fori(0, 4) as bb:
                    for k in range(3, 11):
                        window(8 * bb + k)
                        if k % 4 == 1:
                            weight_sums(2 * bb + (k - 5) // 4, (k - 5) // 4)
                        if k % 4 == 2:
                            count_rest(2 * bb + (k - 6) // 4, (k - 6) // 4)
                for w in range(35, NW):
                    window(w)
                    if w == 37:
                        weight_sums(NT - 2, 0)
                    if w == 38:
                        count_rest(NT - 2, 0)
                weight_sums(NT - 1, 1)
                count_rest(NT - 1, 1)

            pool.wait_ge(s_bias, 16)
            with pool.Fori(0, NT) as i:
                pool.wait_ge(s_xn, R_GNN0 + i + 1)
                g.tensor_tensor(x[:, i, :], x[:, i, :], bias_b[:, :], ALU.add).then_inc(s_biased, 1)
            with pool.Fori(0, NT) as i:
                rstd_tile(1, i, 2)

            pool.wait_ge(s_mm, 1 + NT)
            g.iota(iota_lo[:, :], [[1, P]], base=0, channel_multiplier=0, **ok).then_inc(s_const, 1)
            g.iota(tok_f[:, :], [[0, 2], [P, NT]], base=0, channel_multiplier=1, **ok).then_inc(s_const, 1)
            g.memset(valid_m[:, :, :, :], 1.0).then_inc(s_const, 1)
            g.memset(scan_m[:, :, :], 1.0).then_inc(s_const, 1)
            pool.wait_ge(s_const, 20)
            for k in range(2):
                g.affine_select(out=valid_m[:, k, NT - 1, :], in_=valid_m[:, k, NT - 1, :],
                                pattern=[[0, NE]], compare_op=ALU.is_ge, fill=0.0, base=LAST - 1,
                                channel_multiplier=-1).then_inc(s_const, 1)
            g.memset(scan_m[:, :, 0:1], 0.0).then_inc(s_const, 1)

            pool.wait_ge(s_toki, 1)
            pool.wait_ge(s_xstore, 16 * NT)
            for n in range(3 * NE):
                m = SM[n % 3]
                if n >= 2:
                    pool.wait_ge(s_gtl, n - 1)
                pool.indirect_dma_start(out=gx[0:m, n % 2, :], out_offset=None, in_=xs_d[:, :],
                                        in_offset=bass.IndirectOffsetOnAxis(ap=tok_i[0:m, n:n + 1], axis=0)
                                        ).then_inc(s_g[n % 2], 16)
            for u in range(2):
                pool.wait_ge(s_eout[u], 16 + 16 * 3 * NE // 2)
            for n in range(2 * NT):
                col = (n % 2) * NT + n // 2
                if n >= 4:
                    pool.wait_ge(s_mix, n - 3)
                pool.indirect_dma_start(out=back[n % 4], out_offset=None, in_=eo_d[:, :],
                                        in_offset=bass.IndirectOffsetOnAxis(ap=slot_i[:, col:col + 1], axis=0)
                                        ).then_inc(s_back[n % 4], 16)
                if n == 3:
                    pool.wait_ge(s_degp, 1)
                    g.tensor_tensor(dinv[:, 0, :], dinv[:, 1, :], consts[:, 1:2].to_broadcast([P, NT]), ALU.pow).then_inc(s_dinv, 1)
                if n % 2 == 1 and n >= 3:
                    rstd_tile(2, n // 2 - 1, 2)
            rstd_tile(2, NT - 1, 2)
            with pool.Fori(0, NT) as i:
                rstd_tile(3, i, 3)

        @block.tensor
        def _(pe):
            mm, tr = nc.tensor.matmul, nc.tensor.transpose
            pe.sem_inc(s_chunk, 10)
            pe.sem_inc(s_mm, 1)
            pe.sem_inc(s_g2, 1)
            pe.sem_inc(s_wtp, 2)
            pe.sem_inc(s_ft, 2)

            pe.wait_ge(s_const, 16)
            pe.wait_ge(s_natf, 2)
            pe.wait_ge(s_edges, 16 * 9)
            for v in range(3):
                for a in range(3):
                    last = tr(ps[:, v, a * P:(a + 1) * P], nat_w[:, a, :] if v == 2 else nat_f[:, v, a, :], id32[:, :])
            last.then_inc(s_et, 1)
            pe.wait_ge(s_cmb, 1)
            for v in range(2):
                for a in range(3):
                    last = mm(ps[0:48, 3 + v, a * P:(a + 1) * P], cmb[:, 3 * v + a, :], id16[:, :], start=True, stop=True)
            last.then_inc(s_cmw, 1)
            pe.wait_ge(s_kk, 1)
            for v in range(2):
                last = mm(ps[0:1, 5, 48 * v:48 * v + 48], kk16[:, v:v + 1], id16[0:48, 0:48], start=True, stop=True)
            last.then_inc(s_kr, 1)
            pe.wait_ge(s_rows, 1)

            with pe.register("pe_chunks") as chunks:
                pe.reg_mov(chunks, 0)

                def window(w, u):
                    groups = pe.value_load(rows_i[0:1, 1, bass.ds(w, 1)], min_val=1, max_val=NG_MAX)
                    pe.wait_ge(s_winread, w + 1)
                    for r in range(3):
                        mm(ps[0:96, 3 * u + r, 0:2], zero16[:, :], zero16[:, 0:2], start=True, stop=False,
                           skip_group_check=True)
                    with pe.Fori(0, groups):
                        n = pe.snap(chunks, min_val=0, max_val=1 << 20)
                        for half in range(2):
                            pe.wait_ge(s_st, n + 5 * half + 5)
                            for c in range(RING):
                                pe.wait_ge(s_oh, n + 5 * half + c + 1)
                                for r in range(3):
                                    cols = slice(512 * r, min(512 * r + 512, NP))
                                    last = mm(ps[0:96, 3 * u + r, 0:cols.stop - cols.start], st_e[:, half, c, :],
                                              oh[:, c, cols], start=False, stop=False, skip_group_check=True)
                                last.then_inc(s_chunk, 1)
                        pe.reg_add(chunks, chunks, G)
                    for r in range(3):
                        last = mm(ps[0:96, 3 * u + r, 0:2], zero16[:, :], zero16[:, 0:2], start=False, stop=True,
                                  skip_group_check=True)
                    last.then_inc(s_win, 1)

                window(0, 0)
                with pe.Fori(0, NW // 8 - 1) as bb:
                    for v in range(1, 9):
                        window(8 * bb + v, v % 2)
                for w in range(NW - 7, NW):
                    window(w, w % 2)

            def transposes(n, u):
                hi, lo = parts(n, u)
                pe.wait_ge(s_xh, n + 1)
                if not isinstance(n, int) or n > 0:
                    pe.wait_ge(s_xth, n)
                for k in range(KD):
                    last = tr(bank16(4)[:, k * P:(k + 1) * P], hi[:, k * P:(k + 1) * P], id16[:, :])
                last.then_inc(s_th, 1)
                pe.wait_ge(s_xl, n + 1)
                if not isinstance(n, int) or n > 0:
                    pe.wait_ge(s_xtl, n)
                for k in range(KD):
                    last = tr(bank16(5)[:, k * P:(k + 1) * P], lo[:, k * P:(k + 1) * P], id16[:, :])
                last.then_inc(s_tl, 1)

            def product(n, u, rh, rl):
                pe.wait_ge(s_xth, n + 1)
                pe.wait_ge(s_xtl, n + 1)
                pe.wait_ge(s_mmread, n + 1)
                for k in range(KD):
                    for a, (lhs, rhs) in enumerate(((xth, rh), (xth, rl), (xtl, rh))):
                        for h in range(2):
                            last = mm(ps[:, 2 * u + h, :], lhs[:, u, k, :], rhs[:, k, h * 512:(h + 1) * 512],
                                      start=(k == 0 and a == 0), stop=(k == KD - 1 and a == 2))
                last.then_inc(s_mm, 1)

            def normalised(r, body, peeled=2):
                transposes(r, 0)

                def step(i, u):
                    if not last_of(i, NT):
                        transposes(r + i + 1, 1 - u)
                    body(i, u)

                pairs(pe, step, peeled=peeled)

            pe.wait_ge(s_winread, 2 + NW)
            pe.wait_ge(s_built, 2 + NT)
            normalised(R_GNN0, lambda i, u: product(R_GNN0 + i, u, wt_h, wt_l))

            pe.wait_ge(s_small, 2)

            def logits_of(i, u):
                n = R_MOE + i
                pe.wait_ge(s_xth, n + 1)
                pe.wait_ge(s_xtl, n + 1)
                pe.wait_ge(s_mmread, n + 1)
                for k in range(KD):
                    for a, lhs in enumerate((xth, xtl)):
                        last = mm(ps[:, 6 + u, 0:2 * NE], lhs[:, u, k, :], wgs[:, k, :],
                                  start=(k == 0 and a == 0), stop=(k == KD - 1 and a == 1))
                last.then_inc(s_mm, 1)

            normalised(R_MOE, logits_of, peeled=NT)
            pe.wait_ge(s_mask, 1)
            masks = mask[:, :, :, :].rearrange("p k t e -> p (k t e)")
            mm(ps[:, 0, 0:2 * NT * NE], tri[:, :], masks, start=True, stop=True)
            mm(ps[:, 1, 0:2 * NT * NE], ones16[:, :], masks, start=True, stop=True).then_inc(s_cum, 1)
            pe.wait_ge(s_ohr, 1)
            for n in range(2 * NT):
                last = mm(ps[:, 2, 0:3 * NE], oh_lo[:, n, :], oh_hi2[:, n, :], start=(n == 0), stop=(n == 2 * NT - 1))
            last.then_inc(s_tok, 1)
            pe.wait_ge(s_toki, 1)

            def gathered(e, ep):
                for s in range(3):
                    m, n, u = SM[s], 3 * e + s, (ep + s) % 2
                    pe.wait_ge(s_g[u], 8 * n - 8 * u + 16)
                    for part, (b, read, done) in enumerate(((4, s_gch, s_gth), (5, s_gcl, s_gtl))):
                        pe.wait_ge(read, n + 1)
                        hold(pe)
                        for k in range(KD):
                            c = part * D + k * P
                            last = tr(bank16(b)[:, k * P:k * P + m], gx[0:m, u, c:c + P], id16[0:m, 0:m])
                        last.then_inc(done, 1)

            def expert(e, ep):
                pe.wait_ge(s_gch, 1 + 3 * e + 3)
                pe.wait_ge(s_gcl, 1 + 3 * e + 3)
                pe.wait_ge(s_wl, 4 * e + 2)
                for hb in range(KH):
                    pe.wait_ge(s_g1r, 4 * e + hb + 1)
                    for k in range(KD):
                        for a, (lhs, rhs) in enumerate(((w1h, xdh), (w1h, xdl), (w1l, xdh))):
                            last = mm(ps[:, 6 + hb % 2, 0:CAP], lhs[:, k, hb * P:(hb + 1) * P], rhs[:, k, :],
                                      start=(k == 0 and a == 0), stop=(k == KD - 1 and a == 2))
                    last.then_inc(s_g1, 1)
                if not last_of(e, NE):
                    gathered(e + 1, 1 - ep)
                pe.wait_ge(s_hl, 2 + 4 * e + 4)
                pe.wait_ge(s_wl, 4 * e + 4)
                for s in range(3):
                    m = SM[s]
                    for h in range(2):
                        pe.wait_ge(s_g2r, 6 * e + 2 * s + h + 1)
                        for k in range(KH):
                            for a, (lhs, rhs) in enumerate(((hth, w2h), (hth, w2l), (htl, w2h))):
                                last = mm(ps[0:m, (2 * s + h) % 3, :], lhs[:, k, s * P:s * P + m],
                                          rhs[:, k, h * 512:(h + 1) * 512],
                                          start=(k == 0 and a == 0), stop=(k == KH - 1 and a == 2))
                        last.then_inc(s_g2, 1)

            gathered(0, 0)
            pairs(pe, expert, NE)

            def w1_t(i, u):
                pe.wait_ge(s_gnh, i + 1)
                pe.wait_ge(s_wth, i + 1)
                for k in range(KD):
                    tr(bank16(4)[:, k * P:(k + 1) * P], gnh[:, u, k * P:(k + 1) * P], id16[:, :])
                pe.wait_ge(s_gnl, 2 + i + 1)
                pe.wait_ge(s_wtl, i + 1)
                for k in range(KD):
                    last = tr(bank16(5)[:, k * P:(k + 1) * P], gnl[:, u, k * P:(k + 1) * P], id16[:, :])
                last.then_inc(s_wtp, 1)

            pairs(pe, w1_t, KD)
            for i in range(NT):
                for b in range(NT):
                    for a, t in enumerate((at_h, at_l)):
                        last = mm(ps[:, 6, i:i + 1], t[:, b, i * P:(i + 1) * P], ones16[:, 0:1],
                                  start=(b == 0 and a == 0), stop=(b == NT - 1 and a == 1))
            last.then_inc(s_deg, 1)
            pe.wait_ge(s_swp, 1)
            mm(ps[:, 7, 0:2], ones32[:, :], sw[:, 0:2], start=True, stop=True).then_inc(s_swm, 1)
            pe.wait_ge(s_wth, 1 + KD)
            pe.wait_ge(s_wtl, 1 + KD)
            normalised(R_LIN1, lambda i, u: product(R_LIN1 + i, u, gwt_h, gwt_l))

            pe.wait_ge(s_hsh, NT)
            pe.wait_ge(s_hsl, 1 + NT)

            def weight_piece(n):
                pe.wait_ge(s_fq, 4 + n + 1)
                pe.wait_ge(s_fc, n + 1)
                for k in range(KD):
                    last = tr(bank16(4 + n % 4)[:, k * P:(k + 1) * P], fq[:, n % 2, k * P:(k + 1) * P], id16[:, :])
                last.then_inc(s_ft, 1)

            for i in range(NT):
                u = i % 2
                pe.wait_ge(s_aggread, i + 1)
                for a, rhs in enumerate((hs_h, hs_l)):
                    for h in range(2):
                        mm(ps[:, 2 * u + h, :], id16[:, :], rhs[:, i, h * 512:(h + 1) * 512], start=(a == 0), stop=False)
                for b in range(NT):
                    for a, (lhs, rhs) in enumerate(((at_h, hs_h), (at_h, hs_l), (at_l, hs_h))):
                        for h in range(2):
                            last = mm(ps[:, 2 * u + h, :], lhs[:, b, i * P:(i + 1) * P], rhs[:, b, h * 512:(h + 1) * 512],
                                      start=False, stop=(b == NT - 1 and a == 2))
                    if i < 8 and b >= 2:
                        weight_piece(8 * i + b - 2)
                last.then_inc(s_agg, 1)

            def ffn_in(i, u):
                pe.wait_ge(s_xq, i + 1)
                for k in range(KD):
                    last = tr(bank16(6)[:, k * P:(k + 1) * P], xq[:, u, k * P:(k + 1) * P], id16[:, :])
                last.then_inc(s_xqt, 1)
                pe.wait_ge(s_xqc, i + 1)
                for n in range(8):
                    pe.wait_ge(s_ge, 8 * i + n + 1)
                    hold(pe)
                    for k in range(KD):
                        last = mm(ps[:, n % 4, :], xqt[:, u, k, :], w1q[:, k, n * 512:(n + 1) * 512],
                                  start=(k == 0), stop=(k == KD - 1))
                    last.then_inc(s_f1, 1)

            def ffn_out(i):
                def hidden_t(q):
                    for k in range(KD):
                        last = tr(bank16(7 - q % 2)[:, k * P:(k + 1) * P], hq[:, (8 * q + k) * P:(8 * q + k + 1) * P], id16[:, :])
                    last.then_inc(s_hqt, 1)

                pe.wait_ge(s_hq, 2 + i + 1)
                hidden_t(0)
                hidden_t(1)
                if not isinstance(i, int) or i > 0:
                    pe.wait_ge(s_f2r, i)
                for q in range(4):
                    pe.wait_ge(s_hqc, 4 * i + q + 1)
                    hold(pe)
                    if 1 <= q <= 2:
                        hidden_t(q + 1)
                    for k in range(8 * q, 8 * q + 8):
                        for h in range(2):
                            last = mm(ps[:, 4 + h, :], hqt[:, k, :], w2q[:, k, h * 512:(h + 1) * 512],
                                      start=(k == 0), stop=(k == KF - 1))
                last.then_inc(s_f2, 1)

            pe.wait_ge(s_fc, 4 + 64)
            pe.wait_ge(s_aggread, 2 + NT)
            ffn_in(0, 0)
            ffn_in(1, 1)
            ffn_out(0)

            def ffn(i, u):
                ffn_in(i + 1, 1 - u)
                ffn_out(i)

            with pe.Fori(0, NT // 2 - 1) as j:
                ffn(2 * j + 1, 1)
                ffn(2 * j + 2, 0)
            ffn_out(NT - 1)

        @block.scalar
        def _(act):
            cp = nc.scalar.activation
            act.sem_inc(s_winread, 2)
            act.sem_inc(s_abs, 2)
            act.sem_inc(s_gch, 1)
            act.sem_inc(s_g1r, 2)
            act.sem_inc(s_wth, 1)
            act.sem_inc(s_fc, 4)
            act.sem_inc(s_ge, 4)

            def window(w, u, j, blk, ub):
                act.wait_ge(s_win, w + 1)
                act.wait_ge(s_built, blk + 1)
                rows = slice(WIN * j, WIN * j + WIN)
                pw = ps[:, 3 * u:3 * u + 3, :].rearrange("p b c -> p (b c)")
                cp(st_a[rows, ub, :], pw[0:32, 0:NP], ACT.Copy).then_inc(s_stage, 1)
                cp(st_wh[rows, ub, :], pw[32:64, 0:D], ACT.Copy).then_inc(s_stage, 1)
                cp(st_wl[rows, ub, :], pw[64:96, 0:D], ACT.Copy).then_inc(s_stage, 1)
                act.wait_ge(s_stage, 3 * w + 3)
                act.sem_inc(s_winread, 1)

            def abs_piece(n, u):
                act.wait_ge(s_absin[u], 8 * n - 8 * u + 16)
                hold(act)
                cp(abs_in[:, u, :], abs_in[:, u, :], ACT.Abs, accum_out=abs_acc[:, bass.ds(n, 1)]).then_inc(s_abs, 1)

            def counts_high(b, ub):
                hold(act)
                cp(at_h[:, b, :] if isinstance(b, int) else at_flat[:, bass.ds(b * NP, NP)], st_a[:, ub, :],
                   ACT.Copy).then_inc(s_ath, 1)

            def weights_high(b, ub):
                act.wait_ge(s_wsum, b + 1)
                hold(act)
                cp(wt_h[:, b, :] if isinstance(b, int) else wt_flat[:, bass.ds(b * D, D)], st_wh[:, ub, :],
                   ACT.Copy).then_inc(s_wtb, 1)

            at_flat = at_h[:, :, :].rearrange("p t c -> p (t c)")
            wt_flat = wt_h[:, :, :].rearrange("p t d -> p (t d)")
            for w in range(3):
                window(w, w % 2, w, 0, 0)
            with act.Fori(0, 4) as bb:
                for k in range(3, 11):
                    window(8 * bb + k, k % 2, k % 4, 2 * bb + k // 4, (k // 4) % 2)
                    if k % 4 == 3:
                        counts_high(2 * bb + (k - 3) // 4, (k - 3) // 4)
                    if k % 4 == 2:
                        weights_high(2 * bb + (k - 6) // 4, (k - 6) // 4)
                    if k in (4, 5, 8, 9):
                        abs_piece(4 * bb + (k - 4) // 2 + k % 2, k % 2)
            for w in range(35, NW):
                window(w, w % 2, w % 4, w // 4, (w // 4) % 2)
                if w % 4 == 3:
                    counts_high(w // 4, (w // 4) % 2)
                if w == 38:
                    weights_high(NT - 2, 0)
            weights_high(NT - 1, 1)

            def high(n, u):
                act.wait_ge(s_xn, n + 1)
                cp(parts(n, u)[0], xn[:, u, :], ACT.Copy).then_inc(s_xh, 1)

            def copy_high(n, u):
                act.wait_ge(s_th, n + 1)
                cp(xth[:, u, :, :].rearrange("p k c -> p (k c)"), bank16(4), ACT.Copy).then_inc(s_xth, 1)

            def normalised(r, body):
                high(r, 0)
                high(r + 1, 1)
                copy_high(r, 0)

                def step(i, u):
                    if not last_of(i, NT):
                        act.wait_ge(s_mm, r + i + 1)
                        copy_high(r + i + 1, 1 - u)
                    if not last_of(i, NT, 2):
                        act.wait_ge(s_tl, r + i + 1)
                        high(r + i + 2, u)
                    body(i, u)

                pairs(act, step)

            act.wait_ge(s_built, 2 + NT)

            def gnn0(i, u):
                if not last_of(i, NT, 2):
                    for k in range(2):
                        abs_piece(16 + 2 * i + k, k)

            normalised(R_GNN0, gnn0)
            act.wait_ge(s_tl, R_MOE)
            act.wait_ge(s_mm, 1 + R_MOE)
            for i in range(3):
                high(R_MOE + i, i % 2)
            copy_high(R_MOE, 0)
            for i in range(NT - 1):
                if i + 3 < NT:
                    high(R_MOE + i + 3, (i + 3) % 2)
                act.wait_ge(s_mm, R_MOE + i + 1)
                copy_high(R_MOE + i + 1, (i + 1) % 2)
            act.wait_ge(s_gd, 1)
            cp(rt[:, 1, 0:NT], rt[:, 0, 0:NT], ACT.Exp).then_inc(s_ex, 1)

            b1s = b1c[:, :, :].rearrange("p e h -> p (e h)")

            def split_high(e, q):
                act.wait_ge(s_wst[q], 16 * e + 16)
                w = w1h[:, 4 * q:4 * q + 4, :] if q < 2 else w2h[:, 2 * q - 4:2 * q - 2, :]
                cp(w.rearrange("p k h -> p (k h)"), wstage[:, q, :], ACT.Copy, scale=SW).then_inc(s_wh, 1)

            def gathered(e):
                for s in range(3):
                    m = SM[s]
                    act.wait_ge(s_gth, 3 * e + s + 1)
                    cp(xdh[:, :, s * P:s * P + m], bank16(4).rearrange("p (k c) -> p k c", k=KD)[:, :, 0:m],
                       ACT.Copy).then_inc(s_gch, 1)

            def expert(e, ep):
                for hb in range(KH):
                    act.wait_ge(s_g1, 4 * e + hb + 1)
                    act.wait_ge(s_hl, 4 * e + hb + 1)
                    if hb == 0:
                        act.wait_ge(s_g2, 6 * e + 1)
                    cp(ht32[:, hb % 2, :], ps[:, 6 + hb % 2, 0:CAP], ACT.Relu, bias=b1s[:, bass.ds(4 * e + hb, 1)],
                       scale=SH / (SX * SW)).then_inc(s_g1r, 1)
                    act.wait_ge(s_g1r, 2 + 4 * e + hb + 1)
                    cp(hth[:, hb, :], ht32[:, hb % 2, :], ACT.Copy).then_inc(s_hh, 1)
                if not last_of(e, NE):
                    gathered(e + 1)
                    for q in range(2):
                        split_high(e + 1, q)
                    act.wait_ge(s_g2, 1 + 6 * e + 6)
                    for q in range(2, 4):
                        split_high(e + 1, q)

            for q in range(2):
                split_high(0, q)
            act.wait_ge(s_toki, 1)
            act.wait_ge(s_xstore, 16 * NT)
            act.wait_ge(s_small, 2)
            gathered(0)
            for q in range(2, 4):
                split_high(0, q)
            pairs(act, expert, NE)

            act.wait_ge(s_g2, 1 + 6 * NE)

            def w1_high(i, u):
                act.wait_ge(s_gn[u], 8 * i - 8 * u + 16)
                act.wait_ge(s_wtp, i + 1)
                cp(gnh[:, u, :], gnat[:, u, :], ACT.Copy, scale=SW).then_inc(s_gnh, 1)

            w1_high(0, 0)

            def w1_part(i, u):
                if not last_of(i, KD):
                    w1_high(i + 1, 1 - u)
                act.wait_ge(s_wtp, 2 + i + 1)
                cp(gwt_h[:, :, bass.ds(i * P, P)], bank16(4).rearrange("p (k c) -> p k c", k=KD), ACT.Copy).then_inc(s_wth, 1)

            pairs(act, w1_part, KD)

            def h_high(i, u):
                act.wait_ge(s_mmread, 2 + R_LIN1 + i + 1)
                flat = hs_h[:, :, :].rearrange("p t d -> p (t d)")
                cp(flat[:, bass.ds(i * D, D)], h32[:, :], ACT.Copy, scale=dinv[:, 1, bass.ds(i, 1)]).then_inc(s_hsh, 1)

            act.wait_ge(s_dinv2, 2)
            normalised(R_LIN1, h_high)

            act.wait_ge(s_mm, 1 + R_LIN1 + NT)
            act.wait_ge(s_hsl, 1 + NT)
            for n in range(64):
                act.wait_ge(s_ft, 2 + n + 1)
                if n < 32:
                    part = w1q[:, :, n * P:(n + 1) * P]
                else:
                    b, o = (n - 32) // 8, (n - 32) % 8
                    part = w2q[:, 8 * b:8 * b + 8, o * P:(o + 1) * P]
                cp(part, bank16(4 + n % 4).rearrange("p (k c) -> p k c", k=KD), ACT.Copy, saturate=False).then_inc(s_fc, 1)

            def ffn_in(i, u):
                act.wait_ge(s_xqt, i + 1)
                cp(xqt[:, u, :, :].rearrange("p k c -> p (k c)"), bank16(6), ACT.Copy).then_inc(s_xqc, 1)
                act.wait_ge(s_hq, i + 1)
                for n in range(8):
                    act.wait_ge(s_f1, 8 * i + n + 1)
                    cp(hf[:, u, n * 512:(n + 1) * 512], ps[:, n % 4, :], ACT.Gelu, scale=fs[:, u, 3:4]).then_inc(s_ge, 1)

            def ffn_out(i):
                for q in range(4):
                    act.wait_ge(s_hqt, 4 * i + q + 1)
                    cp(hqt[:, 8 * q:8 * q + 8, :].rearrange("p k c -> p (k c)"), bank16(7 - q % 2), ACT.Copy).then_inc(s_hqc, 1)

            act.wait_ge(s_fc, 4 + 64)
            act.wait_ge(s_agg, NT)
            ffn_in(0, 0)
            ffn_in(1, 1)
            ffn_out(0)
            with act.Fori(0, NT // 2 - 1) as j:
                ffn_in(2 * j + 2, 0)
                ffn_out(2 * j + 1)
                ffn_in(2 * j + 3, 1)
                ffn_out(2 * j + 2)
            ffn_out(NT - 1)

        @block.vector
        def _(dve):
            v = nc.vector
            steps = Steps(dve, s_dv)

            def do(ins):
                steps.inc(ins)
                steps.wait()

            dve.sem_inc(s_built, 2)
            dve.sem_inc(s_mmread, 2)
            dve.sem_inc(s_gcl, 1)
            dve.sem_inc(s_hl, 2)
            dve.sem_inc(s_g2r, 3)
            dve.sem_inc(s_gnl, 2)
            dve.sem_inc(s_hsl, 1)
            dve.sem_inc(s_wtl, 1)
            dve.sem_inc(s_aggread, 2)
            dve.sem_inc(s_fq, 4)
            dve.sem_inc(s_hq, 2)

            v.memset(nat_i[:, 0, 2, :], -1).then_inc(s_pad, 1)
            v.memset(nat_i[:, 1, 2, :], NP - 1).then_inc(s_pad, 1)
            v.memset(nat_w[:, 2, :], 0.0).then_inc(s_pad, 1)
            dve.wait_ge(s_edges, 16 * 9)
            for a in range(2):
                v.tensor_copy(nat_f[:, a, :, :], nat_i[:, a, :, :]).then_inc(s_natf, 1)
            dve.wait_ge(s_natf, 2)
            steps.inc(v.tensor_reduce(cm[:, 0, :], nat_f[:, 1, :, :], AX.X, ALU.min))
            do(v.tensor_reduce(cm[:, 1, :], nat_f[:, 1, :, :], AX.X, ALU.max))
            v.tensor_copy(cmb[:, :, :], cm[:, :, :].rearrange("p v a -> p (v a)").unsqueeze(2).to_broadcast([P, 6, 48])
                          ).then_inc(s_cmb, 1)
            dve.wait_ge(s_et, 1)
            steps.inc(v.tensor_copy(src_t[:, :], ps[:, 0, 0:CHP]))
            steps.inc(v.tensor_copy(dst_t[:, :], ps[:, 1, 0:CHP]))
            do(v.tensor_scalar(ew32_t[:, :], ps[:, 2, 0:CHP], SW, None, ALU.mult))
            do(v.tensor_copy(ewh_t[:, :], ew32_t[:, :]))
            do(v.tensor_tensor(ewl_t[:, :], ew32_t[:, :], ewh_t[:, :], ALU.subtract))
            dve.wait_ge(s_const, 16)
            dve.wait_ge(s_cmw, 1)
            do(v.tensor_scalar(ov[:, 0, 0:CH], ps[0:48, 4, 0:CH], w_lo[:, 0:1], None, ALU.is_ge))
            do(v.scalar_tensor_tensor(out=ov[:, 1, 0:CH], in0=ps[0:48, 3, 0:CH], scalar=w_lo[:, 1:2], in1=ov[:, 0, 0:CH],
                                      op0=ALU.is_le, op1=ALU.mult))
            do(v.scalar_tensor_tensor(out=ov[:, 0, 0:CH], in0=q_iota[:, 0:CH], scalar=-512.0, in1=ov[:, 1, 0:CH],
                                      op0=ALU.add, op1=ALU.mult))
            do(v.tensor_reduce(kk[:, 0:1], ov[:, 0, 0:CH], AX.X, ALU.min))
            do(v.tensor_scalar(kk[:, 1:2], kk[:, 0:1], 512.0, float(CH), ALU.add, ALU.min))
            do(v.scalar_tensor_tensor(out=ov[:, 0, 0:CH], in0=q_iota[:, 0:CH], scalar=1.0, in1=ov[:, 1, 0:CH],
                                      op0=ALU.add, op1=ALU.mult))
            do(v.tensor_reduce(kk[:, 2:3], ov[:, 0, 0:CH], AX.X, ALU.max))
            do(v.tensor_tensor(kk[:, 3:4], kk[:, 2:3], kk[:, 1:2], ALU.subtract))
            do(v.tensor_scalar(ov[:, 0, 0:NG_MAX], j_iota[:, 0:NG_MAX], kk[:, 3:4], None, ALU.is_lt))
            do(v.tensor_reduce(kk[:, 4:5], ov[:, 0, 0:NG_MAX], AX.X, ALU.add))
            steps.inc(v.tensor_copy(kk16[:, 0:1], kk[:, 1:2]))
            v.tensor_scalar(kk16[:, 1:2], kk[:, 4:5], 1.0, None, ALU.add).then_inc(s_kk, 1)
            dve.wait_ge(s_kr, 1)
            v.tensor_copy(rows_i[:, :, :].rearrange("p a w -> p (a w)"), ps[0:1, 5, 0:96]).then_inc(s_rows, 1)
            dve.wait_ge(s_rows, 1)

            dve.wait_ge(s_b1, 16)
            v.tensor_scalar(b1c[:, :, :], b1c[:, :, :], SH, None, ALU.mult).then_inc(s_small, 1)
            dve.wait_ge(s_wg, 16)
            do(v.tensor_scalar(wg32[:, :, :], wg32[:, :, :], SW, None, ALU.mult))
            do(v.tensor_copy(wgs[:, :, 0:NE], wg32[:, :, :]))
            v.tensor_tensor(wgs[:, :, NE:2 * NE], wg32[:, :, :], wgs[:, :, 0:NE], ALU.subtract).then_inc(s_small, 1)

            def statistics(n, i):
                hold(dve)
                for h in range(2):
                    v.bn_stats(stats[:, h, :], x[:, i, h * 512:(h + 1) * 512]).then_inc(s_bn, 1)
                dve.wait_ge(s_bn, 3 * n + 2)
                hold(dve)
                v.bn_aggr(mv_one[:, :], stats[:, :, :]).then_inc(s_bn, 1)
                dve.wait_ge(s_bn, 3 * n + 3)
                v.tensor_copy(mv[:, i, :], mv_one[:, :]).then_inc(s_stat, 1)

            dve.wait_ge(s_x, 32)
            with dve.Fori(0, NT) as i:
                statistics(i, i)

            with dve.register("dve_chunks") as chunks, dve.register("dve_first") as first:
                dve.reg_mov(chunks, 0)

                def window(w):
                    dve.reg_load(first, rows_i[0:1, 0, bass.ds(w, 1)])
                    groups = dve.value_load(rows_i[0:1, 1, bass.ds(w, 1)], min_val=1, max_val=NG_MAX)
                    with dve.Fori(0, groups):
                        n = dve.snap(chunks, min_val=0, max_val=1 << 20)
                        at = dve.snap(first, min_val=0, max_val=CHP - G)
                        for half in range(2):
                            dve.wait_ge(s_chunk, n + 5 * half + 5)
                            v.tensor_copy(src_g[:, half, :], src_t[:, bass.ds(at + 5 * half, RING)]).then_inc(s_srcg, 5)
                            v.tensor_tensor(st_e[:, half, :, 0:WIN],
                                            iota_r[:, bass.ds(w * WIN, WIN)].unsqueeze(1).to_broadcast([P, RING, WIN]),
                                            dst_t[:, bass.ds(at + 5 * half, RING)].unsqueeze(2).to_broadcast([P, RING, WIN]),
                                            ALU.is_equal).then_inc(s_onehot, 5)
                            dve.wait_ge(s_srcg, n + 5 * half + 5)
                            for c in range(RING):
                                dve.wait_ge(s_chunk, n + 5 * half + c + 6)
                                v.tensor_scalar(oh[:, c, :], iota_r[:, 0:NP], src_g[:, half, c:c + 1], None,
                                                ALU.is_equal).then_inc(s_oh, 1)
                        dve.reg_add(chunks, chunks, G)
                        dve.reg_add(first, first, G)

                def block_low(b, ub):
                    dve.wait_ge(s_wtb, b + 1)
                    v.tensor_tensor(wt_l[:, b, :], st_wh[:, ub, :], wt_h[:, b, :], ALU.subtract)
                    dve.wait_ge(s_atlo, b + 1)
                    hold(dve)
                    v.tensor_copy(at_lo[:, :], at_lo16[:, :], saturate=False).then_inc(s_blk, 1)
                    dve.wait_ge(s_blk, b + 1)
                    v.tensor_copy(at_l[:, b, :].bitcast(I16), at_lo[:, :].bitcast(I16)).then_inc(s_built, 1)

                for w in range(4):
                    window(w)
                with dve.Fori(0, 4) as bb:
                    for k in range(4, 12):
                        window(8 * bb + k)
                        if k % 4 == 3:
                            block_low(2 * bb + (k - 7) // 4, (k - 7) // 4)
                for w in range(36, NW):
                    window(w)
                block_low(NT - 2, 0)
                block_low(NT - 1, 1)

            def norm(r, i, u):
                dve.wait_ge(s_rstd, r + i + 1)
                v.tensor_scalar(xn[:, u, :], x[:, i, :], mv[:, i, 0:1], rstd[:, bass.ds(i, 1)], ALU.subtract, ALU.mult).then_inc(s_xn, 1)

            def low(n, u):
                dve.wait_ge(s_xh, n + 1)
                hi, lo = parts(n, u)
                v.tensor_tensor(lo, xn[:, u, :], hi, ALU.subtract).then_inc(s_xl, 1)

            def copy_low(n, u):
                dve.wait_ge(s_tl, n + 1)
                v.tensor_copy(xtl[:, u, :, :].rearrange("p k c -> p (k c)"), bank16(5)).then_inc(s_xtl, 1)

            def normalised(r, body, peeled=2):
                norm(r, 0, 0)
                norm(r, 1, 1)
                low(r, 0)
                low(r + 1, 1)
                copy_low(r, 0)

                def step(i, u):
                    if not last_of(i, NT):
                        dve.wait_ge(s_mm, r + i + 1)
                        copy_low(r + i + 1, 1 - u)
                    if not last_of(i, NT, 2):
                        norm(r, i + 2, u)
                        low(r + i + 2, u)
                    body(i, u)

                pairs(dve, step, peeled=peeled)

            def pair_banks(u):
                return ps[:, 2 * u:2 * u + 2, :].rearrange("p b c -> p (b c)")

            def gnn0(i, u):
                dve.wait_ge(s_biased, i + 1)
                dve.wait_ge(s_mm, 1 + R_GNN0 + i + 1)
                v.scalar_tensor_tensor(out=x[:, i, :], in0=pair_banks(u), scalar=1.0 / (SX * SW), in1=x[:, i, :],
                                       op0=ALU.mult, op1=ALU.add).then_inc(s_mmread, 1)
                dve.wait_ge(s_mmread, 2 + R_GNN0 + i + 1)
                statistics(NT + i, i)

            dve.wait_ge(s_built, 2 + NT)
            normalised(R_GNN0, gnn0)

            def logits_of(i, u):
                dve.wait_ge(s_mm, 1 + R_MOE + i + 1)
                v.tensor_reduce(logits[:, i, :], ps[:, 6 + u, 0:2 * NE].rearrange("p (a e) -> p e a", a=2), AX.X,
                                ALU.add).then_inc(s_mmread, 1)

            def norm_ahead(i):
                if i >= 2:
                    dve.wait_ge(s_xl, R_MOE + i - 1)
                norm(R_MOE, i, i % 2)

            norm_ahead(0)
            norm_ahead(1)
            for i in range(2):
                low(R_MOE + i, i)
                norm_ahead(i + 2)
            low(R_MOE + 2, 0)
            copy_low(R_MOE, 0)
            for i in range(NT):
                if i + 4 < NT:
                    norm_ahead(i + 4)
                if i + 3 < NT:
                    low(R_MOE + i + 3, (i + 3) % 2)
                if i + 1 < NT:
                    dve.wait_ge(s_mm, R_MOE + i + 1)
                    copy_low(R_MOE + i + 1, (i + 1) % 2)
                logits_of(i, i % 2)
            dve.wait_ge(s_mmread, 2 + R_MOE + NT)
            dve.wait_ge(s_const, 23)
            do(v.tensor_scalar(logits[:, :, :], logits[:, :, :], 1.0 / (SX * SW), None, ALU.mult))
            for t in range(NT):
                steps.inc(v.max(lmax[:, t, :], logits[:, t, :]))
            steps.wait()
            for t in range(NT):
                steps.inc(v.max_index(lidx[:, t, :], lmax[:, t, :], logits[:, t, :]))
            v.tensor_tensor(rt[:, 0, 0:NT], lmax[:, :, 1], lmax[:, :, 0], ALU.subtract).then_inc(s_gd, 1)
            steps.wait()
            do(v.tensor_copy(lidf[:, :, :], lidx[:, :, :]))
            for k in range(2):
                steps.inc(v.tensor_tensor(mask[:, k, :, :], iota_lo[:, 0:NE].unsqueeze(1).to_broadcast([P, NT, NE]),
                                          lidf[:, :, k:k + 1].to_broadcast([P, NT, NE]), ALU.is_equal))
                steps.inc(v.tensor_copy(rt[:, 5, k * NT:(k + 1) * NT], lidf[:, :, k]))
            steps.wait()
            v.tensor_tensor(mask[:, :, :, :], mask[:, :, :, :], valid_m[:, :, :, :], ALU.mult).then_inc(s_mask, 1)
            dve.wait_ge(s_ex, 1)
            do(v.tensor_scalar(rt[:, 2, 0:NT], rt[:, 1, 0:NT], 1.0, None, ALU.add))
            do(v.reciprocal(gates[:, 0, :], rt[:, 2, 0:NT]))
            do(v.tensor_tensor(gates[:, 1, :], rt[:, 1, 0:NT], gates[:, 0, :], ALU.mult))
            dve.wait_ge(s_cum, 1)
            dve.wait_ge(s_mask, 1)
            by_e = "p (n e) -> p e n"
            do(v.tensor_copy(tot_e[:, :, :], ps[:, 1, 0:2 * NT * NE].rearrange(by_e, e=NE)))
            do(v.tensor_tensor_scan(scan_o[:, :, :].rearrange("p e n -> p (e n)"), scan_m[:, :, :].rearrange("p e n -> p (e n)"),
                                    tot_e[:, :, :].rearrange("p e n -> p (e n)"), 0.0, ALU.mult, ALU.add))
            do(v.tensor_tensor(scan_o[:, :, :], scan_o[:, :, :], tot_e[:, :, :], ALU.subtract))
            do(v.scalar_tensor_tensor(out=loc3[:, :, :], in0=ps[:, 0, 0:2 * NT * NE].rearrange("p (n e) -> p n e", e=NE),
                                      scalar=-1.0, in1=scan_o[:, :, :].rearrange("p e n -> p n e"), op0=ALU.add, op1=ALU.add))
            do(v.tensor_tensor(loc3[:, :, :], loc3[:, :, :], mask[:, :, :, :].rearrange("p k t e -> p (k t) e"), ALU.mult))
            do(v.tensor_reduce(rt[:, 2, :], loc3[:, :, :], AX.X, ALU.add))
            do(v.tensor_scalar(rt[:, 3, :], rt[:, 2, :], float(CAP), None, ALU.is_lt))
            steps.inc(v.tensor_tensor(gates[:, :, :].rearrange("p k t -> p (k t)"), gates[:, :, :].rearrange("p k t -> p (k t)"),
                                      rt[:, 3, :], ALU.mult))
            do(v.tensor_tensor(rt[:, 4, :], rt[:, 3, :], valid_m[:, :, :, 0].rearrange("p k t -> p (k t)"), ALU.mult))
            do(v.tensor_scalar(rt[:, 6, :], rt[:, 2, :], float(CAP - 1), None, ALU.min))
            do(v.scalar_tensor_tensor(out=rt[:, 7, :], in0=rt[:, 5, :], scalar=float(CAP), in1=rt[:, 6, :],
                                      op0=ALU.mult, op1=ALU.add))
            steps.inc(v.tensor_copy(slot_i[:, :], rt[:, 7, :]))
            steps.inc(v.tensor_scalar(rt[:, 8, :], rt[:, 2, :], float(P), None, ALU.is_ge))
            do(v.tensor_scalar(rt[:, 9, :], rt[:, 2, :], float(2 * P), None, ALU.is_ge))
            do(v.tensor_tensor(rt[:, 8, :], rt[:, 8, :], rt[:, 9, :], ALU.add))
            steps.inc(v.scalar_tensor_tensor(out=rt[:, 10, :], in0=rt[:, 8, :], scalar=-float(P), in1=rt[:, 2, :],
                                             op0=ALU.mult, op1=ALU.add))
            do(v.scalar_tensor_tensor(out=rt[:, 11, :], in0=rt[:, 5, :], scalar=3.0, in1=rt[:, 8, :],
                                      op0=ALU.mult, op1=ALU.add))
            do(v.scalar_tensor_tensor(out=rt[:, 9, :], in0=rt[:, 11, :], scalar=1.0, in1=rt[:, 4, :],
                                      op0=ALU.add, op1=ALU.mult))
            do(v.tensor_scalar(rt[:, 11, :], rt[:, 9, :], -1.0, None, ALU.add))
            steps.inc(v.tensor_tensor(oh_lo[:, :, :], iota_lo[:, :].unsqueeze(1).to_broadcast([P, 2 * NT, P]),
                                      rt[:, 10, :].unsqueeze(2).to_broadcast([P, 2 * NT, P]), ALU.is_equal))
            do(v.tensor_tensor(oh_hi[:, :, :], iota_lo[:, 0:3 * NE].unsqueeze(1).to_broadcast([P, 2 * NT, 3 * NE]),
                               rt[:, 11, :].unsqueeze(2).to_broadcast([P, 2 * NT, 3 * NE]), ALU.is_equal))
            v.tensor_tensor(oh_hi2[:, :, :], oh_hi[:, :, :], tok_f[:, :].unsqueeze(2).to_broadcast([P, 2 * NT, 3 * NE]),
                            ALU.mult).then_inc(s_ohr, 1)
            dve.wait_ge(s_tok, 1)
            v.tensor_copy(tok_i[:, :], ps[:, 2, 0:3 * NE]).then_inc(s_toki, 1)

            def split_low(e, q):
                dve.wait_ge(s_wh, 4 * e + q + 1)
                hi, lo = (w1h, w1l) if q < 2 else (w2h, w2l)
                part = slice(4 * q, 4 * q + 4) if q < 2 else slice(2 * q - 4, 2 * q - 2)
                flat = "p k h -> p (k h)"
                v.scalar_tensor_tensor(out=lo[:, part, :].rearrange(flat), in0=wstage[:, q, :], scalar=SW,
                                       in1=hi[:, part, :].rearrange(flat), op0=ALU.mult, op1=ALU.subtract).then_inc(s_wl, 1)

            def gathered(e):
                for s in range(3):
                    m = SM[s]
                    dve.wait_ge(s_gtl, 3 * e + s + 1)
                    v.tensor_copy(xdl[:, :, s * P:s * P + m],
                                  bank16(5).rearrange("p (k c) -> p k c", k=KD)[:, :, 0:m]).then_inc(s_gcl, 1)

            def expert(e, ep):
                for hb in range(KH):
                    dve.wait_ge(s_hh, 4 * e + hb + 1)
                    v.tensor_tensor(htl[:, hb, :], ht32[:, hb % 2, :], hth[:, hb, :], ALU.subtract).then_inc(s_hl, 1)
                if not last_of(e, NE):
                    gathered(e + 1)
                    for q in range(2):
                        split_low(e + 1, q)
                dve.wait_ge(s_b2, 16 * e + 16)
                for s in range(3):
                    m, u = SM[s], (ep + s) % 2
                    dve.wait_ge(s_eout[u], 24 * e + 8 * s - 8 * u + 16)
                    for h in range(2):
                        dve.wait_ge(s_g2, 1 + 6 * e + 2 * s + h + 1)
                        cols = slice(h * 512, (h + 1) * 512)
                        v.scalar_tensor_tensor(out=eo[0:m, u, cols], in0=ps[0:m, (2 * s + h) % 3, :], scalar=1.0 / (SH * SW),
                                               in1=b2b[0:m, cols], op0=ALU.mult, op1=ALU.add).then_inc(s_g2r, 1)
                if not last_of(e, NE):
                    for q in range(2, 4):
                        split_low(e + 1, q)

            dve.wait_ge(s_toki, 1)
            dve.wait_ge(s_xstore, 16 * NT)
            for q in range(2):
                split_low(0, q)
            gathered(0)
            for q in range(2, 4):
                split_low(0, q)
            pairs(dve, expert, NE)

            def w1_low(i, u):
                dve.wait_ge(s_gnh, i + 1)
                dve.wait_ge(s_wtp, i + 1)
                v.scalar_tensor_tensor(out=gnl[:, u, :], in0=gnat[:, u, :], scalar=SW, in1=gnh[:, u, :],
                                       op0=ALU.mult, op1=ALU.subtract).then_inc(s_gnl, 1)

            w1_low(0, 0)

            def w1_part(i, u):
                if not last_of(i, KD):
                    w1_low(i + 1, 1 - u)
                dve.wait_ge(s_wtp, 2 + i + 1)
                v.tensor_copy(gwt_l[:, :, bass.ds(i * P, P)], bank16(5).rearrange("p (k c) -> p k c", k=KD)).then_inc(s_wtl, 1)

            pairs(dve, w1_part, KD)

            def mixture(i, u):
                for k in range(2):
                    dve.wait_ge(s_back[2 * u + k], 8 * i - 8 * u + 16)
                    v.scalar_tensor_tensor(out=x[:, i, :], in0=back[2 * u + k], scalar=gates[:, k, bass.ds(i, 1)],
                                           in1=x[:, i, :], op0=ALU.mult, op1=ALU.add).then_inc(s_mix, 1)
                    dve.wait_ge(s_mix, 2 * i + k + 1)
                statistics(2 * NT + i, i)

            dve.wait_ge(s_deg, 1)
            v.tensor_scalar(dinv[:, 1, :], ps[:, 6, 0:NT], 1.0, None, ALU.add).then_inc(s_degp, 1)
            dve.wait_ge(s_dinv, 1)
            v.tensor_scalar(dinv[:, 1, :], dinv[:, 0, :], SH, None, ALU.mult).then_inc(s_dinv2, 1)
            v.tensor_scalar(dinv[:, 2, :], dinv[:, 0, :], 1.0 / SH, None, ALU.mult).then_inc(s_dinv2, 1)
            dve.wait_ge(s_dinv2, 2)
            dve.wait_ge(s_abs, 2 + 32)
            v.tensor_reduce(sw[:, 0:2], abs_acc[:, :].rearrange("p (m n) -> p m n", m=2), AX.X, ALU.add).then_inc(s_swp, 1)
            dve.wait_ge(s_swm, 1)
            do(v.tensor_scalar(sw[:, 2:4], ps[:, 7, 0:2], 1.0 / (D * FH), Q_EPS, ALU.mult, ALU.max))
            steps.inc(v.tensor_scalar(sw[:, 4:6], sw[:, 2:4], 0.5, None, ALU.mult))
            do(v.tensor_scalar(sw[:, 6:8], sw[:, 2:4], -0.5, None, ALU.mult))
            dve.wait_ge(s_bias, 32)
            for i in range(3):
                mixture(i, i % 2)

            def lin1(i, u):
                if not last_of(i, NT, 3):
                    mixture(i + 3, 1 - u)
                elif i == NT - 3:
                    dve.wait_ge(s_mix, 2 * NT)
                dve.wait_ge(s_hsl, i + 1)
                dve.wait_ge(s_mm, 1 + R_LIN1 + i + 1)
                v.scalar_tensor_tensor(out=h32[:, :], in0=pair_banks(u), scalar=1.0 / (SX * SW), in1=bias_b[:, :],
                                       op0=ALU.mult, op1=ALU.add).then_inc(s_mmread, 1)
                dve.wait_ge(s_hsh, i + 1)
                v.scalar_tensor_tensor(out=hs_l[:, i, :], in0=h32[:, :], scalar=dinv[:, 1, bass.ds(i, 1)],
                                       in1=hs_h[:, i, :], op0=ALU.mult, op1=ALU.subtract).then_inc(s_hsl, 1)

            normalised(R_LIN1, lin1, peeled=4)

            def agg(i, u):
                dve.wait_ge(s_agg, i + 1)
                v.scalar_tensor_tensor(out=x[:, i, :], in0=pair_banks(u), scalar=dinv[:, 2, bass.ds(i, 1)], in1=x[:, i, :],
                                       op0=ALU.mult, op1=ALU.add).then_inc(s_aggread, 1)
                dve.wait_ge(s_aggread, 2 + i + 1)
                statistics(3 * NT + i, i)

            def below(n):
                if n >= 2:
                    dve.wait_ge(s_fq, 4 + n - 1)
                dve.wait_ge(s_fn[n % 4], 16 * (n // 4) + 16)
                m = n // 32
                v.tensor_scalar(fneg[:, n % 2, :], fnat[n % 4], sw[:, 6 + m:7 + m], None, ALU.is_lt,
                                saturate=False).then_inc(s_fneg, 1)

            def weight_piece(n):
                m = n // 32
                if n < 63:
                    below(n + 1)
                dve.wait_ge(s_fneg, n + 1)
                dve.wait_ge(s_ft, n + 1)
                v.scalar_tensor_tensor(out=fq[:, n % 2, :], in0=fnat[n % 4], scalar=sw[:, 4 + m:5 + m],
                                       in1=fneg[:, n % 2, :], op0=ALU.is_gt, op1=ALU.subtract).then_inc(s_fq, 1)

            below(0)
            for i in range(8):
                for k in range(8):
                    weight_piece(8 * i + k)
                    if k == 2 and i > 0:
                        agg(i - 1, (i - 1) % 2)

            qsteps = Steps(dve, s_dq)

            def dq(ins):
                qsteps.inc(ins)
                qsteps.wait()

            def quantise(i, u):
                qsteps.at(0 if isinstance(i, int) and i == 0 else 10 * i - 5)
                dve.wait_ge(s_rstd, 3 * NT + i + 1)
                one = bass.ds(i, 1)
                dq(v.tensor_scalar(xn_f[:, u, :], x[:, i, :], mv[:, i, 0:1], rstd[:, one], ALU.subtract, ALU.mult))
                dq(v.tensor_reduce(fs[:, u, 0:1], xn_f[:, u, :], AX.X, ALU.max, apply_absolute_value=True))
                dq(v.tensor_scalar(fs[:, u, 1:2], fs[:, u, 0:1], Q_EPS, 1.0 / 127.0, ALU.max, ALU.mult))
                v.tensor_tensor(fs[:, u, 3:4], fs[:, u, 1:2], sw[:, 2:3], ALU.mult)
                dq(v.reciprocal(fs[:, u, 2:3], fs[:, u, 1:2]))
                dq(v.tensor_scalar(xn_f[:, u, :], xn_f[:, u, :], fs[:, u, 2:3], MAGIC, ALU.mult, ALU.add))
                v.tensor_scalar(xq[:, u, :], xn_f[:, u, :], -MAGIC, 127.0, ALU.add, ALU.min).then_inc(s_xq, 1)

            def quantise_hidden(i, u):
                qsteps.at(10 * i + 5 if last_of(i, NT) else 10 * i + 10)
                for n in range(8):
                    dve.wait_ge(s_ge, 4 + 8 * i + n + 1)
                    last = v.tensor_reduce(hm[:, u, n:n + 1], hf[:, u, n * 512:(n + 1) * 512], AX.X, ALU.max,
                                           apply_absolute_value=True)
                dq(last)
                dq(v.tensor_reduce(fs[:, u, 8:9], hm[:, u, :], AX.X, ALU.max))
                dq(v.tensor_scalar(fs[:, u, 9:10], fs[:, u, 8:9], Q_EPS, 1.0 / 127.0, ALU.max, ALU.mult))
                v.tensor_tensor(fs[:, u, 11:12], fs[:, u, 9:10], sw[:, 3:4], ALU.mult)
                dq(v.reciprocal(fs[:, u, 10:11], fs[:, u, 9:10]))
                dq(v.tensor_scalar(hf[:, u, :], hf[:, u, :], fs[:, u, 10:11], MAGIC, ALU.mult, ALU.add))
                if not isinstance(i, int) or i > 0:
                    dve.wait_ge(s_hqt, 4 * i)
                v.tensor_scalar(hq[:, :], hf[:, u, :], -MAGIC, 127.0, ALU.add, ALU.min).then_inc(s_hq, 1)

            def result(i, u):
                dve.wait_ge(s_f2, i + 1)
                dve.wait_ge(s_out[u], 8 * i - 8 * u + 16)
                v.scalar_tensor_tensor(out=out_t[:, u, :], in0=ps[:, 4:6, :].rearrange("p b c -> p (b c)"),
                                       scalar=fs[:, u, 11:12], in1=x[:, i, :], op0=ALU.mult, op1=ALU.add).then_inc(s_f2r, 1)

            def ffn(i, u):
                quantise_hidden(i + 1, 1 - u)
                if not last_of(i, NT, 3):
                    quantise(i + 3, 1 - u)
                result(i, u)

            dve.wait_ge(s_ft, 2 + 64)
            agg(NT - 3, 1)
            quantise(0, 0)
            quantise(1, 1)
            agg(NT - 2, 0)
            agg(NT - 1, 1)
            quantise_hidden(0, 0)
            quantise(2, 0)
            with dve.Fori(0, NT // 2 - 2) as j:
                for u in range(2):
                    ffn(2 * j + u, u)
            for i in range(NT - 4, NT - 1):
                ffn(i, i % 2)
            result(NT - 1, (NT - 1) % 2)


_INS = ["x", "src", "dst", "edge_weight", "L0_gnn_bias", "L0_ffn_wg", "L0_ffn_w1", "L0_ffn_b1", "L0_ffn_w2", "L0_ffn_b2",
        "L1_gnn_W", "L1_gnn_b", "L1_ffn_w1", "L1_ffn_w2"]


def kernel(**inputs):
    import numpy as np
    import concourse.bacc as bacc
    from concourse.bass_utils import run_bass_kernel_spmd

    nc = bacc.Bacc("TRN2", target_bir_lowering=False, num_devices=1)
    arrays, args = {}, []
    for name in _INS:
        a = np.ascontiguousarray(inputs[name])
        arrays[f"in_{name}"] = a
        args.append(nc.dram_tensor(f"in_{name}", a.shape, mybir.dt.from_np(a.dtype), kind="ExternalInput").ap())
    out = nc.dram_tensor("out_x", (N, D), F32, kind="ExternalOutput").ap()
    build_kernel(nc, *args, out)
    r = run_bass_kernel_spmd(nc, [arrays], core_ids=[0])
    return r.results[0]["out_x"]
```
